# Optimizing a Trainium2 kernel written in Bass

```python
import numpy as np
import jax
import jax.numpy as jnp

def _softmax(x, axis=-1):
    return jax.nn.softmax(x, axis=axis)

def _gelu(x):
    return jax.nn.gelu(x, approximate=True)

def _silu(x):
    return jax.nn.silu(x)

def _sigmoid(x):
    return jax.nn.sigmoid(x)

def _layernorm(x, axis=-1, eps=1e-05):
    m = jnp.mean(x, axis=axis, keepdims=True)
    v = jnp.var(x, axis=axis, keepdims=True)
    return (x - m) / jnp.sqrt(v + eps)

def _scatter_add(tgt, idx, src, axis=0):
    return tgt.at[idx].add(src)

def _segment_sum(src, seg, n):
    return jax.ops.segment_sum(src, seg, n)
kernel_name = 'mk_seq_preln_d4_jaxref_r8_00d3c4'

def setup_inputs(seed: int=0):
    np.random.seed(seed)
    _w = jnp.asarray

    def _L0_attn_setup():
        import jax, jax.numpy as jnp
        import numpy as np
        import math
        NUM_HEADS = 16
        D_MODEL = 128
        B, T = (1, 512)
        key = jax.random.key(seed)
        kx, kq, kk, kv, ko = jax.random.split(key, 5)
        s = 1.0 / math.sqrt(D_MODEL)
        return {'x': jax.random.normal(kx, (B, T, D_MODEL), dtype=jnp.float32), 'Wq': jax.random.normal(kq, (D_MODEL, D_MODEL), dtype=jnp.float32) * s, 'Wk': jax.random.normal(kk, (D_MODEL, D_MODEL), dtype=jnp.float32) * s, 'Wv': jax.random.normal(kv, (D_MODEL, D_MODEL), dtype=jnp.float32) * s, 'Wo': jax.random.normal(ko, (D_MODEL, D_MODEL), dtype=jnp.float32) * s}
    _L0_attn_in = _L0_attn_setup()

    def _L0_ffn_setup():
        import jax, jax.numpy as jnp
        import numpy as np
        B, S, H = (2, 256, 128)
        E, K, F_EXP, F_SHARED = (16, 2, 64, 128)
        key = jax.random.key(seed)
        ks = jax.random.split(key, 9)
        sc = 1.0 / np.sqrt(H)
        scf = 1.0 / np.sqrt(F_EXP)
        scfs = 1.0 / np.sqrt(F_SHARED)
        return {'x': jax.random.normal(ks[0], (B, S, H), dtype=jnp.float32), 'router_w': jax.random.normal(ks[1], (H, E), dtype=jnp.float32) * sc, 'gate_w': jax.random.normal(ks[2], (E, H, F_EXP), dtype=jnp.float32) * sc, 'up_w': jax.random.normal(ks[3], (E, H, F_EXP), dtype=jnp.float32) * sc, 'down_w': jax.random.normal(ks[4], (E, F_EXP, H), dtype=jnp.float32) * scf, 'shared_gate_w': jax.random.normal(ks[5], (H, F_SHARED), dtype=jnp.float32) * sc, 'shared_up_w': jax.random.normal(ks[6], (H, F_SHARED), dtype=jnp.float32) * sc, 'shared_down_w': jax.random.normal(ks[7], (F_SHARED, H), dtype=jnp.float32) * scfs}
    _L0_ffn_in = _L0_ffn_setup()

    def _L1_attn_setup():
        import jax, jax.numpy as jnp
        import numpy as np
        D_MODEL = 128
        NHEAD = 16
        HEAD_DIM = D_MODEL // NHEAD
        SCALE = HEAD_DIM ** (-0.5)
        EPS_LN = 1e-05
        key = jax.random.key(seed)
        ks = jax.random.split(key, 7)
        B, T, D = (2, 256, D_MODEL)
        x = jax.random.normal(ks[0], (B, T, D), dtype=jnp.float32)
        ln_gamma = jnp.ones((D,), dtype=jnp.float32)
        ln_beta = jnp.zeros((D,), dtype=jnp.float32)
        s = 1.0 / np.sqrt(D)
        W_qkv = jax.random.uniform(ks[1], (D, 3 * D), minval=-s, maxval=s, dtype=jnp.float32)
        b_qkv = jax.random.uniform(ks[2], (3 * D,), minval=-s, maxval=s, dtype=jnp.float32)
        W_proj = jax.random.uniform(ks[3], (D, D), minval=-s, maxval=s, dtype=jnp.float32)
        b_proj = jax.random.uniform(ks[4], (D,), minval=-s, maxval=s, dtype=jnp.float32)
        return {'x': x, 'ln_gamma': ln_gamma, 'ln_beta': ln_beta, 'W_qkv': W_qkv, 'b_qkv': b_qkv, 'W_proj': W_proj, 'b_proj': b_proj}
    _L1_attn_in = _L1_attn_setup()

    def _L1_ffn_setup():
        import jax, jax.numpy as jnp
        import numpy as np
        DIM = 128

        def _reference_tuple_inner(x, W_r, W_k, W_v, mu_r, mu_k):
            B, T, C = x.shape
            x_prev = jnp.concatenate([jnp.zeros((B, 1, C), x.dtype), x[:, :-1, :]], axis=1)
            xr = mu_r * x + (1.0 - mu_r) * x_prev
            xk = mu_k * x + (1.0 - mu_k) * x_prev
            r = jax.nn.sigmoid(jnp.einsum('btc,dc->btd', xr, W_r))
            k = jnp.einsum('btc,dc->btd', xk, W_k)
            k_act = jnp.square(jax.nn.relu(k))
            out = r * jnp.einsum('btc,dc->btd', k_act, W_v)
            new_state = x[:, -1, :]
            return (out, new_state)
        key = jax.random.key(seed)
        ks = jax.random.split(key, 6)
        B, T, C = (8, 256, DIM)
        x = jax.random.normal(ks[0], (B, T, C), dtype=jnp.float32)
        s = 1.0 / np.sqrt(C)
        W_r = jax.random.uniform(ks[1], (C, C), jnp.float32, -s, s)
        W_k = jax.random.uniform(ks[2], (C, C), jnp.float32, -s, s)
        W_v = jax.random.uniform(ks[3], (C, C), jnp.float32, -s, s)
        mu_r = jax.random.uniform(ks[4], (C,), jnp.float32)
        mu_k = jax.random.uniform(ks[5], (C,), jnp.float32)
        return {'x': x, 'W_r': W_r, 'W_k': W_k, 'W_v': W_v, 'mu_r': mu_r, 'mu_k': mu_k}
    _L1_ffn_in = _L1_ffn_setup()

    def _L2_attn_setup():
        import jax, jax.numpy as jnp
        import numpy as np
        H = 8
        D = 64
        E = 128

        def sinusoidal_pe(T, d, dtype=jnp.float32):
            pos = jnp.arange(T, dtype=jnp.float32)[:, None]
            div = jnp.exp(jnp.arange(0, d, 2, dtype=jnp.float32) * (-np.log(10000.0) / d))
            ang = pos * div
            pe = jnp.stack([jnp.sin(ang), jnp.cos(ang)], axis=-1).reshape(T, d)
            return pe.astype(dtype)
        key = jax.random.key(seed)
        k1, k2, k3 = jax.random.split(key, 3)
        B, T = (2, 256)
        x = jax.random.normal(k1, (B, T, E), dtype=jnp.float32)
        Wqkv = jax.random.normal(k2, (3 * H * D, E), dtype=jnp.float32) * (1.0 / np.sqrt(E))
        Wo = jax.random.normal(k3, (E, H * D), dtype=jnp.float32) * (1.0 / np.sqrt(H * D))
        return {'x': x, 'Wqkv': Wqkv, 'Wo': Wo}
    _L2_attn_in = _L2_attn_setup()

    def _L2_ffn_setup():
        import math
        import jax, jax.numpy as jnp
        import numpy as np
        B, S, D, F, E = (8, 256, 128, 512, 8)
        CAPACITY_FACTOR = 1.0
        key = jax.random.key(seed)
        k1, k2, k3, k4 = jax.random.split(key, 4)
        x = jax.random.normal(k1, (B, S, D), dtype=jnp.float32)
        Wr = jax.random.normal(k2, (D, E), dtype=jnp.float32) * (1.0 / math.sqrt(D))
        W1 = jax.random.normal(k3, (E, D, F), dtype=jnp.float32) * (1.0 / math.sqrt(D))
        W2 = jax.random.normal(k4, (E, F, D), dtype=jnp.float32) * (1.0 / math.sqrt(F))
        return {'x': x, 'Wr': Wr, 'W1': W1, 'W2': W2}
    _L2_ffn_in = _L2_ffn_setup()

    def _L3_attn_setup():
        import jax, jax.numpy as jnp
        import numpy as np
        H = 8
        DIM = 128
        DH = DIM // H // 2
        B, N = (2, 256)
        LAMBDA_INIT = 0.5
        COS_MIN, COS_MAX = (0.0, 15.0)
        ALPHA = 0.5
        COS_EPS = 1e-06
        RMS_EPS = 1e-05
        RAW_INIT = float(np.log(1.0 / 15.0 / (1.0 - 1.0 / 15.0)))

        def _l2norm(t):
            return t / jnp.maximum(jnp.linalg.norm(t, axis=-1, keepdims=True), COS_EPS)
        key = jax.random.key(seed)
        ks = jax.random.split(key, 10)
        s = 1.0 / np.sqrt(DIM)
        return {'x': jax.random.normal(ks[0], (B, N, DIM), jnp.float32), 'Wq': jax.random.normal(ks[1], (DIM, DIM), jnp.float32) * s, 'Wk': jax.random.normal(ks[2], (DIM, DIM), jnp.float32) * s, 'Wv': jax.random.normal(ks[3], (DIM, DIM), jnp.float32) * s, 'Wo': jax.random.normal(ks[4], (DIM, DIM), jnp.float32) * s, 'bo': jnp.zeros((DIM,), jnp.float32), 'lambda_q1': jax.random.normal(ks[5], (DH,), jnp.float32) * 0.1, 'lambda_k1': jax.random.normal(ks[6], (DH,), jnp.float32) * 0.1, 'lambda_q2': jax.random.normal(ks[7], (DH,), jnp.float32) * 0.1, 'lambda_k2': jax.random.normal(ks[8], (DH,), jnp.float32) * 0.1, 'delta_gain': jax.random.normal(ks[9], (H,), jnp.float32) * 0.1, 'cos_head_delta': jnp.zeros((H,), jnp.float32), 'cos_logit_scale_raw': jnp.float32(RAW_INIT), 'subln_weight': jnp.ones((2 * DH,), jnp.float32)}
    _L3_attn_in = _L3_attn_setup()

    def _L3_ffn_setup():
        import jax, jax.numpy as jnp
        import numpy as np
        key = jax.random.key(seed)
        ks = jax.random.split(key, 5)
        B, Sq, M, E, H = (4, 256, 128, 8, 512)
        x = jax.random.normal(ks[0], (B, Sq, M), dtype=jnp.float32)
        wg = jax.random.normal(ks[1], (M, E), dtype=jnp.float32) * (1.0 / np.sqrt(M))
        w1 = jax.random.normal(ks[2], (E, M, H), dtype=jnp.float32) * (1.0 / np.sqrt(M))
        b1 = jnp.zeros((E, H), dtype=jnp.float32)
        w2 = jax.random.normal(ks[3], (E, H, M), dtype=jnp.float32) * (1.0 / np.sqrt(H))
        b2 = jnp.zeros((E, M), dtype=jnp.float32)
        return {'x': x, 'wg': wg, 'w1': w1, 'b1': b1, 'w2': w2, 'b2': b2}
    _L3_ffn_in = _L3_ffn_setup()
    _d = {'L0_attn_x': _L0_attn_in['x'], 'L0_attn_Wq': _L0_attn_in['Wq'], 'L0_attn_Wk': _L0_attn_in['Wk'], 'L0_attn_Wv': _L0_attn_in['Wv'], 'L0_attn_Wo': _L0_attn_in['Wo'], 'L0_ffn_router_w': _L0_ffn_in['router_w'], 'L0_ffn_gate_w': _L0_ffn_in['gate_w'], 'L0_ffn_up_w': _L0_ffn_in['up_w'], 'L0_ffn_down_w': _L0_ffn_in['down_w'], 'L0_ffn_shared_gate_w': _L0_ffn_in['shared_gate_w'], 'L0_ffn_shared_up_w': _L0_ffn_in['shared_up_w'], 'L0_ffn_shared_down_w': _L0_ffn_in['shared_down_w'], 'L1_attn_ln_gamma': _L1_attn_in['ln_gamma'], 'L1_attn_ln_beta': _L1_attn_in['ln_beta'], 'L1_attn_W_qkv': _L1_attn_in['W_qkv'], 'L1_attn_b_qkv': _L1_attn_in['b_qkv'], 'L1_attn_W_proj': _L1_attn_in['W_proj'], 'L1_attn_b_proj': _L1_attn_in['b_proj'], 'L1_ffn_W_r': _L1_ffn_in['W_r'], 'L1_ffn_W_k': _L1_ffn_in['W_k'], 'L1_ffn_W_v': _L1_ffn_in['W_v'], 'L1_ffn_mu_r': _L1_ffn_in['mu_r'], 'L1_ffn_mu_k': _L1_ffn_in['mu_k'], 'L2_attn_Wqkv': _L2_attn_in['Wqkv'], 'L2_attn_Wo': _L2_attn_in['Wo'], 'L2_ffn_Wr': _L2_ffn_in['Wr'], 'L2_ffn_W1': _L2_ffn_in['W1'], 'L2_ffn_W2': _L2_ffn_in['W2'], 'L3_attn_Wq': _L3_attn_in['Wq'], 'L3_attn_Wk': _L3_attn_in['Wk'], 'L3_attn_Wv': _L3_attn_in['Wv'], 'L3_attn_Wo': _L3_attn_in['Wo'], 'L3_attn_bo': _L3_attn_in['bo'], 'L3_attn_lambda_q1': _L3_attn_in['lambda_q1'], 'L3_attn_lambda_k1': _L3_attn_in['lambda_k1'], 'L3_attn_lambda_q2': _L3_attn_in['lambda_q2'], 'L3_attn_lambda_k2': _L3_attn_in['lambda_k2'], 'L3_attn_delta_gain': _L3_attn_in['delta_gain'], 'L3_attn_cos_head_delta': _L3_attn_in['cos_head_delta'], 'L3_attn_cos_logit_scale_raw': _L3_attn_in['cos_logit_scale_raw'], 'L3_attn_subln_weight': _L3_attn_in['subln_weight'], 'L3_ffn_wg': _L3_ffn_in['wg'], 'L3_ffn_w1': _L3_ffn_in['w1'], 'L3_ffn_b1': _L3_ffn_in['b1'], 'L3_ffn_w2': _L3_ffn_in['w2'], 'L3_ffn_b2': _L3_ffn_in['b2']}
    _x0 = _d['L0_attn_x']
    _d['L0_attn_x'] = jax.random.normal(jax.random.fold_in(jax.random.key(seed), 1), (4, 1024, 128), dtype=_x0.dtype)
    del _x0
    return _d

def reference(L0_attn_x, L0_attn_Wq, L0_attn_Wk, L0_attn_Wv, L0_attn_Wo, L0_ffn_router_w, L0_ffn_gate_w, L0_ffn_up_w, L0_ffn_down_w, L0_ffn_shared_gate_w, L0_ffn_shared_up_w, L0_ffn_shared_down_w, L1_attn_ln_gamma, L1_attn_ln_beta, L1_attn_W_qkv, L1_attn_b_qkv, L1_attn_W_proj, L1_attn_b_proj, L1_ffn_W_r, L1_ffn_W_k, L1_ffn_W_v, L1_ffn_mu_r, L1_ffn_mu_k, L2_attn_Wqkv, L2_attn_Wo, L2_ffn_Wr, L2_ffn_W1, L2_ffn_W2, L3_attn_Wq, L3_attn_Wk, L3_attn_Wv, L3_attn_Wo, L3_attn_bo, L3_attn_lambda_q1, L3_attn_lambda_k1, L3_attn_lambda_q2, L3_attn_lambda_k2, L3_attn_delta_gain, L3_attn_cos_head_delta, L3_attn_cos_logit_scale_raw, L3_attn_subln_weight, L3_ffn_wg, L3_ffn_w1, L3_ffn_b1, L3_ffn_w2, L3_ffn_b2):

    def _L0_attn_ref(x, Wq, Wk, Wv, Wo):
        import jax, jax.numpy as jnp
        import numpy as np
        import math
        NUM_HEADS = 16
        D_MODEL = 128
        B, T = (1, 512)
        Bx, Tx, D = x.shape
        H = NUM_HEADS
        dk = D // H
        q = (x @ Wq.T).reshape(Bx, Tx, H, dk)
        k = (x @ Wk.T).reshape(Bx, Tx, H, dk)
        v = (x @ Wv.T).reshape(Bx, Tx, H, dk)
        scores = jnp.einsum('bthd,bshd->bhts', q, k) / math.sqrt(dk)
        causal_mask = jnp.triu(jnp.ones((Tx, Tx), dtype=bool), k=1)
        scores = jnp.where(causal_mask, jnp.float32(-jnp.inf), scores).astype(jnp.float32)
        attn = jax.nn.softmax(scores, axis=-1)
        out = jnp.einsum('bhts,bshd->bthd', attn, v).reshape(Bx, Tx, D)
        return out @ Wo.T

    def _L0_ffn_ref(x, router_w, gate_w, up_w, down_w, shared_gate_w, shared_up_w, shared_down_w):
        import jax, jax.numpy as jnp
        import numpy as np
        B, S, H = (2, 256, 128)
        E, K, F_EXP, F_SHARED = (16, 2, 64, 128)
        b, s, h = x.shape
        T = b * s
        x_flat = x.reshape(T, h)
        shared_out = jax.nn.silu(x @ shared_gate_w) * (x @ shared_up_w) @ shared_down_w
        router_probs = jax.nn.softmax(x_flat @ router_w, axis=-1)
        topk_probs, topk_idx = jax.lax.top_k(router_probs, K)
        coeff = jnp.einsum('tk,tke->te', topk_probs, jax.nn.one_hot(topk_idx, E, dtype=x.dtype))

        def expert_step(acc, ws):
            g, u, d, c = ws
            inter = jax.nn.silu(x_flat @ g) * (x_flat @ u)
            return (acc + inter @ d * c[:, None], None)
        routed, _ = jax.lax.scan(expert_step, jnp.zeros((T, h), dtype=x.dtype), (gate_w, up_w, down_w, coeff.T))
        return routed.reshape(b, s, h) + shared_out

    def _L1_attn_ref(x, ln_gamma, ln_beta, W_qkv, b_qkv, W_proj, b_proj):
        import jax, jax.numpy as jnp
        import numpy as np
        D_MODEL = 128
        NHEAD = 16
        HEAD_DIM = D_MODEL // NHEAD
        SCALE = HEAD_DIM ** (-0.5)
        EPS_LN = 1e-05
        B, T, D = x.shape
        h, dh = (NHEAD, HEAD_DIM)
        mu = jnp.mean(x, axis=-1, keepdims=True)
        var = jnp.mean(jnp.square(x - mu), axis=-1, keepdims=True)
        x_n = (x - mu) * jax.lax.rsqrt(var + EPS_LN) * ln_gamma + ln_beta
        qkv = x_n @ W_qkv + b_qkv
        q, k, v = jnp.split(qkv, 3, axis=-1)
        q = q.reshape(B, T, h, dh).transpose(0, 2, 1, 3)
        k = k.reshape(B, T, h, dh).transpose(0, 2, 1, 3)
        v = v.reshape(B, T, h, dh).transpose(0, 2, 1, 3)
        scores = jnp.einsum('bhqd,bhkd->bhqk', q, k) * SCALE
        scores = scores - jnp.max(scores, axis=-1, keepdims=True)
        attn = jnp.exp(scores)
        attn = attn / jnp.maximum(jnp.sum(attn, axis=-1, keepdims=True), 1e-12)
        ctx = jnp.einsum('bhqk,bhkd->bhqd', attn, v)
        ctx = ctx.transpose(0, 2, 1, 3).reshape(B, T, D)
        return ctx @ W_proj + b_proj

    def _L1_ffn_ref(x, W_r, W_k, W_v, mu_r, mu_k):
        import jax, jax.numpy as jnp
        import numpy as np
        DIM = 128

        def _reference_tuple_inner(x, W_r, W_k, W_v, mu_r, mu_k):
            B, T, C = x.shape
            x_prev = jnp.concatenate([jnp.zeros((B, 1, C), x.dtype), x[:, :-1, :]], axis=1)
            xr = mu_r * x + (1.0 - mu_r) * x_prev
            xk = mu_k * x + (1.0 - mu_k) * x_prev
            r = jax.nn.sigmoid(jnp.einsum('btc,dc->btd', xr, W_r))
            k = jnp.einsum('btc,dc->btd', xk, W_k)
            k_act = jnp.square(jax.nn.relu(k))
            out = r * jnp.einsum('btc,dc->btd', k_act, W_v)
            new_state = x[:, -1, :]
            return (out, new_state)
        return _reference_tuple_inner(x, W_r, W_k, W_v, mu_r, mu_k)[0]

    def _L2_attn_ref(x, Wqkv, Wo):
        import jax, jax.numpy as jnp
        import numpy as np
        H = 8
        D = 64
        E = 128

        def sinusoidal_pe(T, d, dtype=jnp.float32):
            pos = jnp.arange(T, dtype=jnp.float32)[:, None]
            div = jnp.exp(jnp.arange(0, d, 2, dtype=jnp.float32) * (-np.log(10000.0) / d))
            ang = pos * div
            pe = jnp.stack([jnp.sin(ang), jnp.cos(ang)], axis=-1).reshape(T, d)
            return pe.astype(dtype)
        B, T, _ = x.shape
        qkv = jnp.einsum('bte,fe->btf', x, Wqkv)
        qkv = qkv.reshape(B, T, H, 3 * D)
        q, k, v = jnp.split(qkv, 3, axis=-1)
        q = q.transpose(0, 2, 1, 3)
        k = k.transpose(0, 2, 1, 3)
        v = v.transpose(0, 2, 1, 3)
        pe = sinusoidal_pe(T, D, q.dtype)
        q = q + pe[None, None]
        k = k + pe[None, None]
        causal = jnp.tril(jnp.ones((T, T), dtype=bool))
        scores = jnp.einsum('bhtd,bhsd->bhts', q, k) / jnp.sqrt(jnp.asarray(D, q.dtype))
        scores = jnp.where(causal[None, None], scores, jnp.asarray(-jnp.inf, q.dtype))
        probs = jax.nn.softmax(scores, axis=-1)
        attn = jnp.einsum('bhts,bhsd->bhtd', probs, v)
        out = attn.transpose(0, 2, 1, 3).reshape(B, T, H * D)
        out = jnp.einsum('btf,ef->bte', out, Wo)
        return out

    def _L2_ffn_ref(x, Wr, W1, W2):
        import math
        import jax, jax.numpy as jnp
        import numpy as np
        B, S, D, F, E = (8, 256, 128, 512, 8)
        CAPACITY_FACTOR = 1.0
        b, s, d = x.shape
        t = b * s
        cap = max(math.ceil(t * CAPACITY_FACTOR / E), 1)
        xf = x.reshape(t, d)
        probs = jax.nn.softmax(xf.astype(jnp.float32) @ Wr, axis=-1)
        eidx = jnp.argmax(probs, axis=-1)
        p_tok = jnp.take_along_axis(probs, eidx[:, None], axis=1)[:, 0]
        onehot = jax.nn.one_hot(eidx, E, dtype=jnp.int32)
        rank_all = jnp.cumsum(onehot, axis=0) - onehot
        rank = jnp.take_along_axis(rank_all, eidx[:, None], axis=1)[:, 0]
        keep = rank < cap
        slot = jnp.where(keep, rank, cap)
        dispatch = jnp.zeros((E, cap + 1), dtype=jnp.int32).at[eidx, slot].set(jnp.arange(t, dtype=jnp.int32))
        valid = jnp.zeros((E, cap + 1), dtype=bool).at[eidx, slot].set(keep)
        dispatch = dispatch[:, :cap]
        valid = valid[:, :cap]
        xe = xf[dispatch]
        h = jnp.maximum(jnp.einsum('ecd,edf->ecf', xe, W1), 0.0)
        ye = jnp.einsum('ecf,efd->ecd', h, W2)
        pe = p_tok[dispatch]
        ye = ye * (pe * valid.astype(ye.dtype))[:, :, None]
        y = jnp.zeros((t, d), dtype=x.dtype).at[dispatch.reshape(-1)].add(ye.reshape(E * cap, d).astype(x.dtype))
        return y.reshape(b, s, d)

    def _L3_attn_ref(x, Wq, Wk, Wv, Wo, bo, lambda_q1, lambda_k1, lambda_q2, lambda_k2, delta_gain, cos_head_delta, cos_logit_scale_raw, subln_weight):
        import jax, jax.numpy as jnp
        import numpy as np
        H = 8
        DIM = 128
        DH = DIM // H // 2
        B, N = (2, 256)
        LAMBDA_INIT = 0.5
        COS_MIN, COS_MAX = (0.0, 15.0)
        ALPHA = 0.5
        COS_EPS = 1e-06
        RMS_EPS = 1e-05
        RAW_INIT = float(np.log(1.0 / 15.0 / (1.0 - 1.0 / 15.0)))

        def _l2norm(t):
            return t / jnp.maximum(jnp.linalg.norm(t, axis=-1, keepdims=True), COS_EPS)
        b, n, c = x.shape
        q = (x @ Wq.T).reshape(b, n, H, 2, DH).transpose(0, 2, 3, 1, 4)
        k = (x @ Wk.T).reshape(b, n, H, 2, DH).transpose(0, 2, 3, 1, 4)
        v = (x @ Wv.T).reshape(b, n, H, 2 * DH).transpose(0, 2, 1, 3)
        q1, q2 = (q[:, :, 0], q[:, :, 1])
        k1, k2 = (k[:, :, 0], k[:, :, 1])
        gscale = COS_MIN + (COS_MAX - COS_MIN) * jax.nn.sigmoid(cos_logit_scale_raw)
        head_delta = cos_head_delta - cos_head_delta.mean()
        cos_scale = (gscale * (1.0 + ALPHA * jnp.tanh(head_delta))).reshape(1, H, 1, 1)
        L1 = jnp.einsum('bhnd,bhmd->bhnm', _l2norm(q1), _l2norm(k1)) * cos_scale
        L2 = jnp.einsum('bhnd,bhmd->bhnm', _l2norm(q2), _l2norm(k2)) * cos_scale
        L1 = jnp.nan_to_num(L1)
        L2 = jnp.nan_to_num(L2)
        G = jnp.tanh(delta_gain.reshape(1, H, 1, 1) * (L1 - L2))
        A1 = jax.nn.softmax((L1 + G).astype(jnp.float32), axis=-1).astype(x.dtype)
        A2 = jax.nn.softmax((L2 - G).astype(jnp.float32), axis=-1).astype(x.dtype)
        lambda_1 = jnp.exp(jnp.sum(lambda_q1 * lambda_k1))
        lambda_2 = jnp.exp(jnp.sum(lambda_q2 * lambda_k2))
        lambda_full = (lambda_1 - lambda_2 + LAMBDA_INIT).astype(x.dtype)
        attn = A1 - lambda_full * A2
        y = jnp.einsum('bhnm,bhmd->bhnd', attn, v)
        y = y * jax.lax.rsqrt(jnp.mean(y * y, axis=-1, keepdims=True) + RMS_EPS) * subln_weight
        y = y * (1.0 - LAMBDA_INIT)
        y = y.transpose(0, 2, 1, 3).reshape(b, n, c)
        return y @ Wo.T + bo

    def _L3_ffn_ref(x, wg, w1, b1, w2, b2):
        import jax, jax.numpy as jnp
        import numpy as np
        B, Sq, M = x.shape
        E = wg.shape[1]
        S = B * Sq
        C = S // E
        xt = x.reshape(S, M)
        gates = jax.nn.softmax(xt @ wg, axis=-1)
        expert_idx = jnp.argmax(gates, axis=-1)
        mask1 = jax.nn.one_hot(expert_idx, E, dtype=xt.dtype)
        locations = jnp.cumsum(mask1, axis=0) - 1.0
        pos = jnp.sum(locations * mask1, axis=1).astype(jnp.int32)
        keep = (pos < C).astype(xt.dtype)
        gate_val = jnp.sum(gates * mask1, axis=1) * keep
        slot = expert_idx.astype(jnp.int32) * C + jnp.clip(pos, 0, C - 1)
        disp = jnp.zeros((E * C, M), dtype=xt.dtype).at[slot].add(xt * keep[:, None])
        disp = disp.reshape(E, C, M)
        h = jax.nn.relu(jnp.einsum('ecm,emh->ech', disp, w1) + b1[:, None, :])
        eo = jnp.einsum('ech,ehm->ecm', h, w2) + b2[:, None, :]
        out = eo.reshape(E * C, M)[slot] * gate_val[:, None]
        return out.reshape(B, Sq, M)
    x = L0_attn_x
    x = x + _L0_attn_ref(_layernorm(x, axis=-1), L0_attn_Wq, L0_attn_Wk, L0_attn_Wv, L0_attn_Wo)
    x = x + _L0_ffn_ref(_layernorm(x, axis=-1), L0_ffn_router_w, L0_ffn_gate_w, L0_ffn_up_w, L0_ffn_down_w, L0_ffn_shared_gate_w, L0_ffn_shared_up_w, L0_ffn_shared_down_w)
    x = x + _L1_attn_ref(_layernorm(x, axis=-1), L1_attn_ln_gamma, L1_attn_ln_beta, L1_attn_W_qkv, L1_attn_b_qkv, L1_attn_W_proj, L1_attn_b_proj)
    x = x + _L1_ffn_ref(_layernorm(x, axis=-1), L1_ffn_W_r, L1_ffn_W_k, L1_ffn_W_v, L1_ffn_mu_r, L1_ffn_mu_k)
    x = x + _L2_attn_ref(_layernorm(x, axis=-1), L2_attn_Wqkv, L2_attn_Wo)
    x = x + _L2_ffn_ref(_layernorm(x, axis=-1), L2_ffn_Wr, L2_ffn_W1, L2_ffn_W2)
    x = x + _L3_attn_ref(_layernorm(x, axis=-1), L3_attn_Wq, L3_attn_Wk, L3_attn_Wv, L3_attn_Wo, L3_attn_bo, L3_attn_lambda_q1, L3_attn_lambda_k1, L3_attn_lambda_q2, L3_attn_lambda_k2, L3_attn_delta_gain, L3_attn_cos_head_delta, L3_attn_cos_logit_scale_raw, L3_attn_subln_weight)
    x = x + _L3_ffn_ref(_layernorm(x, axis=-1), L3_ffn_wg, L3_ffn_w1, L3_ffn_b1, L3_ffn_w2, L3_ffn_b2)
    return x

_drawn_inputs = setup_inputs


def setup_inputs(seed=0):
    import zlib

    import numpy as np

    out = dict(_drawn_inputs(seed))
    spreads = {'L1_attn_ln_gamma': (1.0, 0.546),
     'L1_attn_ln_beta': (0.0, 0.1),
     'L3_attn_bo': (0.0, 0.1),
     'L3_attn_cos_head_delta': (0.0, 0.44),
     'L3_attn_subln_weight': (1.0, 0.2),
     'L3_ffn_b1': (0.0, 0.478),
     'L3_ffn_b2': (0.0, 0.34)}
    factors = {'L1_ffn_mu_r': 2.979, 'L3_attn_lambda_q1': 3.736, 'L3_attn_lambda_k1': 2.749}
    for name, (base, spread) in spreads.items():
        noise = np.random.default_rng([zlib.crc32(name.encode()), seed]).standard_normal(out[name].shape)
        drawn = base * np.exp(spread * noise) if base else spread * noise
        out[name] = jnp.asarray(drawn.astype(out[name].dtype))
    for name, factor in factors.items():
        out[name] = (out[name] * factor).astype(out[name].dtype)
    return out
```

```python
from contextlib import ExitStack, contextmanager

import numpy as np
import concourse.bass as bass
from concourse import mybir

FP32 = mybir.dt.float32
BF16 = mybir.dt.bfloat16
U32 = mybir.dt.uint32
ALU = mybir.AluOpType
ACT = mybir.ActivationFunctionType
AX = mybir.AxisListType
ds = bass.ds

P = 128
BATCH, T, D = 4, 1024, 128
TOK = BATCH * T
TILES = TOK // P
CH = 512
CPT = CH // P
CHUNKS = TOK // CH
KB = T // P
GROUPS = 4
UNITS = BATCH * GROUPS
EPS = 1e-5
NEG = -1e30


@contextmanager
def cleared_semaphores(nc):
    before = nc.snapshot_sems()
    yield
    nc.clear_and_free_semaphores(nc.allocated_since(before))
    nc.all_engine_barrier()


def layer_stats(nc, name, src, mv, rstd, dst=None):
    with ExitStack() as ctx:
        stats = ctx.enter_context(nc.sbuf_tensor(name + "_stats", [P, TILES * 6], FP32))
        eps = ctx.enter_context(nc.sbuf_tensor(name + "_eps", [P, 1], FP32))
        std = ctx.enter_context(nc.sbuf_tensor(name + "_std", [P, TILES], FP32))
        stats_done = nc.alloc_semaphore(name + "_stats_done")
        mv_done = nc.alloc_semaphore(name + "_mv_done")
        std_done = nc.alloc_semaphore(name + "_std_done")
        rstd_done = nc.alloc_semaphore(name + "_rstd_done")
        block = ctx.enter_context(nc.Block())

        @block.scalar
        def _(act):
            act.wait_ge(mv_done, TILES + 1)
            nc.scalar.activation(std[:], mv[:, :, 1], ACT.Sqrt, bias=eps[:, 0:1]).then_inc(std_done, 1)

        @block.vector
        def _(dve):
            nc.vector.memset(eps[:], EPS).then_inc(mv_done, 1)
            with dve.Fori(0, BATCH) as b:
                for k in range(KB):
                    t = b * KB + k
                    nc.vector.bn_stats(stats[:, ds(t * 6, 6)], src[:, ds(t * D, D)]).then_inc(stats_done, 1)
            dve.wait_ge(stats_done, TILES)
            for t in range(TILES):
                nc.vector.bn_aggr(mv[:, t, :], stats[:, t * 6:(t + 1) * 6]).then_inc(mv_done, 1)
            dve.wait_ge(std_done, 1)
            nc.vector.reciprocal(rstd[:], std[:]).then_inc(rstd_done, 1)
            dve.wait_ge(rstd_done, 1)
            nc.vector.tensor_tensor(std[:], rstd[:], rstd[:], ALU.mult).then_inc(rstd_done, 1)
            dve.wait_ge(rstd_done, 2)
            nc.vector.scalar_tensor_tensor(out=std[:], in0=mv[:, :, 1], scalar=EPS, in1=std[:],
                                           op0=ALU.add, op1=ALU.mult).then_inc(rstd_done, 1)
            dve.wait_ge(rstd_done, 3)
            nc.vector.tensor_scalar(std[:], std[:], -0.5, 1.5, ALU.mult, ALU.add).then_inc(rstd_done, 1)
            dve.wait_ge(rstd_done, 4)
            nc.vector.tensor_tensor(rstd[:], rstd[:], std[:], ALU.mult).then_inc(rstd_done, 1)
            dve.wait_ge(rstd_done, 5)
            if dst is not None:
                with dve.Fori(0, BATCH) as b:
                    for k in range(KB):
                        t = b * KB + k
                        nc.vector.tensor_scalar(dst[:, ds(t * D, D)], src[:, ds(t * D, D)], column(mv, t),
                                                rstd[:, ds(t, 1)], ALU.subtract, ALU.mult)


def column(mv, tile):
    return mv[:].rearrange("p t s -> p (t s)")[:, ds(tile * 2, 1)]


def apply_norm(nc, dst, src, mv, rstd, tile0):
    for t in range(CPT):
        ins = nc.vector.tensor_scalar(dst[:, t * D:(t + 1) * D], src[:, ds((tile0 + t) * D, D)],
                                      column(mv, tile0 + t), rstd[:, ds(tile0 + t, 1)],
                                      ALU.subtract, ALU.mult)
    return ins


def project(nc, name, src, mv, rstd, wq, wk, wv, qs, ks, vs, ident, heads, v_width,
            gain=None, qk_bias=None, v_bias=None, pos=None):
    q_tiles = wq.shape[1] // P
    items = 2 * q_tiles
    vdim = wv.shape[1]
    hd = vdim // heads
    v_items = vdim // P
    with ExitStack() as ctx:
        def sb(n, shape, dt=FP32):
            return ctx.enter_context(nc.sbuf_tensor(f"{name}_{n}", shape, dt))

        def ps(n):
            return ctx.enter_context(nc.psum_tensor(f"{name}_{n}", [P, CH], FP32))

        def sem(n):
            return nc.alloc_semaphore(f"{name}_{n}")

        w_qk = sb("w_qk", [P, items, P])
        w_v = sb("w_v", [P, vdim])
        xn = [sb(f"xn{i}", [P, CH]) for i in range(2)]
        xnT = sb("xnT", [P, 2, CH])
        NB = 4
        val = [sb(f"val{i}", [P, CH]) for i in range(NB)]
        rem = [sb(f"rem{i}", [P, CH]) for i in range(NB)]
        parts = [sb(f"parts{i}", [P, 3, CH], BF16) for i in range(NB)]
        vpad = [sb(f"vpad{i}", [P, CPT, heads, v_width]) for i in range(2)]
        gain_sb = sb("gain_sb", [P, 2])
        bias_sb = sb("bias_sb", [P, items])
        vb_sb = sb("vb_sb", [P, vdim])
        pos_sb = sb("pos_sb", [P, T])
        t_ps = [ps(f"t_ps{i}") for i in range(2)]
        item_ps = [ps(f"item_ps{i}") for i in range(NB)]
        v_ps = [ps(f"v_ps{i}") for i in range(2)]
        xn_done = sem("xn_done")
        loaded, xT_ready, xT_done = sem("loaded"), sem("xT_ready"), sem("xT_done")
        item_ready, val_done, hi_done = sem("item_ready"), sem("val_done"), sem("hi_done")
        rem_done, mid_done, lo_done = sem("rem_done"), sem("mid_done"), sem("lo_done")
        v_ready, v_done, v_preset = sem("v_ready"), sem("v_done"), sem("v_preset")
        stored = [sem(f"stored{i}") for i in range(NB)]
        v_stored = [sem(f"v_stored{i}") for i in range(2)]
        n_loads = 3 + sum(a is not None for a in (gain, qk_bias, v_bias, pos))
        block = ctx.enter_context(nc.Block())

        @block.sync
        def _(sp):
            sp.dma_start(w_qk[:, 0:q_tiles, :], wq.rearrange("c (n d) -> c n d", d=P)).then_inc(loaded, 16)
            sp.dma_start(w_qk[:, q_tiles:, :], wk.rearrange("c (n d) -> c n d", d=P)).then_inc(loaded, 16)
            sp.dma_start(w_v[:], wv).then_inc(loaded, 16)
            if gain is not None:
                sp.dma_start(gain_sb[:], gain).then_inc(loaded, 16)
            if qk_bias is not None:
                sp.dma_start(bias_sb[:], qk_bias).then_inc(loaded, 16)
            if v_bias is not None:
                sp.dma_start(vb_sb[:], v_bias.to_broadcast([P, vdim])).then_inc(loaded, 16)
            if pos is not None:
                sp.dma_start(pos_sb[:], pos).then_inc(loaded, 16)
            with sp.Fori(0, BATCH) as b:
                for half in range(2):
                    c = b * 2 + half
                    for i in range(items):
                        dram, tile = (qs, i) if i < q_tiles else (ks, i - q_tiles)
                        buf = (half * items + i) % NB
                        sp.wait_ge(lo_done, c * items + (i + 1 + NB))
                        sp.dma_start(dram[ds(b, 1), :, tile * P:(tile + 1) * P, half * CH:(half + 1) * CH]
                                     .rearrange("a k f t -> f (a k) t"), parts[buf][:]).then_inc(stored[buf], 16)
                    sp.wait_ge(v_done, (c + 1) * v_items + 2)
                    sp.dma_start(vs[ds(b, 1), :, half * CPT:(half + 1) * CPT, :].rearrange("a p k v -> (a p) k v"),
                                 vpad[half][:].rearrange("p k h v -> p k (h v)")).then_inc(v_stored[half], 16)
            for i in range(NB):
                sp.wait_ge(stored[i], 16 * (CHUNKS * items // NB + 1))
            for i in range(2):
                sp.wait_ge(v_stored[i], 16 * (BATCH + 1))

        @block.tensor
        def _(te):
            te.wait_ge(loaded, 16 * n_loads)
            te.sem_inc(xT_done, 2)
            te.sem_inc(val_done, NB)
            te.sem_inc(v_done, 2)
            with te.Fori(0, BATCH) as b:
                for half in range(2):
                    c = b * 2 + half
                    te.wait_ge(xT_done, c + 1)
                    te.wait_ge(xn_done, c + 1)
                    for t in range(CPT):
                        mm = nc.tensor.transpose(t_ps[half][:, t * P:(t + 1) * P], xn[half][:, t * P:(t + 1) * P], ident[:])
                    mm.then_inc(xT_ready, 1)
                for half in range(2):
                    c = b * 2 + half
                    te.wait_ge(xT_done, c + 3)
                    for i in range(items):
                        te.wait_ge(val_done, c * items + (i + 1))
                        nc.tensor.matmul(item_ps[(half * items + i) % NB][:], w_qk[:, i, :], xnT[:, half, :],
                                         start=True, stop=True).then_inc(item_ready, 1)
                    for i in range(v_items):
                        bank = v_ps[half if v_items == 1 else i % 2]
                        te.wait_ge(v_done, c * v_items + (i + 1))
                        for t in range(CPT // v_items):
                            r = (i + t) * P
                            mm = nc.tensor.matmul(bank[:, t * vdim:(t + 1) * vdim], xnT[:, half, r:r + P], w_v[:],
                                                  start=True, stop=True)
                        mm.then_inc(v_ready, 1)

        @block.scalar
        def _(act):
            for i in range(NB):
                act.sem_inc(stored[i], 16)
            act.wait_ge(loaded, 16 * n_loads)
            with act.Fori(0, BATCH) as b:
                for half in range(2):
                    act.wait_ge(xT_ready, b * 2 + (half + 1))
                    if gain is None:
                        nc.scalar.activation(xnT[:, half, :], t_ps[half][:], ACT.Copy).then_inc(xT_done, 1)
                    else:
                        nc.scalar.activation(xnT[:, half, :], t_ps[half][:], ACT.Identity, bias=gain_sb[:, 1:2],
                                             scale=gain_sb[:, 0:1]).then_inc(xT_done, 1)
                for n in range(2 * items + 1):
                    k = b * (2 * items) + n
                    if n < 2 * items:
                        act.wait_ge(val_done, k + (1 + NB))
                        act.wait_ge(stored[n % NB], (b * (2 * items // NB) + (n // NB + 1)) * 16)
                        nc.scalar.activation(parts[n % NB][:, 0, :], val[n % NB][:], ACT.Copy).then_inc(hi_done, 1)
                    if n > 0:
                        act.wait_ge(rem_done, k + NB)
                        nc.scalar.activation(parts[(n - 1) % NB][:, 1, :], rem[(n - 1) % NB][:], ACT.Copy).then_inc(mid_done, 1)

        @block.gpsimd
        def _(pool):
            for vp in vpad:
                nc.gpsimd.memset(vp[:], 0.0).then_inc(v_preset, 1)
            pool.wait_ge(v_preset, 2)
            for vp in vpad:
                nc.gpsimd.memset(vp[:, :, :, hd:hd + 1], 1.0).then_inc(v_preset, 1)
            pool.sem_inc(lo_done, NB)
            with pool.Fori(0, BATCH) as b:
                for n in range(2 * items):
                    pool.wait_ge(mid_done, b * (2 * items) + (n + 1))
                    nc.gpsimd.tensor_tensor(parts[n % NB][:, 2, :], rem[n % NB][:], parts[n % NB][:, 1, :],
                                            ALU.subtract).then_inc(lo_done, 1)

        @block.vector
        def _(dve):
            dve.sem_inc(v_stored[0], 16)
            dve.sem_inc(v_stored[1], 16)
            dve.sem_inc(rem_done, NB)
            dve.wait_ge(v_preset, 4)
            dve.wait_ge(loaded, 16 * n_loads)
            with dve.Fori(0, BATCH) as b:
                for half in range(2):
                    apply_norm(nc, xn[half], src, mv, rstd, b * KB + half * CPT).then_inc(xn_done, 1)
                def value(n):
                    k, half, i = b * (2 * items) + n, n // items, n % items
                    dve.wait_ge(item_ready, k + 1)
                    dve.wait_ge(rem_done, k + 1)
                    out, fresh = val[n % NB][:], item_ps[n % NB][:]
                    if qk_bias is not None:
                        ins = nc.vector.tensor_scalar(out, fresh, bias_sb[:, i:i + 1], None, ALU.add)
                    elif pos is not None:
                        ins = nc.vector.tensor_tensor(out, fresh, pos_sb[:, half * CH:(half + 1) * CH], ALU.add)
                    else:
                        ins = nc.vector.tensor_copy(out, fresh)
                    ins.then_inc(val_done, 1)

                def remainder(n):
                    k = b * (2 * items) + n
                    dve.wait_ge(hi_done, k + 1)
                    dve.wait_ge(lo_done, k + 1)
                    nc.vector.tensor_tensor(rem[n % NB][:], val[n % NB][:], parts[n % NB][:, 0, :],
                                            ALU.subtract).then_inc(rem_done, 1)

                def values_out(half):
                    c = b * 2 + half
                    for i in range(v_items):
                        dve.wait_ge(v_ready, c * v_items + (i + 1))
                        if i == 0:
                            dve.wait_ge(v_stored[half], (b + 1) * 16)
                        bank = v_ps[half if v_items == 1 else i % 2]
                        t0, tn = (0, CPT) if v_items == 1 else (i, 1)
                        out = vpad[half][:, t0:t0 + tn, :, 0:hd]
                        fresh = bank[:].rearrange("p (t h v) -> p t h v", t=tn, v=hd)
                        if v_bias is None:
                            ins = nc.vector.tensor_copy(out, fresh)
                        else:
                            ins = nc.vector.tensor_tensor(
                                out, fresh, vb_sb[:].rearrange("p (o h v) -> p o h v", o=1, v=hd)
                                .to_broadcast([P, tn, heads, hd]), ALU.add)
                        ins.then_inc(v_done, 1)

                value(0)
                for n in range(2 * items):
                    if n == items - 1:
                        values_out(0)
                    if n + 1 < 2 * items:
                        value(n + 1)
                    remainder(n)
                values_out(1)


PAIRS = 9
SPLIT_ROWS = 96


class Shape:

    def __init__(self, heads, hd, v_width, causal):
        self.heads, self.hd, self.v_width, self.causal = heads, hd, v_width, causal
        self.wide = hd == 64
        self.per_exp = 1 if self.wide else 2
        self.exps = heads // self.per_exp
        self.steps = [(hq, kb) for hq in range(2) for kb in range(KB) if not causal or kb < CPT * (hq + 1)]
        self.slots = [(j, qt, kh) for j in range(heads) for qt in range(KB) for kh in range(2)
                      if not causal or CPT * kh <= qt]
        self.half_end = [max(n for n, (hq, _) in enumerate(self.steps) if hq == h) for h in range(2)]
        self.lead = 3
        self.n = len(self.steps)

    def off(self, hq, kb):
        return max(0, kb - CPT * hq) * P if self.causal else 0

    def a_slots(self, n):
        total = len(self.slots)
        first, last = (n + self.lead) * total // self.n, (n + 1 + self.lead) * total // self.n
        return [(1 + s // total, s % total) for s in range(first, last)]

    def head_start(self):
        return range(self.lead * len(self.slots) // self.n)


def attention(nc, name, shape, scale, qs, ks, vs, ctx_nat, consts, floor=None):
    H, W, S = shape.heads, shape.wide, shape.n
    NA = len(shape.slots)
    vcols = H * shape.v_width
    feats = ctx_nat.shape[1] // TILES
    unit_feats = H * shape.hd
    rows = shape.v_width if W else P
    with ExitStack() as ctx:
        def sb(n, shp, dt=FP32):
            return ctx.enter_context(nc.sbuf_tensor(f"{name}_{n}", shp, dt))

        def ps(n, shp):
            return ctx.enter_context(nc.psum_tensor(f"{name}_{n}", shp, FP32))

        def sem(n):
            return nc.alloc_semaphore(f"{name}_{n}")

        ident, ident_bf, mask_a, mask_b = consts["ident"], consts["ident_bf"], consts["mask_a"], consts["mask_b"]
        R = GROUPS
        NB = 2 if W else 4
        LAG = 1 if W else 2
        TURN = 2
        if W:
            q_op = [sb(f"q_op{i}", [P, 2, H, T], BF16) for i in range(R)]
            k_op = [sb(f"k_op{i}", [P, 3, H, T], BF16) for i in range(R)]
            m_op = [sb(f"m_op{i}", [P, H, T], BF16) for i in range(2)]
        else:
            q_op = [sb(f"q_op{i}", [SPLIT_ROWS, H, T], BF16) for i in range(R)]
            k_op = [sb(f"k_op{i}", [SPLIT_ROWS, H, T], BF16) for i in range(R)]
        v_op = [sb(f"v_op{i}", [P, KB, vcols]) for i in range(R)]
        probs = [sb(f"probs{i}", [P, H, CH]) for i in range(NB)]
        o_sb = [sb(f"o_sb{i}", [P, H if W else 1, CH]) for i in range(2)]
        rec = sb("rec", [P, CPT, H])
        part_max = [sb(f"part_max{i}", [P, 2, H * KB]) for i in range(2)]
        row_max = sb("row_max", [P, H * KB])
        neg_max = sb("neg_max", [H * KB, P])
        neg_rem = sb("neg_rem", [H * KB, P])
        zeros = sb("zeros", [H * KB, 1])
        max_parts = [sb(f"max_parts{i}", [H * KB, 3, P], BF16) for i in range(2)]
        scores = [ps(f"scores{i}", [P, shape.per_exp, CH]) for i in range(2)]
        slot_ps = [ps(f"slot_ps{i}", [P, CH]) for i in range(2)]
        o_ps = ps("o_ps", [P, H if W else 1, CH])
        turn_ps = ps("turn_ps", [P, H if W else 1, CH])

        preset = sem("preset")
        op_loaded = [sem(f"op_loaded{i}") for i in range(R)]
        max_loaded = [sem(f"max_loaded{i}") for i in range(R)]
        slot_ready, slot_done = sem("slot_ready"), sem("slot_done")
        row_max_done, neg_done, parts_done, pool_step = (
            sem("row_max_done"), sem("neg_done"), sem("parts_done"), sem("pool_step"))
        scores_ready, probs_done, pv_done = sem("scores_ready"), sem("probs_done"), sem("pv_done")
        o_copied, turned, turn_free, rec_done = sem("o_copied"), sem("turned"), sem("turn_free"), sem("rec_done")
        block = ctx.enter_context(nc.Block())

        def unit(b, g):
            return b * GROUPS + g

        def next_unit(b, g, d):
            return (b, g + d) if g + d < GROUPS else (b + 1, g + d - GROUPS)

        n_loads = 11 if W else 21
        turns = 3 * GROUPS

        @block.sync
        def _(sp):
            def load(b, g):
                i = g
                b_ = ds(b, 1)
                if not W:
                    f0 = g * 32
                    for a in range(3):
                        for c in range(3):
                            r0 = (3 * a + c) * 8
                            for op, dram, part in ((q_op, qs, a), (k_op, ks, c)):
                                sp.dma_start(op[i][r0:r0 + 8, :, :],
                                             dram[b_, part, f0:f0 + 32, :]
                                             .rearrange("a (j r) t -> (a r) j t", r=8)).then_inc(op_loaded[i], 16)
                    sp.dma_start(q_op[i][72:75, :, :].rearrange("r j t -> r (j t)"), consts["zero_rows"]).then_inc(op_loaded[i], 16)
                    sp.dma_start(k_op[i][72:75, :, :].rearrange("r j t -> r (j t)"), consts["one_rows"]).then_inc(op_loaded[i], 16)
                    sp.dma_start(v_op[i][:], vs[b_, :, :, g * vcols:(g + 1) * vcols]
                                 .rearrange("a p k v -> (a p) k v")).then_inc(op_loaded[i], 16)
                else:
                    f0 = g * H * 64

                    def fetch(op, which, row, dram, part):
                        sp.dma_start(op[i][row:row + 64, which, :, :],
                                     dram[b_, part, f0:f0 + H * 64, :]
                                     .rearrange("a (j r) t -> (a r) j t", r=64)).then_inc(op_loaded[i], 16)

                    fetch(q_op, 0, 0, qs, 0)
                    fetch(q_op, 0, 64, qs, 1)
                    fetch(q_op, 1, 0, qs, 0)
                    fetch(q_op, 1, 64, qs, 2)
                    fetch(k_op, 0, 0, ks, 0)
                    fetch(k_op, 0, 64, ks, 0)
                    fetch(k_op, 1, 0, ks, 1)
                    fetch(k_op, 1, 64, ks, 1)
                    fetch(k_op, 2, 0, ks, 2)
                    fetch(k_op, 2, 64, ks, 0)
                    sp.dma_start(v_op[i][:], vs[b_, :, :, g * vcols:(g + 1) * vcols]
                                 .rearrange("a p k v -> (a p) k v")).then_inc(op_loaded[i], 16)

            def load_max(b, g):
                i = g
                sp.wait_ge(parts_done, unit(b, g) + 1)
                for part in range(3):
                    row = m_op[i % 2][part:part + 1, :, :] if W else q_op[i][72 + part:73 + part, :, :]
                    sp.dma_start(row.rearrange("r j t -> r (j t)"), max_parts[g % 2][:, part, :]).then_inc(max_loaded[i], 16)

            def sequence(b, last):
                for g in range(GROUPS):
                    if g < GROUPS - 1:
                        load_max(b, g + 1)
                    elif not last:
                        load_max(b + 1, 0)
                    if not last:
                        sp.wait_ge(pv_done, (unit(b, g) + 1) * S + NB)
                        load(b + 1, g)

            for g in range(R):
                if not W:
                    sp.wait_ge(preset, g + 1)
                load(0, g)
            if W:
                sp.wait_ge(preset, 1)
            load_max(0, 0)
            with sp.Fori(0, BATCH - 1) as b:
                sequence(b, False)
            sequence(BATCH - 1, True)

        @block.tensor
        def _(te):
            te.sem_inc(probs_done, shape.exps)
            te.sem_inc(o_copied, 1)
            def a_slot(b, g, s):
                j, qt, kh = shape.slots[s]
                i = g
                k = unit(b, g) * NA + s
                if s == 0:
                    te.wait_ge(op_loaded[i], (b + 1) * (16 * n_loads))
                if not (isinstance(k, int) and k < 2):
                    te.wait_ge(slot_done, k - 1)
                width = min(CH, (qt + 1) * P - kh * CH) if shape.causal else CH
                out = slot_ps[s % 2]
                q0, k0 = qt * P, kh * CH
                diag = shape.causal and qt // CPT == kh
                if W:
                    pairs = [(q_op[i][:, 0, j, q0:q0 + P], k_op[i][:, n, j, k0:k0 + width]) for n in range(2)]
                else:
                    pairs = [(q_op[i][:, j, q0:q0 + P], k_op[i][:, j, k0:k0 + width])]
                for n, (q, k_) in enumerate(pairs):
                    mm = nc.tensor.matmul(out[:, 0:width], q, k_, start=n == 0, stop=n == len(pairs) - 1 and not diag)
                if diag:
                    mm = nc.tensor.matmul(out[:, width - P:width], ident_bf[:], mask_a[:], start=False, stop=True)
                mm.then_inc(slot_ready, 1)

            def max_turn(b, g, k):
                te.wait_ge(row_max_done, unit(b, g) + 1)
                if not (isinstance(k, int) and k == 0):
                    te.wait_ge(turn_free, k)
                nc.tensor.transpose(turn_ps[0:H * KB, 0, 0:P], row_max[:], ident[:]).then_inc(turned, 1)

            def o_turn(b, g, hq, k):
                te.wait_ge(o_copied, unit(b, g) * 2 + (hq + 2))
                te.wait_ge(turn_free, k)
                for j in range(H if W else 1):
                    for t in range(CPT):
                        mm = nc.tensor.transpose(turn_ps[:, j, t * rows:(t + 1) * rows],
                                                 o_sb[hq][0:rows, j, t * P:(t + 1) * P], ident[0:rows, 0:rows])
                mm.then_inc(turned, 1)

            def step_scores(b, g, n, e):
                hq, kb = shape.steps[n]
                i = g
                off = shape.off(hq, kb)
                gs = unit(b, g) * S + n
                te.wait_ge(probs_done, gs * shape.exps + (e + 1))
                diag = shape.causal and kb >= CPT * hq
                for jj in range(shape.per_exp):
                    j = e * shape.per_exp + jj
                    out = scores[e][:, jj, off:CH]
                    k0, q0, q1 = kb * P, hq * CH + off, (hq + 1) * CH
                    if W:
                        pairs = [(k_op[i][:, n_, j, k0:k0 + P], q_op[i][:, m_, j, q0:q1]) for n_, m_ in ((0, 0), (1, 0), (2, 1))]
                        pairs.append((consts["one_stat"][:], m_op[i % 2][:, j, q0:q1]))
                    else:
                        pairs = [(k_op[i][:, j, k0:k0 + P], q_op[i][:, j, q0:q1])]
                    for n_, (k_, q) in enumerate(pairs):
                        mm = nc.tensor.matmul(out, k_, q, start=n_ == 0, stop=n_ == len(pairs) - 1 and not diag)
                    if diag:
                        mm = nc.tensor.matmul(scores[e][:, jj, off:off + P], ident_bf[:], mask_b[:], start=False, stop=True)
                mm.then_inc(scores_ready, 1)

            def step_pv(b, g, n, part=None):
                hq, kb = shape.steps[n]
                i = g
                off = shape.off(hq, kb)
                if part != 1:
                    te.wait_ge(probs_done, (unit(b, g) * S + (n + 1)) * shape.exps + shape.exps)
                    if kb == 0:
                        te.wait_ge(o_copied, unit(b, g) * 2 + (hq + 1))
                whole = part is None or kb == 0
                if whole and part == 1:
                    return
                middle = (off + CH) // 2
                c0, c1 = (off, CH) if whole else (off, middle) if part == 0 else (middle, CH)
                for j in range(H):
                    v = v_op[i][:, kb, j * shape.v_width:(j + 1) * shape.v_width]
                    out = o_ps[0:shape.v_width, j, c0:c1] if W else o_ps[32 * j:32 * j + 32, 0, c0:c1]
                    mm = nc.tensor.matmul(out, v, probs[n % NB][:, j, c0:c1], start=kb == 0,
                                          stop=n in shape.half_end and part != 0)
                if whole or part == 1:
                    mm.then_inc(pv_done, 1)

            def behind(b, g, n, k, part=None):
                if n >= LAG:
                    step_pv(b, g, n - LAG, part)
                elif g > 0:
                    step_pv(b, g - 1, S + n - LAG, part)
                if part == 0:
                    return
                if n == TURN and g > 0:
                    o_turn(b, g - 1, 1, k - 1)
                if n == shape.half_end[0] + TURN + 1:
                    o_turn(b, g, 0, k)

            def sequence(b, last):
                for g in range(GROUPS):
                    k = b * turns + (3 * g + 1)
                    te.wait_ge(max_loaded[g], (b + 1) * (3 * 16) + 16)
                    for n in range(S):
                        ahead = [(d, s) for d, s in shape.a_slots(n) if not last or g + d < GROUPS]
                        places = 2 if W else 4
                        cut = [len(ahead) * p // places for p in range(places + 1)]

                        def fill_slots(p):
                            for d, s in ahead[cut[p]:cut[p + 1]]:
                                a_slot(*next_unit(b, g, d), s)

                        if W:
                            for e in range(shape.exps):
                                step_scores(b, g, n, e)
                                fill_slots(e)
                            behind(b, g, n, k)
                        else:
                            for e in range(shape.exps):
                                behind(b, g, n, k, e)
                                fill_slots(2 * e)
                                step_scores(b, g, n, e)
                                fill_slots(2 * e + 1)
                        if n == S - shape.lead and not (last and g == GROUPS - 1):
                            max_turn(*next_unit(b, g, 1), k + 1)
                for n in range(S - LAG, S):
                    step_pv(b, GROUPS - 1, n)
                o_turn(b, GROUPS - 1, 1, b * turns + turns if not last else b * turns + turns - 1)

            for s in range(NA):
                a_slot(0, 0, s)
            max_turn(0, 0, 0)
            for s in shape.head_start():
                a_slot(0, 1, s)
            with te.Fori(0, BATCH - 1) as b:
                sequence(b, False)
            sequence(BATCH - 1, True)

        @block.gpsimd
        def _(pool):
            nc.gpsimd.memset(zeros[:], 0.0).then_inc(pool_step, 1)
            pool.wait_ge(pool_step, 1)
            for i in range(R):
                pool.sem_inc(max_loaded[i], 16)

            def split_max(b, g, k):
                out = max_parts[g % 2]
                u = unit(b, g)
                pool.wait_ge(turn_free, k + 1)
                if not (isinstance(u, int) and u < 2):
                    pool.wait_ge(max_loaded[(g + 2) % R], (b if g < 2 else b + 1) * 48 + 16)
                nc.gpsimd.tensor_tensor(out[:, 0, :], neg_max[:], zeros[:].to_broadcast([H * KB, P]), ALU.add).then_inc(pool_step, 1)
                pool.wait_ge(pool_step, u * 3 + 2)
                nc.gpsimd.tensor_tensor(neg_rem[:], neg_max[:], out[:, 0, :], ALU.subtract).then_inc(pool_step, 1)
                pool.wait_ge(pool_step, u * 3 + 3)
                nc.gpsimd.tensor_tensor(out[:, 1, :], neg_rem[:], zeros[:].to_broadcast([H * KB, P]), ALU.add).then_inc(pool_step, 1)
                pool.wait_ge(pool_step, u * 3 + 4)
                nc.gpsimd.tensor_tensor(out[:, 2, :], neg_rem[:], out[:, 1, :], ALU.subtract).then_inc(parts_done, 1)

            def sequence(b, last):
                for g in range(GROUPS - 1 if last else GROUPS):
                    split_max(*next_unit(b, g, 1), b * turns + (3 * g + 2))

            split_max(0, 0, 0)
            with pool.Fori(0, BATCH - 1) as b:
                sequence(b, False)
            sequence(BATCH - 1, True)

        @block.scalar
        def _(act):
            act.sem_inc(pv_done, NB)

            def copy_out(b, g, hq):
                act.wait_ge(pv_done, unit(b, g) * S + (shape.half_end[hq] + 1 + NB))
                nc.scalar.activation(o_sb[hq][0:rows, :, :], o_ps[0:rows, :, :], ACT.Copy).then_inc(o_copied, 1)

            def copies(b, g, n):
                if n == LAG - 1 and g > 0:
                    copy_out(b, g - 1, 1)
                if n == shape.half_end[0] + LAG:
                    copy_out(b, g, 0)

            def sequence(b):
                for g in range(GROUPS):
                    for n, (hq, kb) in enumerate(shape.steps):
                        off = shape.off(hq, kb)
                        gs = unit(b, g) * S + n
                        if not W:
                            copies(b, g, n)
                        for e in range(shape.exps):
                            act.wait_ge(scores_ready, gs * shape.exps + (e + 1))
                            if e == 0:
                                act.wait_ge(pv_done, gs + 1)
                            j = e * shape.per_exp
                            nc.scalar.activation(probs[n % NB][:, j:j + shape.per_exp, off:CH], scores[e][:, :, off:CH],
                                                 ACT.Exp, scale=scale).then_inc(probs_done, 1)
                        if W:
                            copies(b, g, n)
                copy_out(b, GROUPS - 1, 1)

            with act.Fori(0, BATCH) as b:
                sequence(b)

        @block.vector
        def _(dve):
            if W:
                for i in range(2):
                    ins = nc.vector.memset(m_op[i][:], 0.0)
                ins.then_inc(preset, 1)
            else:
                for i in range(R):
                    nc.vector.memset(q_op[i][64:96, :, :], 0.0)
                    nc.vector.memset(k_op[i][64:96, :, :], 0.0).then_inc(preset, 1)
            if shape.causal:
                for i in range(2):
                    nc.vector.memset(part_max[i][:, 1, :], -3e38).then_inc(rec_done, 1)
            base = 2 if shape.causal else 0

            def a_slot(b, g, s):
                j, qt, kh = shape.slots[s]
                width = min(CH, (qt + 1) * P - kh * CH) if shape.causal else CH
                col = j * KB + qt
                dve.wait_ge(slot_ready, unit(b, g) * NA + (s + 1))
                nc.vector.tensor_reduce(part_max[g % 2][:, kh, col:col + 1], slot_ps[s % 2][:, 0:width],
                                        axis=AX.X, op=ALU.max).then_inc(slot_done, 1)

            def row_maxima(b, g, k):
                u = unit(b, g)
                dve.wait_ge(slot_done, (u + 1) * NA)
                nc.vector.tensor_tensor(row_max[:], part_max[g % 2][:, 0, :], part_max[g % 2][:, 1, :],
                                        ALU.max).then_inc(row_max_done, 1)
                dve.wait_ge(turned, k + 1)
                if not (isinstance(u, int) and u == 0):
                    dve.wait_ge(parts_done, u)
                nc.vector.tensor_scalar(neg_max[:], turn_ps[0:H * KB, 0, 0:P], -1.0, None, ALU.mult).then_inc(turn_free, 1)

            def normalise(b, g, hq, k):
                dve.wait_ge(turned, k + 1)
                count = (unit(b, g) * 2 + hq) * (2 if floor else 1) + (1 + base)
                if W:
                    o = turn_ps[:, :, 0:CPT * rows].rearrange("p j (t v) -> p t j v", v=rows)
                else:
                    o = turn_ps[:, 0, :].rearrange("p (t j v) -> p t j v", t=CPT, j=H)
                sums = o[:, :, :, shape.hd]
                if floor:
                    nc.vector.tensor_scalar(rec[:], sums, floor, None, ALU.max).then_inc(rec_done, 1)
                    dve.wait_ge(rec_done, count)
                    nc.vector.reciprocal(rec[:], rec[:]).then_inc(rec_done, 1)
                    dve.wait_ge(rec_done, count + 1)
                else:
                    nc.vector.reciprocal(rec[:], sums).then_inc(rec_done, 1)
                    dve.wait_ge(rec_done, count)
                out = (ctx_nat[:, ds(b * (KB * feats) + hq * CPT * feats, CPT * feats)]
                       .rearrange("p (t f) -> p t f", f=feats)[:, :, g * unit_feats:(g + 1) * unit_feats]
                       .rearrange("p t (j d) -> p t j d", d=shape.hd))
                nc.vector.tensor_tensor(out, o[:, :, :, 0:shape.hd],
                                        rec[:].unsqueeze(3).to_broadcast([P, CPT, H, shape.hd]),
                                        ALU.mult).then_inc(turn_free, 1)

            def sequence(b, last):
                for g in range(GROUPS):
                    k = b * turns + (3 * g + 1)
                    for n in range(S):
                        for d, s in shape.a_slots(n):
                            if not last or g + d < GROUPS:
                                a_slot(*next_unit(b, g, d), s)
                        if n == TURN and g > 0:
                            normalise(b, g - 1, 1, k - 1)
                        if n == shape.half_end[0] + TURN + 1:
                            normalise(b, g, 0, k)
                        if n == S - shape.lead and not (last and g == GROUPS - 1):
                            row_maxima(*next_unit(b, g, 1), k + 1)
                normalise(b, GROUPS - 1, 1, b * turns + (turns - 1 if last else turns))

            for s in range(NA):
                a_slot(0, 0, s)
            row_maxima(0, 0, 0)
            for s in shape.head_start():
                a_slot(0, 1, s)
            with dve.Fori(0, BATCH - 1) as b:
                sequence(b, False)
            sequence(BATCH - 1, True)


def out_project(nc, name, nat, feats, wo, x, consts, bias=None, rms=None):
    ft = feats // P
    with ExitStack() as ctx:
        def sb(n, shp, dt=FP32):
            return ctx.enter_context(nc.sbuf_tensor(f"{name}_{n}", shp, dt))

        def sem(n):
            return nc.alloc_semaphore(f"{name}_{n}")

        w = sb("w", [P, ft, D])
        bias_sb = sb("bias_sb", [P, D])
        stage = [sb(f"stage{i}", [P, CPT * feats]) for i in range(2)]
        natT = [sb(f"natT{i}", [P, ft, CH]) for i in range(2)]
        biased = sb("biased", [P, CPT, D])
        t_ps = ctx.enter_context(nc.psum_tensor(f"{name}_t_ps", [P, ft, CH], FP32))
        y_ps = [ctx.enter_context(nc.psum_tensor(f"{name}_y_ps{i}", [P, CH], FP32)) for i in range(2)]
        loaded, staged, turned, copied, y_ready, y_done, biased_done = (
            sem(n) for n in ("loaded", "staged", "turned", "copied", "y_ready", "y_done", "biased_done"))
        if rms is not None:
            group, eps_value, factor, weight = rms
            n_groups = TILES * feats // group
            weight_sb = sb("weight_sb", [P, 1])
            eps = sb("eps", [P, 1])
            square = sb("square", [P, TILES * feats])
            ms = sb("ms", [P, n_groups])
            rs = sb("rs", [P, n_groups])
            sq_done, ms_done, root_done, rs_done = (sem(n) for n in ("sq_done", "ms_done", "root_done", "rs_done"))
        n_loads = 1 + (bias is not None) + (rms is not None)
        block = ctx.enter_context(nc.Block())

        @block.sync
        def _(sp):
            sp.dma_start(w[:], wo.rearrange("(n p) d -> p n d", p=P)).then_inc(loaded, 16)
            if bias is not None:
                sp.dma_start(bias_sb[:], bias.to_broadcast([P, D])).then_inc(loaded, 16)
            if rms is not None:
                sp.dma_start(weight_sb[:], weight).then_inc(loaded, 16)

        @block.tensor
        def _(te):
            te.wait_ge(loaded, 16 * n_loads)
            te.sem_inc(copied, 1)
            te.sem_inc(y_done, 2)
            with te.Fori(0, BATCH) as b:
                for half in range(2):
                    c = b * 2 + half
                    te.wait_ge(staged, c + 1)
                    te.wait_ge(copied, c + 1)
                    for f in range(ft):
                        for t in range(CPT):
                            mm = nc.tensor.transpose(t_ps[:, f, t * P:(t + 1) * P],
                                                     stage[half][:, t * feats + f * P:t * feats + (f + 1) * P],
                                                     consts["ident"][:])
                    mm.then_inc(turned, 1)
                    te.wait_ge(copied, c + 2)
                    te.wait_ge(y_done, c + 1)
                    for t in range(CPT):
                        for f in range(ft):
                            mm = nc.tensor.matmul(y_ps[half][:, t * D:(t + 1) * D], natT[half][:, f, t * P:(t + 1) * P],
                                                  w[:, f, :], start=f == 0, stop=f == ft - 1)
                    mm.then_inc(y_ready, 1)

        @block.scalar
        def _(act):
            act.wait_ge(loaded, 16 * n_loads)
            if rms is not None:
                nc.scalar.activation(square[:], nat[:], ACT.Square).then_inc(sq_done, 1)
                act.wait_ge(ms_done, 2)
                nc.scalar.activation(rs[:], ms[:], ACT.Sqrt, bias=eps[:, 0:1], scale=1.0 / group).then_inc(root_done, 1)
            with act.Fori(0, BATCH) as b:
                for half in range(2):
                    act.wait_ge(turned, b * 2 + (half + 1))
                    if rms is None:
                        nc.scalar.activation(natT[half][:], t_ps[:], ACT.Copy).then_inc(copied, 1)
                    else:
                        nc.scalar.activation(natT[half][:], t_ps[:], ACT.Copy, scale=weight_sb[:, 0:1]).then_inc(copied, 1)

        @block.vector
        def _(dve):
            dve.wait_ge(loaded, 16 * n_loads)
            if rms is not None:
                nc.vector.memset(eps[:], eps_value).then_inc(ms_done, 1)
                dve.wait_ge(sq_done, 1)
                nc.vector.tensor_reduce(ms[:], square[:].rearrange("p (n g) -> p n g", g=group),
                                        axis=AX.X, op=ALU.add).then_inc(ms_done, 1)
                dve.wait_ge(root_done, 1)
                nc.vector.reciprocal(rs[:], rs[:]).then_inc(rs_done, 1)
                dve.wait_ge(rs_done, 1)
                nc.vector.tensor_scalar(rs[:], rs[:], factor, None, ALU.mult).then_inc(rs_done, 1)
                dve.wait_ge(rs_done, 2)
            with dve.Fori(0, BATCH) as b:
                for half in range(2):
                    part = nat[:, ds(b * (KB * feats) + half * CPT * feats, CPT * feats)]
                    if rms is None:
                        nc.vector.tensor_scalar(stage[half][:], part, 1.0, None, ALU.mult).then_inc(staged, 1)
                    else:
                        n = CPT * feats // group
                        nc.vector.tensor_tensor(stage[half][:].rearrange("p (n g) -> p n g", g=group),
                                                part.rearrange("p (n g) -> p n g", g=group),
                                                rs[:, ds(b * (2 * n) + half * n, n)].unsqueeze(2)
                                                .to_broadcast([P, n, group]), ALU.mult).then_inc(staged, 1)
                for half in range(2):
                    c = b * 2 + half
                    rows = x[:, ds(b * (KB * D) + half * CH, CH)]
                    dve.wait_ge(y_ready, c + 1)
                    if bias is None:
                        nc.vector.tensor_tensor(rows, rows, y_ps[half][:], ALU.add).then_inc(y_done, 1)
                    else:
                        dve.wait_ge(y_done, c + 2)
                        nc.vector.tensor_tensor(biased[:], y_ps[half][:].rearrange("p (t d) -> p t d", d=D),
                                                bias_sb[:].unsqueeze(1).to_broadcast([P, CPT, D]),
                                                ALU.add).then_inc(biased_done, 1)
                        dve.wait_ge(biased_done, c + 1)
                        nc.vector.tensor_tensor(rows, rows, biased[:].rearrange("p t d -> p (t d)"),
                                                ALU.add).then_inc(y_done, 1)


PAIR_PARTS = [(0, 0), (0, 1), (1, 0), (0, 2), (2, 0), (1, 1)]
MAP_ROWS = len(PAIR_PARTS) * 8


def cosine_scales(nc, name, raw, delta_col, delta_row, gain_col, sign_col, lambdas, factors, neg_lambda):
    with ExitStack() as ctx:
        def sb(n, shp):
            return ctx.enter_context(nc.sbuf_tensor(f"{name}_{n}", shp, FP32))

        raw_sb, col, row = sb("raw_sb", [P, 1]), sb("col", [P, 1]), sb("row", [P, 8])
        gain, sign, lam = sb("gain", [P, 1]), sb("sign", [P, 1]), sb("lam", [P, 4, 8])
        prod, dots, mean, tanh, sig = sb("prod", [P, 2, 8]), sb("dots", [P, 2]), sb("mean", [P, 1]), sb("tanh", [P, 1]), sb("sig", [P, 1])
        loaded = nc.alloc_semaphore(f"{name}_loaded")
        step = nc.alloc_semaphore(f"{name}_step")
        acted = nc.alloc_semaphore(f"{name}_acted")
        block = ctx.enter_context(nc.Block())

        @block.sync
        def _(sp):
            sp.dma_start(raw_sb[:], raw.to_broadcast([P, 1])).then_inc(loaded, 16)
            sp.dma_start(col[:], delta_col).then_inc(loaded, 16)
            sp.dma_start(row[:], delta_row.to_broadcast([P, 8])).then_inc(loaded, 16)
            sp.dma_start(gain[:], gain_col).then_inc(loaded, 16)
            sp.dma_start(sign[:], sign_col).then_inc(loaded, 16)
            sp.dma_start(lam[:].rearrange("p a b -> p (a b)"), lambdas.to_broadcast([P, 32])).then_inc(loaded, 16)

        @block.scalar
        def _(act):
            act.wait_ge(loaded, 96)
            nc.scalar.activation(sig[:], raw_sb[:], ACT.Exp, scale=-1.0).then_inc(acted, 1)
            act.wait_ge(step, 3)
            nc.scalar.activation(tanh[:], col[:], ACT.Tanh).then_inc(acted, 1)
            act.wait_ge(step, 5)
            nc.scalar.activation(dots[:], dots[:], ACT.Exp).then_inc(acted, 1)

        @block.vector
        def _(dve):
            count = [0]

            def then(ins):
                count[0] += 1
                ins.then_inc(step, 1)
                dve.wait_ge(step, count[0])

            dve.wait_ge(loaded, 96)
            then(nc.vector.tensor_reduce(mean[:], row[:], axis=AX.X, op=ALU.add))
            then(nc.vector.tensor_scalar(mean[:], mean[:], 1.0 / 8, None, ALU.mult))
            then(nc.vector.tensor_tensor(col[:], col[:], mean[:], ALU.subtract))
            then(nc.vector.tensor_tensor(prod[:], lam[:, 0:2, :], lam[:, 2:4, :], ALU.mult))
            then(nc.vector.tensor_reduce(dots[:], prod[:], axis=AX.X, op=ALU.add))
            dve.wait_ge(acted, 3)
            then(nc.vector.tensor_scalar(sig[:], sig[:], 1.0, None, ALU.add))
            then(nc.vector.reciprocal(sig[:], sig[:]))
            then(nc.vector.tensor_scalar(sig[:], sig[:], 15.0, None, ALU.mult))
            then(nc.vector.tensor_scalar(tanh[:], tanh[:], 0.5, 1.0, ALU.mult, ALU.add))
            then(nc.vector.tensor_tensor(factors[:, 0:1], sig[:], tanh[:], ALU.mult))
            then(nc.vector.tensor_tensor(gain[:], gain[:], sign[:], ALU.mult))
            then(nc.vector.tensor_tensor(factors[:, 1:2], factors[:, 0:1], gain[:], ALU.mult))
            then(nc.vector.tensor_tensor(neg_lambda[:], dots[:, 1:2], dots[:, 0:1], ALU.subtract))
            then(nc.vector.tensor_scalar(neg_lambda[:], neg_lambda[:], -0.5, None, ALU.add))


def project_cosine(nc, name, src, mv, rstd, wq, wk, wv, factors, ql, qd, ks, vs, ident):
    items = 3
    with ExitStack() as ctx:
        def sb(n, shp, dt=FP32):
            return ctx.enter_context(nc.sbuf_tensor(f"{name}_{n}", shp, dt))

        def ps(n):
            return ctx.enter_context(nc.psum_tensor(f"{name}_{n}", [P, CH], FP32))

        def sem(n):
            return nc.alloc_semaphore(f"{name}_{n}")

        w = [sb(f"w{i}", [P, D]) for i in range(3)]
        NB = 2 * items
        UNITS_B = 4
        xn = [sb(f"xn{i}", [P, CH]) for i in range(2)]
        xnT = sb("xnT", [P, 2, CH])
        square = [sb(f"square{i}", [P, CH]) for i in range(UNITS_B)]
        groups = CH // 8
        ss = sb("ss", [P, UNITS_B, groups])
        root = sb("root", [P, UNITS_B, groups])
        newton = sb("newton", [P, UNITS_B, groups])
        unit = [sb(f"unit{i}", [P, CH]) for i in range(UNITS_B)]
        val = [sb(f"val{i}", [P, CH]) for i in range(NB)]
        rem = [sb(f"rem{i}", [P, CH]) for i in range(NB)]
        parts = [sb(f"parts{i}", [P, 3, CH], BF16) for i in range(NB)]
        vpad = [sb(f"vpad{i}", [P, CPT, 8, 32]) for i in range(2)]
        v_ps = [ps(f"v_ps{i}") for i in range(2)]
        nat_ps = [ps(f"nat_ps{i}") for i in range(UNITS_B)]
        turn_ps = [ps(f"turn_ps{i}") for i in range(2)]
        (loaded, xn_done, xT_ready, xT_done, nat_ready, sq_done, ss_done, root_done, step, unit_done, unitT_ready,
         val_done, hi_done, rem_done, mid_done, lo_done, v_ready, v_done, v_preset) = (sem(n) for n in (
             "loaded", "xn_done", "xT_ready", "xT_done", "nat_ready", "sq_done", "ss_done", "root_done", "step",
             "unit_done", "unitT_ready", "val_done", "hi_done", "rem_done", "mid_done", "lo_done", "v_ready",
             "v_done", "v_preset"))
        stored = [sem(f"stored{i}") for i in range(NB)]
        v_stored = [sem(f"v_stored{i}") for i in range(2)]
        block = ctx.enter_context(nc.Block())

        @block.sync
        def _(sp):
            for i, dram in enumerate((wq, wk, wv)):
                sp.dma_start(w[i][:], dram).then_inc(loaded, 16)
            with sp.Fori(0, BATCH) as b:
                for half in range(2):
                    for i, dram in enumerate((ql, ks, qd)):
                        n = half * items + i
                        sp.wait_ge(lo_done, b * NB + (n + 1))
                        sp.dma_start(dram[ds(b, 1), :, :, half * CH:(half + 1) * CH]
                                     .rearrange("a k f t -> f (a k) t"), parts[n][:]).then_inc(stored[n], 16)
                    sp.wait_ge(v_done, b * 2 + (half + 3))
                    sp.dma_start(vs[ds(b, 1), :, half * CPT:(half + 1) * CPT, :].rearrange("a p k v -> (a p) k v"),
                                 vpad[half][:].rearrange("p k h v -> p k (h v)")).then_inc(v_stored[half], 16)
            for i in range(NB):
                sp.wait_ge(stored[i], 16 * (BATCH + 1))
            for i in range(2):
                sp.wait_ge(v_stored[i], 16 * (BATCH + 1))

        @block.tensor
        def _(te):
            te.wait_ge(loaded, 48)
            te.sem_inc(val_done, 1)
            te.sem_inc(v_done, 2)
            with te.Fori(0, BATCH) as b:
                te.wait_ge(val_done, b * NB + 1)
                for half in range(2):
                    te.wait_ge(xn_done, b * 2 + (half + 1))
                    for t in range(CPT):
                        mm = nc.tensor.transpose(turn_ps[half][:, t * P:(t + 1) * P], xn[half][:, t * P:(t + 1) * P], ident[:])
                    mm.then_inc(xT_ready, 1)
                for half in range(2):
                    te.wait_ge(xT_done, b * 2 + (half + 1))
                    for i in range(2):
                        for t in range(CPT):
                            mm = nc.tensor.matmul(nat_ps[2 * half + i][:, t * P:(t + 1) * P], xnT[:, half, t * P:(t + 1) * P],
                                                  w[i][:], start=True, stop=True)
                        mm.then_inc(nat_ready, 1)
                for half in range(2):
                    te.wait_ge(v_done, b * 2 + (half + 1))
                    for t in range(CPT):
                        mm = nc.tensor.matmul(v_ps[half][:, t * P:(t + 1) * P], xnT[:, half, t * P:(t + 1) * P], w[2][:],
                                              start=True, stop=True)
                    mm.then_inc(v_ready, 1)
                for half in range(2):
                    if half:
                        te.wait_ge(val_done, b * NB + (items + 1))
                    for i in range(2):
                        u = 2 * half + i
                        te.wait_ge(unit_done, b * UNITS_B + (u + 1))
                        for t in range(CPT):
                            mm = nc.tensor.transpose(turn_ps[i][:, t * P:(t + 1) * P], unit[u][:, t * P:(t + 1) * P], ident[:])
                        mm.then_inc(unitT_ready, 1)

        @block.scalar
        def _(act):
            for i in range(NB):
                act.sem_inc(stored[i], 16)
            with act.Fori(0, BATCH) as b:
                for half in range(2):
                    act.wait_ge(xT_ready, b * 2 + (half + 1))
                    nc.scalar.activation(xnT[:, half, :], turn_ps[half][:], ACT.Copy).then_inc(xT_done, 1)
                for u in range(UNITS_B):
                    act.wait_ge(nat_ready, b * UNITS_B + (u + 1))
                    nc.scalar.activation(square[u][:], nat_ps[u][:], ACT.Square).then_inc(sq_done, 1)
                act.wait_ge(ss_done, (b + 1) * (UNITS_B + 1))
                nc.scalar.activation(root[:], ss[:], ACT.Sqrt).then_inc(root_done, 1)
                for n in range(NB + 1):
                    if n < NB:
                        act.wait_ge(val_done, b * NB + (n + 2))
                        act.wait_ge(stored[n], (b + 1) * 16)
                        nc.scalar.activation(parts[n][:, 0, :], val[n][:], ACT.Copy).then_inc(hi_done, 1)
                    if n > 0:
                        act.wait_ge(rem_done, b * NB + n)
                        nc.scalar.activation(parts[n - 1][:, 1, :], rem[n - 1][:], ACT.Copy).then_inc(mid_done, 1)

        @block.gpsimd
        def _(pool):
            for vp in vpad:
                nc.gpsimd.memset(vp[:], 0.0).then_inc(v_preset, 1)
            pool.wait_ge(v_preset, 2)
            for vp in vpad:
                nc.gpsimd.memset(vp[:, :, :, 16:17], 1.0).then_inc(v_preset, 1)
            with pool.Fori(0, BATCH) as b:
                for n in range(NB):
                    pool.wait_ge(mid_done, b * NB + (n + 1))
                    nc.gpsimd.tensor_tensor(parts[n][:, 2, :], rem[n][:], parts[n][:, 1, :], ALU.subtract).then_inc(lo_done, 1)

        @block.vector
        def _(dve):
            dve.sem_inc(v_stored[0], 16)
            dve.sem_inc(v_stored[1], 16)
            dve.wait_ge(v_preset, 4)
            with dve.Fori(0, BATCH) as b:
                for half in range(2):
                    apply_norm(nc, xn[half], src, mv, rstd, b * KB + half * CPT).then_inc(xn_done, 1)
                for u in range(UNITS_B):
                    dve.wait_ge(sq_done, b * UNITS_B + (u + 1))
                    nc.vector.tensor_reduce(ss[:, u, :], square[u][:].rearrange("p (n g) -> p n g", g=8),
                                            axis=AX.X, op=ALU.add).then_inc(ss_done, 1)
                dve.wait_ge(ss_done, b * (UNITS_B + 1) + UNITS_B)
                nc.vector.tensor_scalar(ss[:], ss[:], 1e-12, None, ALU.max).then_inc(ss_done, 1)
                for half in range(2):
                    dve.wait_ge(v_ready, b * 2 + (half + 1))
                    dve.wait_ge(v_stored[half], (b + 1) * 16)
                    nc.vector.tensor_copy(vpad[half][:, :, :, 0:16], v_ps[half][:].rearrange("p (t h v) -> p t h v", t=CPT, v=16)) \
                        .then_inc(v_done, 1)
                dve.wait_ge(root_done, b + 1)
                nc.vector.reciprocal(root[:], root[:]).then_inc(step, 1)
                dve.wait_ge(step, b * 5 + 1)
                nc.vector.tensor_tensor(newton[:], root[:], root[:], ALU.mult).then_inc(step, 1)
                dve.wait_ge(step, b * 5 + 2)
                nc.vector.tensor_tensor(newton[:], newton[:], ss[:], ALU.mult).then_inc(step, 1)
                dve.wait_ge(step, b * 5 + 3)
                nc.vector.tensor_scalar(newton[:], newton[:], -0.5, 1.5, ALU.mult, ALU.add).then_inc(step, 1)
                dve.wait_ge(step, b * 5 + 4)
                nc.vector.tensor_tensor(root[:], root[:], newton[:], ALU.mult).then_inc(step, 1)
                dve.wait_ge(step, b * 5 + 5)
                for u in range(UNITS_B):
                    nc.vector.tensor_tensor(unit[u][:].rearrange("p (n g) -> p n g", g=8),
                                            nat_ps[u][:].rearrange("p (n g) -> p n g", g=8),
                                            root[:, u, :].unsqueeze(2).to_broadcast([P, groups, 8]),
                                            ALU.mult).then_inc(unit_done, 1)

                def value(n):
                    half, i = n // items, n % items
                    if i < 2:
                        dve.wait_ge(unitT_ready, b * UNITS_B + (2 * half + i + 1))
                    if i == 1:
                        ins = nc.vector.tensor_copy(val[n][:], turn_ps[1][:])
                    else:
                        ins = nc.vector.tensor_scalar(val[n][:], turn_ps[0][:], factors[:, i // 2:i // 2 + 1], None, ALU.mult)
                    ins.then_inc(val_done, 1)

                def remainder(n):
                    dve.wait_ge(hi_done, b * NB + (n + 1))
                    nc.vector.tensor_tensor(rem[n][:], val[n][:], parts[n][:, 0, :], ALU.subtract).then_inc(rem_done, 1)

                value(0)
                for n in range(NB):
                    if n + 1 < NB:
                        value(n + 1)
                    remainder(n)


def cosine_attention(nc, name, ql, qd, ks, vs, neg_lambda, ctx_nat, ident):
    S = 2 * KB
    NS = GROUPS * S
    with ExitStack() as ctx:
        def sb(n, shp, dt=FP32):
            return ctx.enter_context(nc.sbuf_tensor(f"{name}_{n}", shp, dt))

        def ps(n, shp):
            return ctx.enter_context(nc.psum_tensor(f"{name}_{n}", shp, FP32))

        def sem(n):
            return nc.alloc_semaphore(f"{name}_{n}")

        ops = [[sb(f"{n}{i}", [2 * MAP_ROWS, 2, T], BF16) for n in ("k_op", "qd_op", "q1_op", "q2_op")]
               for i in range(GROUPS)]
        v_op = [sb(f"v_op{i}", [P, KB, 64]) for i in range(GROUPS)]
        gate = [sb(f"gate{i}", [P, 2, CH]) for i in range(2)]
        probs = [[sb(f"probs{m}_{i}", [P, 2, CH]) for m in range(2)] for i in range(4)]
        o_sb = [sb(f"o_sb{i}", [P, CH]) for i in range(2)]
        rec = sb("rec", [P, CPT, 4])
        o_norm = sb("o_norm", [P, CPT, 4, 16])
        diff_ps = ps("diff_ps", [P, 2, CH])
        logit_ps = [ps(f"logit_ps{m}", [P, 2, CH]) for m in range(2)]
        o_ps, turn_ps = ps("o_ps", [P, CH]), ps("turn_ps", [P, CH])
        preset = sem("preset")
        op_loaded = [sem(f"op_loaded{i}") for i in range(GROUPS)]
        diff_ready, gate_done, exp_done, pv_done = sem("diff_ready"), sem("gate_done"), sem("exp_done"), sem("pv_done")
        logit_ready = [sem(f"logit_ready{m}") for m in range(2)]
        sum_done = [sem(f"sum_done{m}") for m in range(2)]
        o_copied, turned, turn_free, rec_done = sem("o_copied"), sem("turned"), sem("turn_free"), sem("rec_done")
        block = ctx.enter_context(nc.Block())

        def where(s):
            return s // S, s % S // KB, s % KB

        n_loads = 2 * 3 * len(PAIR_PARTS) + 1

        @block.sync
        def _(sp):
            def load(b, g):
                k_op, qd_op, q1_op, q2_op = ops[g]
                for m in range(2):
                    for n, (qp, kp) in enumerate(PAIR_PARTS):
                        r0 = m * MAP_ROWS + n * 8
                        for op, dram, part in ((k_op, ks, kp), (qd_op, qd, qp), ((q1_op, q2_op)[m], ql, qp)):
                            src = dram[ds(b, 1), part, g * 32:(g + 1) * 32, :] \
                                .rearrange("a (j m r) t -> (a r) m j t", j=2, m=2)[:, m, :, :]
                            sp.dma_start(op[r0:r0 + 8, :, :], src).then_inc(op_loaded[g], 16)
                sp.dma_start(v_op[g][:], vs[ds(b, 1), :, :, g * 64:(g + 1) * 64]
                             .rearrange("a p k v -> (a p) k v")).then_inc(op_loaded[g], 16)

            for g in range(GROUPS):
                sp.wait_ge(preset, g + 1)
                load(0, g)
            with sp.Fori(0, BATCH - 1) as b:
                for g in range(GROUPS):
                    sp.wait_ge(pv_done, b * NS + (g + 1) * S)
                    load(b + 1, g)

        @block.tensor
        def _(te):
            te.sem_inc(gate_done, 1)
            te.sem_inc(sum_done[0], 1)
            te.sem_inc(sum_done[1], 1)
            te.sem_inc(o_copied, 1)
            te.sem_inc(turn_free, 1)
            with te.Fori(0, BATCH) as b:
                def product(out, q, s):
                    g, hq, kb = where(s)
                    for j in range(2):
                        mm = nc.tensor.matmul(out[:, j, :], ops[g][0][:, j, kb * P:(kb + 1) * P],
                                              q[:, j, hq * CH:(hq + 1) * CH], start=True, stop=True)
                    return mm

                for s in range(NS + 5):
                    if s < NS:
                        g, hq, kb = where(s)
                        if s % S == 0:
                            te.wait_ge(op_loaded[g], (b + 1) * (16 * n_loads))
                        te.wait_ge(gate_done, b * NS + (s + 1))
                        product(diff_ps, ops[g][1], s).then_inc(diff_ready, 1)
                        for m in range(2):
                            te.wait_ge(sum_done[m], b * NS + (s + 1))
                            product(logit_ps[m], ops[g][2 + m], s).then_inc(logit_ready[m], 1)
                    if 0 <= s - 2 < NS:
                        g, hq, kb = where(s - 2)
                        te.wait_ge(exp_done, (b * NS + (s - 1)) * 2)
                        if kb == 0:
                            te.wait_ge(o_copied, b * (2 * GROUPS) + (2 * g + hq + 1))
                        for j in range(2):
                            for m in range(2):
                                c0 = 32 * (2 * j + m)
                                mm = nc.tensor.matmul(o_ps[c0:c0 + 32, :], v_op[g][:, kb, j * 32:(j + 1) * 32],
                                                      probs[(s - 2) % 4][m][:, j, :], start=kb == 0, stop=kb == KB - 1)
                        mm.then_inc(pv_done, 1)
                    if 0 <= s - 4 < NS and (s - 4) % KB == KB - 1:
                        g, hq, kb = where(s - 4)
                        h = b * (2 * GROUPS) + (2 * g + hq)
                        te.wait_ge(o_copied, h + 2)
                        te.wait_ge(turn_free, h + 1)
                        for t in range(CPT):
                            mm = nc.tensor.transpose(turn_ps[:, t * P:(t + 1) * P], o_sb[hq][:, t * P:(t + 1) * P], ident[:])
                        mm.then_inc(turned, 1)

        @block.scalar
        def _(act):
            with act.Fori(0, BATCH) as b:
                for s in range(NS + 5):
                    if s < NS:
                        act.wait_ge(diff_ready, b * NS + (s + 1))
                        nc.scalar.activation(gate[s % 2][:], diff_ps[:], ACT.Tanh).then_inc(gate_done, 1)
                    if 0 <= s - 1 < NS:
                        for m in range(2):
                            tile = probs[(s - 1) % 4][m]
                            act.wait_ge(sum_done[m], b * NS + (s + 1))
                            nc.scalar.activation(tile[:], tile[:], ACT.Exp).then_inc(exp_done, 1)

        @block.vector
        def _(dve):
            for g in range(GROUPS):
                nc.vector.memset(ops[g][2][:], 0.0)
                nc.vector.memset(ops[g][3][:], 0.0).then_inc(preset, 1)
            with dve.Fori(0, BATCH) as b:
                for s in range(NS + 5):
                    if 0 <= s - 5 < NS and (s - 5) % KB == KB - 1:
                        g, hq, kb = where(s - 5)
                        h = b * (2 * GROUPS) + (2 * g + hq)
                        o = turn_ps[:].rearrange("p (t j v) -> p t j v", t=CPT, j=4)
                        dve.wait_ge(turned, h + 1)
                        nc.vector.reciprocal(rec[:], o[:, :, :, 16]).then_inc(rec_done, 1)
                        dve.wait_ge(rec_done, h * 2 + 1)
                        nc.vector.tensor_tensor(o_norm[:], o[:, :, :, 0:16], rec[:].unsqueeze(3)
                                                .to_broadcast([P, CPT, 4, 16]), ALU.mult).then_inc(rec_done, 1)
                        dve.wait_ge(rec_done, h * 2 + 2)
                        pair = o_norm[:].rearrange("p t (j m) d -> p t j m d", m=2)
                        out = (ctx_nat[:, ds(b * (KB * D) + hq * CH, CH)].rearrange("p (t f) -> p t f", f=D)
                               [:, :, g * 32:(g + 1) * 32].rearrange("p t (j d) -> p t j d", d=16))
                        nc.vector.scalar_tensor_tensor(out=out, in0=pair[:, :, :, 1, :], scalar=neg_lambda[:, 0:1],
                                                       in1=pair[:, :, :, 0, :], op0=ALU.mult, op1=ALU.add) \
                            .then_inc(turn_free, 1)
                    if 0 <= s - 3 < NS and (s - 3) % KB == KB - 1:
                        hq = where(s - 3)[1]
                        dve.wait_ge(pv_done, b * NS + (s - 2))
                        nc.vector.tensor_copy(o_sb[hq][:], o_ps[:]).then_inc(o_copied, 1)
                    if s < NS:
                        dve.wait_ge(gate_done, b * NS + (s + 2))
                        for m, op in enumerate((ALU.add, ALU.subtract)):
                            dve.wait_ge(logit_ready[m], b * NS + (s + 1))
                            nc.vector.tensor_tensor(probs[s % 4][m][:], logit_ps[m][:], gate[s % 2][:], op) \
                                .then_inc(sum_done[m], 1)


def route(nc, name, xn, w_router, n_experts, logits, ident):
    E = n_experts
    with ExitStack() as ctx:
        def sem(n):
            return nc.alloc_semaphore(f"{name}_{n}")

        w = ctx.enter_context(nc.sbuf_tensor(f"{name}_w", [P, E], FP32))
        xnT = [ctx.enter_context(nc.sbuf_tensor(f"{name}_xnT{i}", [P, CH], FP32)) for i in range(2)]
        t_ps = [ctx.enter_context(nc.psum_tensor(f"{name}_t_ps{i}", [P, CH], FP32)) for i in range(2)]
        l_ps = ctx.enter_context(nc.psum_tensor(f"{name}_l_ps", [P, TILES * E], FP32))
        loaded, turned, copied, l_ready = (sem(n) for n in ("loaded", "turned", "copied", "l_ready"))
        block = ctx.enter_context(nc.Block())

        @block.sync
        def _(sp):
            sp.dma_start(w[:], w_router).then_inc(loaded, 16)

        @block.tensor
        def _(te):
            def turn(c):
                if c >= 2:
                    te.wait_ge(copied, c - 1)
                for t in range(CPT):
                    col = (c * CPT + t) * D
                    mm = nc.tensor.transpose(t_ps[c % 2][:, t * P:(t + 1) * P], xn[:, col:col + D], ident[:])
                mm.then_inc(turned, 1)

            turn(0)
            te.wait_ge(loaded, 16)
            for c in range(CHUNKS):
                if c + 1 < CHUNKS:
                    turn(c + 1)
                te.wait_ge(copied, c + 1)
                for t in range(CPT):
                    col = (c * CPT + t) * E
                    mm = nc.tensor.matmul(l_ps[:, col:col + E], xnT[c % 2][:, t * P:(t + 1) * P], w[:], start=True, stop=True)
                mm.then_inc(l_ready, 1)

        @block.scalar
        def _(act):
            for c in range(CHUNKS):
                act.wait_ge(turned, c + 1)
                if c >= 2:
                    act.wait_ge(l_ready, c - 1)
                nc.scalar.activation(xnT[c % 2][:], t_ps[c % 2][:], ACT.Copy).then_inc(copied, 1)

        @block.vector
        def _(dve):
            dve.wait_ge(l_ready, CHUNKS)
            nc.vector.tensor_copy(logits[:], l_ps[:])


def wide(ap, n):
    return ap.unsqueeze(2).to_broadcast([P, TILES, n])


def first_of_max(nc, then, out, v, best, descending, E):
    then(nc.vector.tensor_reduce(best[:], v, axis=AX.X, op=ALU.max))
    then(nc.vector.tensor_tensor(out[:], v, wide(best[:], E), ALU.is_equal))
    then(nc.vector.tensor_tensor(out[:], out[:], descending[:].unsqueeze(1).to_broadcast([P, TILES, E]), ALU.mult))
    then(nc.vector.tensor_reduce(best[:], out[:], axis=AX.X, op=ALU.max))
    then(nc.vector.tensor_tensor(out[:], out[:], wide(best[:], E), ALU.is_equal))


def top2_coefficients(nc, name, logits, descending, parts):
    E = 16
    with ExitStack() as ctx:
        def sb(n, shp, dt=FP32):
            return ctx.enter_context(nc.sbuf_tensor(f"{name}_{n}", shp, dt))

        prob, first, second = sb("prob", [P, TILES, E]), sb("first", [P, TILES, E]), sb("second", [P, TILES, E])
        best = sb("best", [P, TILES])
        step = nc.alloc_semaphore(f"{name}_step")
        exp_done = nc.alloc_semaphore(f"{name}_exp_done")
        block = ctx.enter_context(nc.Block())

        @block.scalar
        def _(act):
            act.wait_ge(step, 3)
            nc.scalar.activation(prob[:], prob[:], ACT.Exp).then_inc(exp_done, 1)

        @block.vector
        def _(dve):
            count = [0]

            def then(ins):
                count[0] += 1
                ins.then_inc(step, 1)
                dve.wait_ge(step, count[0])

            l = logits[:].rearrange("p (t e) -> p t e", e=E)
            then(nc.vector.memset(parts[:], 0.0))
            then(nc.vector.tensor_reduce(best[:], l, axis=AX.X, op=ALU.max))
            then(nc.vector.tensor_tensor(prob[:], l, wide(best[:], E), ALU.subtract))
            dve.wait_ge(exp_done, 1)
            then(nc.vector.tensor_reduce(best[:], prob[:], axis=AX.X, op=ALU.add))
            then(nc.vector.reciprocal(best[:], best[:]))
            then(nc.vector.tensor_tensor(prob[:], prob[:], wide(best[:], E), ALU.mult))
            first_of_max(nc, then, first, prob[:], best, descending, E)
            then(nc.vector.scalar_tensor_tensor(out=first[:], in0=first[:], scalar=-4.0, in1=prob[:],
                                                op0=ALU.mult, op1=ALU.add))
            first_of_max(nc, then, second, first[:], best, descending, E)
            then(nc.vector.tensor_scalar(first[:], first[:], 0.0, None, ALU.is_lt))
            then(nc.vector.tensor_tensor(second[:], second[:], first[:], ALU.add))
            then(nc.vector.tensor_tensor(prob[:], prob[:], second[:], ALU.mult))
            for i in range(3):
                then(nc.vector.tensor_copy(parts[:, :, 32 * i:32 * i + E], prob[:]))
                if i < 2:
                    then(nc.vector.tensor_tensor(prob[:], prob[:], parts[:, :, 32 * i:32 * i + E], ALU.subtract))


def soft_experts(nc, name, x, mv, rstd, gate_w, up_w, down_w, s_gate, s_up, s_down, coef, select, ident):
    PAIRS_ = 8
    ITEMS = PAIRS_ + 1
    TURN, BACK = 3, 1
    with ExitStack() as ctx:
        def sb(n, shp, dt=FP32):
            return ctx.enter_context(nc.sbuf_tensor(f"{name}_{n}", shp, dt))

        def ps(n, dt=FP32):
            return ctx.enter_context(nc.psum_tensor(f"{name}_{n}", [P, CH], dt))

        def sem(n):
            return nc.alloc_semaphore(f"{name}_{n}")

        g_w, u_w, d_w = sb("g_w", [P, ITEMS, P]), sb("u_w", [P, ITEMS, P]), sb("d_w", [P, ITEMS, D])
        sel = sb("sel", [96, PAIRS_, P], BF16)
        ident_bf = sb("ident_bf", [P, P], BF16)
        xn = [sb(f"xn{i}", [P, CH]) for i in range(2)]
        xnT = [sb(f"xnT{i}", [P, CH]) for i in range(2)]
        coefT = [sb(f"coefT{i}", [96, CH], BF16) for i in range(2)]
        silu = [sb(f"silu{i}", [P, CH]) for i in range(2)]
        product = sb("product", [P, CH])
        inter = [sb(f"inter{i}", [P, CH]) for i in range(2)]
        yT = sb("yT", [P, CH])
        t_ps, c_ps, y_ps, ct_ps = ps("t_ps"), ps("c_ps"), ps("y_ps"), ps("ct_ps", BF16)
        g_ps = [ps(f"g_ps{i}") for i in range(2)]
        u_ps = [ps(f"u_ps{i}") for i in range(2)]
        (loaded, xn_done, turned, xT_done, ct_ready, ct_done, g_ready, uc_ready, silu_done, product_done, inter_done,
         down_done, y_ready, y_copied, back, added) = (sem(n) for n in (
             "loaded", "xn_done", "turned", "xT_done", "ct_ready", "ct_done", "g_ready", "uc_ready", "silu_done",
             "product_done", "inter_done", "down_done", "y_ready", "y_copied", "back", "added"))
        block = ctx.enter_context(nc.Block())

        @block.sync
        def _(sp):
            for w, dram, shared in ((g_w, gate_w, s_gate), (u_w, up_w, s_up)):
                sp.dma_start(w[:, 0:PAIRS_, :].rearrange("c n (e f) -> c (n e) f", f=64),
                             dram.rearrange("e c f -> c e f")).then_inc(loaded, 16)
                sp.dma_start(w[:, PAIRS_, :], shared).then_inc(loaded, 16)
            sp.dma_start(d_w[:, 0:PAIRS_, :], down_w.rearrange("(n e) f d -> (e f) n d", e=2)).then_inc(loaded, 16)
            sp.dma_start(d_w[:, PAIRS_, :], s_down).then_inc(loaded, 16)
            sp.dma_start(sel[:], select[0]).then_inc(loaded, 16)
            sp.dma_start(ident_bf[:], select[1]).then_inc(loaded, 16)

        @block.tensor
        def _(te):
            te.wait_ge(loaded, 16 * 8)
            te.sem_inc(silu_done, 2)
            te.sem_inc(inter_done, 2)
            te.sem_inc(added, 1)
            te.sem_inc(y_copied, 1)
            te.sem_inc(back, 1)
            with te.Fori(0, BATCH) as b:
                def turn(half):
                    c = b * 2 + half
                    if half == 0:
                        te.wait_ge(added, c + 1)
                    te.wait_ge(xn_done, c + 1)
                    for t in range(CPT):
                        mm = nc.tensor.transpose(t_ps[:, t * P:(t + 1) * P], xn[half][:, t * P:(t + 1) * P], ident[:])
                    mm.then_inc(turned, 1)
                    for t in range(CPT):
                        mm = nc.tensor.transpose(ct_ps[0:96, t * P:(t + 1) * P],
                                                 coef[:].rearrange("p t n -> p (t n)")[:, ds((b * KB + half * CPT + t) * 96, 96)],
                                                 ident_bf[:])
                    mm.then_inc(ct_ready, 1)

                def turn_back(half):
                    c = b * 2 + half
                    te.wait_ge(y_copied, c + 2)
                    if half == 1:
                        te.wait_ge(added, c + 1)
                    for t in range(CPT):
                        mm = nc.tensor.transpose(t_ps[:, t * P:(t + 1) * P], yT[:, t * P:(t + 1) * P], ident[:])
                    mm.then_inc(back, 1)

                turn(0)
                for half in range(2):
                    c = b * 2 + half
                    te.wait_ge(xT_done, c + 1)
                    te.wait_ge(ct_done, c + 1)

                    def down(i):
                        te.wait_ge(inter_done, c * ITEMS + (i + 3))
                        if i == 0:
                            te.wait_ge(y_copied, c + 1)
                        nc.tensor.matmul(y_ps[:], d_w[:, i, :], inter[(half + i) % 2][:],
                                         start=i == 0, stop=i == ITEMS - 1).then_inc(down_done, 1)

                    for i in range(ITEMS):
                        k = c * ITEMS + i
                        j = (half + i) % 2
                        te.wait_ge(silu_done, k + 1)
                        nc.tensor.matmul(g_ps[j][:], g_w[:, i, :], xnT[half][:], start=True, stop=True).then_inc(g_ready, 1)
                        te.wait_ge(inter_done, k + 1)
                        mm = nc.tensor.matmul(u_ps[j][:], u_w[:, i, :], xnT[half][:], start=True, stop=True)
                        if i < PAIRS_:
                            te.wait_ge(inter_done, k + 2)
                            mm = nc.tensor.matmul(c_ps[:], sel[:, i, :], coefT[half][:], start=True, stop=True)
                        mm.then_inc(uc_ready, 1)
                        if i > 0:
                            down(i - 1)
                        if half == 0 and i == TURN:
                            turn(1)
                        if half == 1 and i == BACK:
                            turn_back(0)
                    down(ITEMS - 1)
                turn_back(1)

        @block.scalar
        def _(act):
            with act.Fori(0, BATCH) as b:
                def take(half):
                    act.wait_ge(turned, b * 2 + (half + 1))
                    nc.scalar.activation(xnT[half][:], t_ps[:], ACT.Copy).then_inc(xT_done, 1)
                    act.wait_ge(ct_ready, b * 2 + (half + 1))
                    nc.scalar.activation(coefT[half][:], ct_ps[0:96, :], ACT.Copy).then_inc(ct_done, 1)

                take(0)
                for half in range(2):
                    c = b * 2 + half
                    for i in range(ITEMS):
                        k = c * ITEMS + i
                        act.wait_ge(g_ready, k + 1)
                        act.wait_ge(inter_done, k + 1)
                        nc.scalar.activation(silu[(half + i) % 2][:], g_ps[(half + i) % 2][:], ACT.Silu).then_inc(silu_done, 1)
                        if half == 0 and i == TURN:
                            take(1)
                    act.wait_ge(down_done, (c + 1) * ITEMS + 2)
                    act.wait_ge(back, c + 1)
                    nc.scalar.activation(yT[:], y_ps[:], ACT.Copy).then_inc(y_copied, 1)

        @block.vector
        def _(dve):
            dve.sem_inc(down_done, 2)
            with dve.Fori(0, BATCH) as b:
                for half in range(2):
                    apply_norm(nc, xn[half], x, mv, rstd, b * KB + half * CPT).then_inc(xn_done, 1)

                def add(half):
                    dve.wait_ge(back, b * 2 + (half + 2))
                    rows = x[:, ds(b * (KB * D) + half * CH, CH)]
                    nc.vector.tensor_tensor(rows, rows, t_ps[:], ALU.add).then_inc(added, 1)

                for half in range(2):
                    c = b * 2 + half
                    for i in range(ITEMS):
                        k = c * ITEMS + i
                        j = (half + i) % 2
                        dve.wait_ge(silu_done, k + 3)
                        dve.wait_ge(uc_ready, k + 1)
                        if i < PAIRS_:
                            dve.wait_ge(inter_done, k + 2)
                            nc.vector.tensor_tensor(product[:], silu[j][:], u_ps[j][:], ALU.mult).then_inc(product_done, 1)
                            dve.wait_ge(product_done, c * PAIRS_ + (i + 1))
                            dve.wait_ge(down_done, k + 1)
                            nc.vector.tensor_tensor(inter[j][:], product[:], c_ps[:], ALU.mult).then_inc(inter_done, 1)
                        else:
                            dve.wait_ge(down_done, k + 1)
                            nc.vector.tensor_tensor(inter[j][:], silu[j][:], u_ps[j][:], ALU.mult).then_inc(inter_done, 1)
                        if half == 1 and i == BACK:
                            add(0)
                add(1)


def channel_mix(nc, name, x, mv, rstd, w_r, w_k, w_v, mu, ident):
    with ExitStack() as ctx:
        def sb(n, shp):
            return ctx.enter_context(nc.sbuf_tensor(f"{name}_{n}", shp, FP32))

        def ps(n):
            return ctx.enter_context(nc.psum_tensor(f"{name}_{n}", [P, CH], FP32))

        def sem(n):
            return nc.alloc_semaphore(f"{name}_{n}")

        w = [sb(f"w{i}", [P, D]) for i in range(3)]
        mu_sb, rest = sb("mu_sb", [P, 2]), sb("rest", [P, 2])
        xn = [sb(f"xn{i}", [P, CH]) for i in range(2)]
        xnT = sb("xnT", [P, T + 1])
        before = [sb(f"before{i}", [P, CH]) for i in range(2)]
        mixed = [[sb(f"mixed{h}{i}", [P, CH]) for i in range(2)] for h in range(2)]
        relu = [sb(f"relu{i}", [P, CH]) for i in range(2)]
        kact = [sb(f"kact{i}", [P, CH]) for i in range(2)]
        r_sb = [sb(f"r_sb{i}", [P, CH]) for i in range(2)]
        gated = sb("gated", [P, CH])
        t_ps, r_ps, k_ps, o_ps = ([ps(f"{n}{i}") for i in range(2)] for n in ("t_ps", "r_ps", "k_ps", "o_ps"))
        (loaded, ready, xn_done, turned, xT_done, before_done, mixed_done, r_ready, k_ready, relu_done, kact_done, r_done,
         o_ready, gated_done, added) = (sem(n) for n in (
             "loaded", "ready", "xn_done", "turned", "xT_done", "before_done", "mixed_done", "r_ready", "k_ready",
             "relu_done", "kact_done", "r_done", "o_ready", "gated_done", "added"))
        block = ctx.enter_context(nc.Block())

        @block.sync
        def _(sp):
            for sb_, dram in zip(w, (w_r, w_k, w_v)):
                sp.dma_start(sb_[:], dram).then_inc(loaded, 16)
            sp.dma_start(mu_sb[:], mu).then_inc(loaded, 16)

        @block.tensor
        def _(te):
            te.wait_ge(loaded, 64)
            with te.Fori(0, BATCH) as b:
                te.wait_ge(added, b * 2 + 1)
                for h in range(2):
                    te.wait_ge(xn_done, b * 2 + (h + 1))
                    for t in range(CPT):
                        mm = nc.tensor.transpose(t_ps[h][:, t * P:(t + 1) * P], xn[h][:, t * P:(t + 1) * P], ident[:])
                    mm.then_inc(turned, 1)
                for h in range(2):
                    c = b * 2 + h
                    te.wait_ge(mixed_done, c * 2 + 2)
                    nc.tensor.matmul(k_ps[h][:], w[1][:], mixed[h][1][:], start=True, stop=True).then_inc(k_ready, 1)
                    for t in range(CPT):
                        mm = nc.tensor.matmul(r_ps[h][:, t * D:(t + 1) * D], mixed[h][0][:, t * P:(t + 1) * P], w[0][:],
                                              start=True, stop=True)
                    mm.then_inc(r_ready, 1)
                for h in range(2):
                    te.wait_ge(kact_done, b * 2 + (h + 1))
                    for t in range(CPT):
                        mm = nc.tensor.matmul(o_ps[h][:, t * D:(t + 1) * D], kact[h][:, t * P:(t + 1) * P], w[2][:],
                                              start=True, stop=True)
                    mm.then_inc(o_ready, 1)

        @block.scalar
        def _(act):
            act.wait_ge(ready, 2)
            with act.Fori(0, BATCH) as b:
                for h in range(2):
                    act.wait_ge(turned, b * 2 + (h + 1))
                    nc.scalar.activation(xnT[:, 1 + h * CH:1 + (h + 1) * CH], t_ps[h][:], ACT.Copy).then_inc(xT_done, 1)
                for h in range(2):
                    act.wait_ge(k_ready, b * 2 + (h + 1))
                    nc.scalar.activation(relu[h][:], k_ps[h][:], ACT.Relu).then_inc(relu_done, 1)
                    act.wait_ge(r_ready, b * 2 + (h + 1))
                    nc.scalar.activation(r_sb[h][:], r_ps[h][:], ACT.Sigmoid).then_inc(r_done, 1)

        @block.gpsimd
        def _(pool):
            with pool.Fori(0, BATCH) as b:
                for h in range(2):
                    pool.wait_ge(relu_done, b * 2 + (h + 1))
                    nc.gpsimd.tensor_tensor(kact[h][:], relu[h][:], relu[h][:], ALU.mult).then_inc(kact_done, 1)

        @block.vector
        def _(dve):
            dve.sem_inc(added, 1)
            nc.vector.memset(xnT[:, 0:1], 0.0).then_inc(ready, 1)
            dve.wait_ge(loaded, 64)
            nc.vector.tensor_scalar(rest[:], mu_sb[:], -1.0, 1.0, ALU.mult, ALU.add).then_inc(ready, 1)
            dve.wait_ge(ready, 2)
            with dve.Fori(0, BATCH) as b:
                for h in range(2):
                    apply_norm(nc, xn[h], x, mv, rstd, b * KB + h * CPT).then_inc(xn_done, 1)
                for h in range(2):
                    c = b * 2 + h
                    dve.wait_ge(xT_done, c + 1)
                    for i in range(2):
                        nc.vector.tensor_scalar(before[i][:], xnT[:, h * CH:(h + 1) * CH], rest[:, i:i + 1], None,
                                                ALU.mult).then_inc(before_done, 1)
                    for i in range(2):
                        dve.wait_ge(before_done, c * 2 + (i + 1))
                        nc.vector.scalar_tensor_tensor(out=mixed[h][i][:], in0=xnT[:, 1 + h * CH:1 + (h + 1) * CH],
                                                       scalar=mu_sb[:, i:i + 1], in1=before[i][:],
                                                       op0=ALU.mult, op1=ALU.add).then_inc(mixed_done, 1)
                    dve.wait_ge(mixed_done, c * 2 + 2)
                for h in range(2):
                    c = b * 2 + h
                    dve.wait_ge(r_done, c + 1)
                    dve.wait_ge(o_ready, c + 1)
                    nc.vector.tensor_tensor(gated[:], r_sb[h][:], o_ps[h][:], ALU.mult).then_inc(gated_done, 1)
                    dve.wait_ge(gated_done, c + 1)
                    rows = x[:, ds(b * (KB * D) + h * CH, CH)]
                    nc.vector.tensor_tensor(rows, rows, gated[:], ALU.add).then_inc(added, 1)
                    dve.wait_ge(added, c + 2)


EXPERTS = 8
CAP = TOK // EXPERTS
HID = 512


def assign_slots(nc, name, logits, descending, before_me, gate, slot_in, slot_out):
    E = EXPERTS
    with ExitStack() as ctx:
        def sb(n, shp, dt=FP32):
            return ctx.enter_context(nc.sbuf_tensor(f"{name}_{n}", shp, dt))

        shifted, hot, rank = sb("shifted", [P, TILES, E]), sb("hot", [P, TILES, E]), sb("rank", [P, TILES, E])
        hot_bf = sb("hot_bf", [P, TILES, E], BF16)
        sums = [sb(f"sums{i}", [P, TILES, E]) for i in range(2)]
        best, expert, pos, keep, slot = (sb(n, [P, TILES]) for n in ("best", "expert", "pos", "keep", "slot"))
        in_ps = ctx.enter_context(nc.psum_tensor(f"{name}_in_ps", [P, TILES, E], FP32))
        all_ps = ctx.enter_context(nc.psum_tensor(f"{name}_all_ps", [P, TILES, E], FP32))
        step, exp_done, counted = (nc.alloc_semaphore(f"{name}_{n}") for n in ("step", "exp_done", "counted"))
        block = ctx.enter_context(nc.Block())

        @block.scalar
        def _(act):
            act.wait_ge(step, 2)
            nc.scalar.activation(shifted[:], shifted[:], ACT.Exp).then_inc(exp_done, 1)

        @block.tensor
        def _(te):
            te.wait_ge(exp_done, 2)
            flat = hot_bf[:].rearrange("p t e -> p (t e)")
            nc.tensor.matmul(in_ps[:].rearrange("p t e -> p (t e)"), before_me[:, 0, :], flat, start=True, stop=True)
            nc.tensor.matmul(all_ps[:].rearrange("p t e -> p (t e)"), before_me[:, 1, :], flat, start=True, stop=True) \
                .then_inc(counted, 1)

        @block.vector
        def _(dve):
            count = [0]

            def then(ins):
                count[0] += 1
                ins.then_inc(step, 1)
                dve.wait_ge(step, count[0])

            l = logits[:].rearrange("p (t e) -> p t e", e=E)
            then(nc.vector.tensor_reduce(best[:], l, axis=AX.X, op=ALU.max))
            then(nc.vector.tensor_tensor(shifted[:], l, wide(best[:], E), ALU.subtract))
            dve.wait_ge(exp_done, 1)
            then(nc.vector.tensor_reduce(best[:], shifted[:], axis=AX.X, op=ALU.add))
            then(nc.vector.reciprocal(gate[:], best[:]))
            first_of_max(nc, then, hot, l, best, descending, E)
            then(nc.vector.tensor_copy(hot_bf[:], hot[:]))
            dve.sem_inc(exp_done, 1)
            then(nc.vector.tensor_scalar(expert[:], best[:], -1.0, float(E), ALU.mult, ALU.add))
            dve.wait_ge(counted, 1)
            then(nc.vector.tensor_copy(sums[0][:], all_ps[:]))
            a, d = 0, 1
            while d < TILES:
                then(nc.vector.tensor_copy(sums[1 - a][:, 0:d, :], sums[a][:, 0:d, :]))
                then(nc.vector.tensor_tensor(sums[1 - a][:, d:, :], sums[a][:, d:, :], sums[a][:, 0:TILES - d, :], ALU.add))
                a, d = 1 - a, d * 2
            then(nc.vector.tensor_tensor(rank[:], sums[a][:], all_ps[:], ALU.subtract))
            then(nc.vector.tensor_tensor(rank[:], rank[:], in_ps[:], ALU.add))
            then(nc.vector.tensor_tensor(rank[:], rank[:], hot[:], ALU.mult))
            then(nc.vector.tensor_reduce(pos[:], rank[:], axis=AX.X, op=ALU.add))
            then(nc.vector.tensor_scalar(keep[:], pos[:], float(CAP), None, ALU.is_lt))
            then(nc.vector.scalar_tensor_tensor(out=slot[:], in0=expert[:], scalar=float(CAP), in1=pos[:],
                                                op0=ALU.mult, op1=ALU.add))
            then(nc.vector.tensor_tensor(gate[:], gate[:], keep[:], ALU.mult))
            then(nc.vector.tensor_tensor(slot[:], slot[:], keep[:], ALU.mult))
            then(nc.vector.tensor_copy(slot_out[:], slot[:]))
            then(nc.vector.tensor_scalar(keep[:], keep[:], -2.0 * TOK, 2.0 * TOK, ALU.mult, ALU.add))
            then(nc.vector.tensor_tensor(slot[:], slot[:], keep[:], ALU.add))
            then(nc.vector.tensor_copy(slot_in[:], slot[:]))


def dispatch(nc, name, xn, slot_in, slots):
    with ExitStack() as ctx:
        sent = nc.alloc_semaphore(f"{name}_sent")
        block = ctx.enter_context(nc.Block())

        @block.gpsimd
        def _(pool):
            for t in range(TILES):
                nc.gpsimd.indirect_dma_start(out=slots, out_offset=bass.IndirectOffsetOnAxis(ap=slot_in[:, t:t + 1], axis=0),
                                             in_=xn[:, t * D:(t + 1) * D], in_offset=None,
                                             bounds_check=TOK - 1, oob_is_err=False).then_inc(sent, 16)
            pool.wait_ge(sent, 16 * TILES)


def slot_experts(nc, name, slots, w1, w2, biases, results, ident):
    FB = HID // P
    with ExitStack() as ctx:
        def sb(n, shp):
            return ctx.enter_context(nc.sbuf_tensor(f"{name}_{n}", shp, FP32))

        def ps(n):
            return ctx.enter_context(nc.psum_tensor(f"{name}_{n}", [P, CH], FP32))

        def sem(n):
            return nc.alloc_semaphore(f"{name}_{n}")

        w1_sb = [sb(f"w1_sb{i}", [P, HID]) for i in range(2)]
        w2_sb = [sb(f"w2_sb{i}", [P, FB, D]) for i in range(2)]
        b_sb = [sb(f"b_sb{i}", [P, FB + 1]) for i in range(2)]
        rows = [sb(f"rows{i}", [P, CPT, D]) for i in range(2)]
        rowsT = [sb(f"rowsT{i}", [P, CH]) for i in range(2)]
        hid = [sb(f"hid{i}", [P, FB, CH]) for i in range(2)]
        yT = [sb(f"yT{i}", [P, CH]) for i in range(2)]
        out = [sb(f"out{i}", [P, CPT, D]) for i in range(2)]
        t_ps, y_ps, back_ps = ps("t_ps"), ps("y_ps"), ps("back_ps")
        h_ps = [ps(f"h_ps{i}") for i in range(FB)]
        loaded = [sem(f"loaded{i}") for i in range(2)]
        stored, drained = sem("stored"), sem("drained")
        turned, turn_copied, h_ready, h_done, y_ready, y_done, back, out_done = (
            sem(n) for n in ("turned", "turn_copied", "h_ready", "h_done", "y_ready", "y_done", "back", "out_done"))
        n_loads = 3 + (biases is not None)
        block = ctx.enter_context(nc.Block())

        @block.sync
        def _(sp):
            with sp.Fori(0, EXPERTS // 2) as pair:
                for i in range(2):
                    e = pair * 2 + i
                    sp.wait_ge(y_done, e + 1)
                    sp.dma_start(rows[i][:], slots[ds(e * CAP, CAP), :].rearrange("(n p) d -> p n d", p=P)).then_inc(loaded[i], 16)
                    sp.dma_start(w1_sb[i][:], w1[ds(e, 1), :, :].rearrange("a c f -> (a c) f")).then_inc(loaded[i], 16)
                    sp.dma_start(w2_sb[i][:], w2[ds(e, 1), :, :].rearrange("a (n p) d -> (a p) n d", p=P)).then_inc(loaded[i], 16)
                    if biases is not None:
                        sp.dma_start(b_sb[i][:], biases[ds(e, 1), :, :].rearrange("a p n -> (a p) n")).then_inc(loaded[i], 16)

        @block.gpsimd
        def _(pool):
            with pool.Fori(0, EXPERTS // 2) as pair:
                for i in range(2):
                    e = pair * 2 + i
                    pool.wait_ge(out_done, e + 2)
                    pool.dma_start(results[ds(e * CAP, CAP), :].rearrange("(n p) d -> p n d", p=P), out[i][:]).then_inc(stored, 16)
                    pool.wait_ge(stored, e * 16 + 16)
                    pool.sem_inc(drained, 1)

        @block.tensor
        def _(te):
            te.sem_inc(turn_copied, 1)
            te.sem_inc(h_done, FB)
            te.sem_inc(y_done, 2)
            te.sem_inc(out_done, 1)
            with te.Fori(0, EXPERTS // 2) as pair:
                for i in range(2):
                    e = pair * 2 + i
                    te.wait_ge(loaded[i], (pair + 1) * (16 * n_loads))
                    te.wait_ge(turn_copied, e + 1)
                    for t in range(CPT):
                        mm = nc.tensor.transpose(t_ps[:, t * P:(t + 1) * P], rows[i][:, t, :], ident[:])
                    mm.then_inc(turned, 1)
                    te.wait_ge(turn_copied, e + 2)
                    for f in range(FB):
                        te.wait_ge(h_done, e * FB + (f + 1))
                        nc.tensor.matmul(h_ps[f][:], w1_sb[i][:, f * P:(f + 1) * P], rowsT[i][:],
                                         start=True, stop=True).then_inc(h_ready, 1)
                    te.wait_ge(y_done, e + 2)
                    for f in range(FB):
                        te.wait_ge(h_done, e * FB + (f + 1 + FB))
                        mm = nc.tensor.matmul(y_ps[:], w2_sb[i][:, f, :], hid[i][:, f, :], start=f == 0, stop=f == FB - 1)
                    mm.then_inc(y_ready, 1)
                    te.wait_ge(y_done, e + 3)
                    te.wait_ge(out_done, e + 1)
                    for t in range(CPT):
                        mm = nc.tensor.transpose(back_ps[:, t * P:(t + 1) * P], yT[i][:, t * P:(t + 1) * P], ident[:])
                    mm.then_inc(back, 1)

        @block.scalar
        def _(act):
            with act.Fori(0, EXPERTS // 2) as pair:
                for i in range(2):
                    e = pair * 2 + i
                    act.wait_ge(turned, e + 1)
                    nc.scalar.activation(rowsT[i][:], t_ps[:], ACT.Copy).then_inc(turn_copied, 1)
                    for f in range(FB):
                        act.wait_ge(h_ready, e * FB + (f + 1))
                        if biases is None:
                            nc.scalar.activation(hid[i][:, f, :], h_ps[f][:], ACT.Relu).then_inc(h_done, 1)
                        else:
                            nc.scalar.activation(hid[i][:, f, :], h_ps[f][:], ACT.Relu, bias=b_sb[i][:, f:f + 1]).then_inc(h_done, 1)

        @block.vector
        def _(dve):
            dve.sem_inc(drained, 2)
            with dve.Fori(0, EXPERTS // 2) as pair:
                for i in range(2):
                    e = pair * 2 + i
                    dve.wait_ge(y_ready, e + 1)
                    if biases is None:
                        nc.vector.tensor_copy(yT[i][:], y_ps[:]).then_inc(y_done, 1)
                    else:
                        nc.vector.tensor_scalar(yT[i][:], y_ps[:], b_sb[i][:, FB:FB + 1], None, ALU.add).then_inc(y_done, 1)
                    dve.wait_ge(drained, e + 1)
                    dve.wait_ge(back, e + 1)
                    nc.vector.tensor_copy(out[i][:].rearrange("p n d -> p (n d)"), back_ps[:]).then_inc(out_done, 1)


def combine(nc, name, x, results, slot_out, gate):
    with ExitStack() as ctx:
        y = ctx.enter_context(nc.sbuf_tensor(f"{name}_y", [P, TILES * D], FP32))
        fetched = [nc.alloc_semaphore(f"{name}_fetched{b}") for b in range(BATCH)]
        block = ctx.enter_context(nc.Block())

        @block.gpsimd
        def _(pool):
            for t in range(TILES):
                nc.gpsimd.indirect_dma_start(out=y[:, t * D:(t + 1) * D], out_offset=None, in_=results,
                                             in_offset=bass.IndirectOffsetOnAxis(ap=slot_out[:, t:t + 1], axis=0)) \
                    .then_inc(fetched[t // KB], 16)

        @block.vector
        def _(dve):
            for t in range(TILES):
                if t % KB == 0:
                    dve.wait_ge(fetched[t // KB], 16 * KB)
                rows = x[:, t * D:(t + 1) * D]
                nc.vector.scalar_tensor_tensor(out=rows, in0=y[:, t * D:(t + 1) * D], scalar=gate[:, t:t + 1], in1=rows,
                                               op0=ALU.mult, op1=ALU.add)


def four_layers(nc, a, out):
    with ExitStack() as ctx:
        def sb(n, shp, dt=FP32):
            return ctx.enter_context(nc.sbuf_tensor(n, shp, dt))

        def dram(n, shp, dt):
            return nc.dram_tensor(n, shp, dt, kind="Internal").ap()

        x = sb("x_sb", [P, TILES * D])
        mv, rstd = sb("mv", [P, TILES, 2]), sb("rstd", [P, TILES])
        consts = {n: sb(n + "_sb", [P, P], FP32 if n == "ident" else BF16)
                  for n in ("ident", "ident_bf", "mask_a", "mask_b", "one_stat")}
        descending = {n: sb(f"descending{n}", [P, n]) for n in (16, EXPERTS)}
        before_me = sb("before_me_sb", [P, 2, P], BF16)
        consts["zero_rows"], consts["one_rows"] = a["zero_rows"], a["one_rows"]
        ident = consts["ident"]
        scratch = [dram(f"scratch_{n}", [BATCH, 3, D, T], BF16) for n in ("q", "k", "g")]
        scratch_v = dram("scratch_v", [BATCH, P, KB, 512], FP32)
        scratch_v2 = dram("scratch_v2", [BATCH, P, KB, 256], FP32)
        wide_q, wide_k = (dram(f"wide_{n}", [BATCH, 3, 512, T], BF16) for n in ("q", "k"))
        wide_v = dram("wide_v", [BATCH, P, KB, 520], FP32)
        slots = [dram(f"slots{i}", [TOK, D], FP32) for i in range(2)]
        results = [dram(f"results{i}", [TOK, D], FP32) for i in range(2)]
        loaded, zeroed, filled, sent = (nc.alloc_semaphore(n) for n in ("x_loaded", "zeroed", "filled", "sent"))

        with nc.Block() as block:
            @block.sync
            def _(sp):
                sp.dma_start(x[:].rearrange("p (n d) -> p n d", d=D), a["x"].rearrange("(n p) d -> p n d", p=P)).then_inc(loaded, 16)
                for n in ("ident", "ident_bf", "mask_a", "mask_b", "one_stat"):
                    sp.dma_start(consts[n][:], a[n]).then_inc(loaded, 16)
                sp.dma_start(before_me[:], a["before_me"]).then_inc(loaded, 16)
                for n, t in descending.items():
                    sp.dma_start(t[:], a["descending"][:, 16 - n:16].to_broadcast([P, n])).then_inc(loaded, 16)
                sp.wait_ge(loaded, 16 * 9)

        def maxed(name, shape, feats, q, k, v, floor, wo, bias):
            with nc.sbuf_tensor(name + "_nat", [P, TILES * feats], FP32) as nat:
                attention(nc, name, shape, shape.hd ** -0.5, q, k, v, nat, consts, floor)
                out_project(nc, name + "o", nat, feats, wo, x, consts, bias)

        def moe(name, i, w_router, w1, w2, biases):
            with ExitStack() as inner:
                def sbi(n, shp, dt=FP32):
                    return inner.enter_context(nc.sbuf_tensor(f"{name}_{n}", shp, dt))

                xn, logits = sbi("xn", [P, TILES * D]), sbi("logits", [P, TILES * EXPERTS])
                gate, slot_in, slot_out = sbi("gate", [P, TILES]), sbi("slot_in", [P, TILES], U32), sbi("slot_out", [P, TILES], U32)
                layer_stats(nc, name + "n", x, mv, rstd, dst=xn)
                route(nc, name + "r", xn, w_router, EXPERTS, logits, ident)
                assign_slots(nc, name + "a", logits, descending[EXPERTS], before_me, gate, slot_in, slot_out)
                dispatch(nc, name + "d", xn, slot_in, slots[i])
                slot_experts(nc, name + "e", slots[i], w1, w2, biases, results[i], ident)
                combine(nc, name + "c", x, results[i], slot_out, gate)

        with cleared_semaphores(nc):
            with nc.sbuf_tensor("zero_slots", [P, TILES * D], FP32) as zeros:
                with nc.Block() as block:
                    @block.gpsimd
                    def _(pool):
                        nc.gpsimd.memset(zeros[:], 0.0).then_inc(zeroed, 1)

                    @block.sync
                    def _(sp):
                        sp.wait_ge(zeroed, 1)
                        for s in slots:
                            sp.dma_start(s.rearrange("(p n) d -> p (n d)", p=P), zeros[:]).then_inc(filled, 16)

                layer_stats(nc, "n0", x, mv, rstd)
                project(nc, "p0", x, mv, rstd, a["L0_Wq"], a["L0_Wk"], a["L0_Wv"], scratch[0], scratch[1], scratch_v, ident, 16, 32)
                with nc.Block() as block:
                    @block.sync
                    def _(sp):
                        sp.wait_ge(filled, 32)

            maxed("a0", Shape(4, 8, 32, True), D, scratch[0], scratch[1], scratch_v, None, a["L0_Wo"], None)
            with nc.sbuf_tensor("logits0", [P, TILES * 16], FP32) as logits, nc.sbuf_tensor("coef0", [P, TILES, 96], BF16) as coef:
                with nc.sbuf_tensor("xn0", [P, TILES * D], FP32) as xn0:
                    layer_stats(nc, "m0", x, mv, rstd, dst=xn0)
                    route(nc, "r0", xn0, a["L0_router"], 16, logits, ident)
                top2_coefficients(nc, "c0", logits, descending[16], coef)
                soft_experts(nc, "e0", x, mv, rstd, a["L0_gate"], a["L0_up"], a["L0_down"], a["L0_sgate"], a["L0_sup"], a["L0_sdown"],
                             coef, (a["select"], a["ident_bf"]), ident)

        with cleared_semaphores(nc):
            with nc.sbuf_tensor("xn1", [P, TILES * D], FP32) as xn1:
                layer_stats(nc, "n1", x, mv, rstd, dst=xn1)
                layer_stats(nc, "n1b", xn1, mv, rstd)
                project(nc, "p1", xn1, mv, rstd, a["L1_Wq"], a["L1_Wk"], a["L1_Wv"], scratch[0], scratch[1], scratch_v, ident, 16, 32,
                        gain=a["L1_gain"], qk_bias=a["L1_bqk"], v_bias=a["L1_bv"])
            maxed("a1", Shape(4, 8, 32, False), D, scratch[0], scratch[1], scratch_v, 1e-12, a["L1_Wo"], a["L1_bo"])
            layer_stats(nc, "m1", x, mv, rstd)
            channel_mix(nc, "f1", x, mv, rstd, a["L1_Wr"], a["L1_Wkk"], a["L1_Wvv"], a["L1_mu"], ident)

        with cleared_semaphores(nc):
            layer_stats(nc, "n2", x, mv, rstd)
            project(nc, "p2", x, mv, rstd, a["L2_Wq"], a["L2_Wk"], a["L2_Wv"], wide_q, wide_k, wide_v, ident, 8, 65, pos=a["pos"])
            maxed("a2", Shape(2, 64, 65, True), 512, wide_q, wide_k, wide_v, None, a["L2_Wo"], None)
            moe("f2", 0, a["L2_Wr"], a["L2_W1"], a["L2_W2"], None)

        with cleared_semaphores(nc):
            with nc.sbuf_tensor("factors", [P, 2], FP32) as factors, nc.sbuf_tensor("neg_lambda", [P, 1], FP32) as neg_lambda, \
                    nc.sbuf_tensor("nat3", [P, TILES * D], FP32) as nat:
                layer_stats(nc, "n3", x, mv, rstd)
                cosine_scales(nc, "s3", a["L3_raw"], a["L3_delta_col"], a["L3_delta_row"], a["L3_gain"], a["L3_sign"], a["L3_lambdas"],
                              factors, neg_lambda)
                project_cosine(nc, "p3", x, mv, rstd, a["L3_Wq"], a["L3_Wk"], a["L3_Wv"], factors, scratch[0], scratch[2], scratch[1],
                               scratch_v2, ident)
                cosine_attention(nc, "a3", scratch[0], scratch[2], scratch[1], scratch_v2, neg_lambda, nat, ident)
                out_project(nc, "o3", nat, D, a["L3_Wo"], x, consts, bias=a["L3_bo"], rms=(16, 1e-5, 0.5, a["L3_subln"]))
            moe("f3", 1, a["L3_wg"], a["L3_w1"], a["L3_w2"], a["L3_b"])

        with nc.Block() as block:
            @block.sync
            def _(sp):
                sp.dma_start(out.rearrange("(n p) d -> p n d", p=P), x[:].rearrange("p (n d) -> p n d", d=D)).then_inc(sent, 16)
                sp.wait_ge(sent, 16)


def shape_constants():
    bf16 = mybir.dt.np(BF16)
    i = np.arange(P)
    one_stat = np.zeros((P, P))
    one_stat[:3] = 1
    select = np.zeros((96, 8, P))
    for part in range(3):
        for e in range(16):
            select[32 * part + e, e // 2, 64 * (e % 2):64 * (e % 2) + 64] = 1
    before_me = np.stack([i[:, None] < i[None, :], np.ones((P, P), bool)], 1)
    pos = np.arange(T, dtype=np.float32)[:, None]
    div = np.exp(np.arange(0, 64, 2, dtype=np.float32) * np.float32(-np.log(10000.0) / 64))
    ang = pos * div
    pe = np.stack([np.sin(ang), np.cos(ang)], -1).reshape(T, 64).astype(np.float32)
    return {
        "ident": np.eye(P, dtype=np.float32),
        "ident_bf": np.eye(P).astype(bf16),
        "mask_a": np.where(i[None] > i[:, None], NEG, 0).astype(bf16),
        "mask_b": np.where(i[:, None] > i[None], NEG, 0).astype(bf16),
        "one_stat": one_stat.astype(bf16),
        "zero_rows": np.zeros((3, 4 * T), bf16),
        "one_rows": np.ones((3, 4 * T), bf16),
        "select": select.astype(bf16),
        "before_me": before_me.astype(bf16),
        "descending": np.arange(16, 0, -1, dtype=np.float32).reshape(1, 16),
        "pos": np.ascontiguousarray(np.concatenate([pe.T, pe.T])),
        "L3_sign": np.tile(np.repeat(np.array([1, -1], np.float32), 8), 8).reshape(P, 1),
    }


def lay_out(i):
    def t(n):
        return np.ascontiguousarray(i[n].T)

    c = np.ascontiguousarray
    qkv1, b1 = i["L1_attn_W_qkv"], i["L1_attn_b_qkv"]
    qkv2 = c(i["L2_attn_Wqkv"].reshape(8, 3, 64, D).transpose(1, 3, 0, 2)).reshape(3, D, 512)
    return {
        "x": c(i["L0_attn_x"].reshape(TOK, D)),
        "L0_Wq": t("L0_attn_Wq"), "L0_Wk": t("L0_attn_Wk"), "L0_Wv": t("L0_attn_Wv"), "L0_Wo": t("L0_attn_Wo"),
        "L0_router": i["L0_ffn_router_w"], "L0_gate": i["L0_ffn_gate_w"], "L0_up": i["L0_ffn_up_w"],
        "L0_down": i["L0_ffn_down_w"], "L0_sgate": i["L0_ffn_shared_gate_w"], "L0_sup": i["L0_ffn_shared_up_w"],
        "L0_sdown": i["L0_ffn_shared_down_w"],
        "L1_Wq": c(qkv1[:, 0:D]), "L1_Wk": c(qkv1[:, D:2 * D]), "L1_Wv": c(qkv1[:, 2 * D:]),
        "L1_bqk": c(b1[0:2 * D].reshape(2, D).T), "L1_bv": c(b1[2 * D:].reshape(1, D)),
        "L1_gain": c(np.stack([i["L1_attn_ln_gamma"], i["L1_attn_ln_beta"]], 1)),
        "L1_Wo": i["L1_attn_W_proj"], "L1_bo": c(i["L1_attn_b_proj"].reshape(1, D)),
        "L1_Wr": t("L1_ffn_W_r"), "L1_Wkk": t("L1_ffn_W_k"), "L1_Wvv": t("L1_ffn_W_v"),
        "L1_mu": c(np.stack([i["L1_ffn_mu_r"], i["L1_ffn_mu_k"]], 1)),
        "L2_Wq": qkv2[0], "L2_Wk": qkv2[1], "L2_Wv": qkv2[2], "L2_Wo": t("L2_attn_Wo"),
        "L2_Wr": i["L2_ffn_Wr"], "L2_W1": i["L2_ffn_W1"], "L2_W2": i["L2_ffn_W2"],
        "L3_Wq": t("L3_attn_Wq"), "L3_Wk": t("L3_attn_Wk"), "L3_Wv": t("L3_attn_Wv"), "L3_Wo": t("L3_attn_Wo"),
        "L3_bo": c(i["L3_attn_bo"].reshape(1, D)),
        "L3_raw": c(i["L3_attn_cos_logit_scale_raw"].reshape(1, 1)),
        "L3_delta_col": np.repeat(i["L3_attn_cos_head_delta"], 16).reshape(P, 1),
        "L3_delta_row": c(i["L3_attn_cos_head_delta"].reshape(1, 8)),
        "L3_gain": np.repeat(i["L3_attn_delta_gain"], 16).reshape(P, 1),
        "L3_lambdas": np.concatenate([i[f"L3_attn_lambda_{n}"] for n in ("q1", "q2", "k1", "k2")]).reshape(1, 32),
        "L3_subln": np.tile(i["L3_attn_subln_weight"], 8).reshape(P, 1),
        "L3_wg": i["L3_ffn_wg"], "L3_w1": i["L3_ffn_w1"], "L3_w2": i["L3_ffn_w2"],
        "L3_b": c(np.concatenate([i["L3_ffn_b1"].reshape(EXPERTS, 4, P).transpose(0, 2, 1),
                                  i["L3_ffn_b2"].reshape(EXPERTS, P, 1)], 2)),
    }


def kernel(**inputs):
    import concourse.bacc as bacc
    from concourse.bass_utils import run_bass_kernel_spmd

    arrays = {**shape_constants(), **lay_out({n: np.asarray(v) for n, v in inputs.items()})}
    arrays = {f"in_{n}": np.ascontiguousarray(v) for n, v in arrays.items()}
    nc = bacc.Bacc("TRN2", target_bir_lowering=False, num_devices=1)
    a = {n[3:]: nc.dram_tensor(n, v.shape, mybir.dt.from_np(v.dtype), kind="ExternalInput").ap() for n, v in arrays.items()}
    out = nc.dram_tensor("out", (TOK, D), FP32, kind="ExternalOutput").ap()
    four_layers(nc, a, out)
    r = run_bass_kernel_spmd(nc, [arrays], core_ids=[0])
    return r.results[0]["out"].reshape(BATCH, T, D)
```

```python
from contextlib import ExitStack, contextmanager

import numpy as np
import concourse.bass as bass
from concourse import mybir

FP32 = mybir.dt.float32
BF16 = mybir.dt.bfloat16
U32 = mybir.dt.uint32
ALU = mybir.AluOpType
ACT = mybir.ActivationFunctionType
AX = mybir.AxisListType
ds = bass.ds

P = 128
BATCH, T, D = 4, 1024, 128
TOK = BATCH * T
TILES = TOK // P
CH = 512
CPT = CH // P
CHUNKS = TOK // CH
KB = T // P
GROUPS = 4
UNITS = BATCH * GROUPS
EPS = 1e-5
NEG = -1e30


@contextmanager
def cleared_semaphores(nc):
    before = nc.snapshot_sems()
    yield
    nc.clear_and_free_semaphores(nc.allocated_since(before))
    nc.all_engine_barrier()


def tile_stats(nc, stats, src, t):
    return nc.vector.bn_stats(stats[:, t * 6:(t + 1) * 6], src[:, t * D:(t + 1) * D])


def layer_stats(nc, name, src, mv, rstd, dst=None, stats=None):
    with ExitStack() as ctx:
        measured = stats is not None
        if not measured:
            stats = ctx.enter_context(nc.sbuf_tensor(name + "_stats", [P, TILES * 6], FP32))
        eps = ctx.enter_context(nc.sbuf_tensor(name + "_eps", [P, 1], FP32))
        std = ctx.enter_context(nc.sbuf_tensor(name + "_std", [P, TILES], FP32))
        stats_done = nc.alloc_semaphore(name + "_stats_done")
        mv_done = nc.alloc_semaphore(name + "_mv_done")
        std_done = nc.alloc_semaphore(name + "_std_done")
        rstd_done = nc.alloc_semaphore(name + "_rstd_done")
        block = ctx.enter_context(nc.Block())

        @block.scalar
        def _(act):
            act.wait_ge(mv_done, TILES + 1)
            nc.scalar.activation(std[:], mv[:, :, 1], ACT.Sqrt, bias=eps[:, 0:1]).then_inc(std_done, 1)

        @block.vector
        def _(dve):
            nc.vector.memset(eps[:], EPS).then_inc(mv_done, 1)
            if not measured:
                with dve.Fori(0, BATCH) as b:
                    for k in range(KB):
                        t = b * KB + k
                        nc.vector.bn_stats(stats[:, ds(t * 6, 6)], src[:, ds(t * D, D)]).then_inc(stats_done, 1)
                dve.wait_ge(stats_done, TILES)
            for t in range(TILES):
                nc.vector.bn_aggr(mv[:, t, :], stats[:, t * 6:(t + 1) * 6]).then_inc(mv_done, 1)
            dve.wait_ge(std_done, 1)
            nc.vector.reciprocal(rstd[:], std[:]).then_inc(rstd_done, 1)
            dve.wait_ge(rstd_done, 1)
            nc.vector.tensor_tensor(std[:], rstd[:], rstd[:], ALU.mult).then_inc(rstd_done, 1)
            dve.wait_ge(rstd_done, 2)
            nc.vector.scalar_tensor_tensor(out=std[:], in0=mv[:, :, 1], scalar=EPS, in1=std[:],
                                           op0=ALU.add, op1=ALU.mult).then_inc(rstd_done, 1)
            dve.wait_ge(rstd_done, 3)
            nc.vector.tensor_scalar(std[:], std[:], -0.5, 1.5, ALU.mult, ALU.add).then_inc(rstd_done, 1)
            dve.wait_ge(rstd_done, 4)
            nc.vector.tensor_tensor(rstd[:], rstd[:], std[:], ALU.mult).then_inc(rstd_done, 1)
            dve.wait_ge(rstd_done, 5)
            if dst is not None:
                with dve.Fori(0, BATCH) as b:
                    for k in range(KB):
                        t = b * KB + k
                        nc.vector.tensor_scalar(dst[:, ds(t * D, D)], src[:, ds(t * D, D)], column(mv, t),
                                                rstd[:, ds(t, 1)], ALU.subtract, ALU.mult)


def column(mv, tile):
    return mv[:].rearrange("p t s -> p (t s)")[:, ds(tile * 2, 1)]


def apply_norm(nc, dst, src, mv, rstd, tile0):
    for t in range(CPT):
        ins = nc.vector.tensor_scalar(dst[:, t * D:(t + 1) * D], src[:, ds((tile0 + t) * D, D)],
                                      column(mv, tile0 + t), rstd[:, ds(tile0 + t, 1)],
                                      ALU.subtract, ALU.mult)
    return ins


def project(nc, name, src, mv, rstd, wq, wk, wv, qs, ks, vs, ident, heads, v_width,
            gain=None, qk_bias=None, v_bias=None, pos=None):
    q_tiles = wq.shape[1] // P
    items = 2 * q_tiles
    vdim = wv.shape[1]
    hd = vdim // heads
    v_items = vdim // P
    with ExitStack() as ctx:
        def sb(n, shape, dt=FP32):
            return ctx.enter_context(nc.sbuf_tensor(f"{name}_{n}", shape, dt))

        def ps(n):
            return ctx.enter_context(nc.psum_tensor(f"{name}_{n}", [P, CH], FP32))

        def sem(n):
            return nc.alloc_semaphore(f"{name}_{n}")

        w_qk = sb("w_qk", [P, items, P])
        w_v = sb("w_v", [P, vdim])
        xn = [sb(f"xn{i}", [P, CH]) for i in range(2)]
        xnT = sb("xnT", [P, 2, CH])
        NB = 4
        val = [sb(f"val{i}", [P, CH]) for i in range(NB)]
        rem = [sb(f"rem{i}", [P, CH]) for i in range(NB)]
        parts = [sb(f"parts{i}", [P, 3, CH], BF16) for i in range(NB)]
        vpad = [sb(f"vpad{i}", [P, CPT, heads, v_width]) for i in range(2)]
        gain_sb = sb("gain_sb", [P, 2])
        bias_sb = sb("bias_sb", [P, items])
        vb_sb = sb("vb_sb", [P, vdim])
        pos_sb = sb("pos_sb", [P, T])
        t_ps = [ps(f"t_ps{i}") for i in range(2)]
        item_ps = [ps(f"item_ps{i}") for i in range(NB)]
        v_ps = [ps(f"v_ps{i}") for i in range(2)]
        xn_done = sem("xn_done")
        loaded, xT_ready, xT_done = sem("loaded"), sem("xT_ready"), sem("xT_done")
        item_ready, val_done, hi_done = sem("item_ready"), sem("val_done"), sem("hi_done")
        rem_done, mid_done, lo_done = sem("rem_done"), sem("mid_done"), sem("lo_done")
        v_ready, v_done, v_preset = sem("v_ready"), sem("v_done"), sem("v_preset")
        stored = [sem(f"stored{i}") for i in range(NB)]
        v_stored = [sem(f"v_stored{i}") for i in range(2)]
        n_loads = 3 + sum(a is not None for a in (gain, qk_bias, v_bias, pos))
        block = ctx.enter_context(nc.Block())

        @block.sync
        def _(sp):
            sp.dma_start(w_qk[:, 0:q_tiles, :], wq.rearrange("c (n d) -> c n d", d=P)).then_inc(loaded, 16)
            sp.dma_start(w_qk[:, q_tiles:, :], wk.rearrange("c (n d) -> c n d", d=P)).then_inc(loaded, 16)
            sp.dma_start(w_v[:], wv).then_inc(loaded, 16)
            if gain is not None:
                sp.dma_start(gain_sb[:], gain).then_inc(loaded, 16)
            if qk_bias is not None:
                sp.dma_start(bias_sb[:], qk_bias).then_inc(loaded, 16)
            if v_bias is not None:
                sp.dma_start(vb_sb[:], v_bias.to_broadcast([P, vdim])).then_inc(loaded, 16)
            if pos is not None:
                sp.dma_start(pos_sb[:], pos).then_inc(loaded, 16)
            with sp.Fori(0, BATCH) as b:
                for half in range(2):
                    c = b * 2 + half
                    for i in range(items):
                        dram, tile = (qs, i) if i < q_tiles else (ks, i - q_tiles)
                        buf = (half * items + i) % NB
                        sp.wait_ge(lo_done, c * items + (i + 1 + NB))
                        sp.dma_start(dram[ds(b, 1), :, tile * P:(tile + 1) * P, half * CH:(half + 1) * CH]
                                     .rearrange("a k f t -> f (a k) t"), parts[buf][:]).then_inc(stored[buf], 16)
                    sp.wait_ge(v_done, (c + 1) * v_items + 2)
                    sp.dma_start(vs[ds(b, 1), :, half * CPT:(half + 1) * CPT, :].rearrange("a p k v -> (a p) k v"),
                                 vpad[half][:].rearrange("p k h v -> p k (h v)")).then_inc(v_stored[half], 16)
            for i in range(NB):
                sp.wait_ge(stored[i], 16 * (CHUNKS * items // NB + 1))
            for i in range(2):
                sp.wait_ge(v_stored[i], 16 * (BATCH + 1))

        @block.tensor
        def _(te):
            te.wait_ge(loaded, 16 * n_loads)
            te.sem_inc(xT_done, 2)
            te.sem_inc(val_done, NB)
            te.sem_inc(v_done, 2)
            with te.Fori(0, BATCH) as b:
                for half in range(2):
                    c = b * 2 + half
                    te.wait_ge(xT_done, c + 1)
                    te.wait_ge(xn_done, c + 1)
                    for t in range(CPT):
                        mm = nc.tensor.transpose(t_ps[half][:, t * P:(t + 1) * P], xn[half][:, t * P:(t + 1) * P], ident[:])
                    mm.then_inc(xT_ready, 1)
                for half in range(2):
                    c = b * 2 + half
                    te.wait_ge(xT_done, c + 3)
                    for i in range(items):
                        te.wait_ge(val_done, c * items + (i + 1))
                        nc.tensor.matmul(item_ps[(half * items + i) % NB][:], w_qk[:, i, :], xnT[:, half, :],
                                         start=True, stop=True).then_inc(item_ready, 1)
                    for i in range(v_items):
                        bank = v_ps[half if v_items == 1 else i % 2]
                        te.wait_ge(v_done, c * v_items + (i + 1))
                        for t in range(CPT // v_items):
                            r = (i + t) * P
                            mm = nc.tensor.matmul(bank[:, t * vdim:(t + 1) * vdim], xnT[:, half, r:r + P], w_v[:],
                                                  start=True, stop=True)
                        mm.then_inc(v_ready, 1)

        @block.scalar
        def _(act):
            for i in range(NB):
                act.sem_inc(stored[i], 16)
            act.wait_ge(loaded, 16 * n_loads)
            with act.Fori(0, BATCH) as b:
                for half in range(2):
                    act.wait_ge(xT_ready, b * 2 + (half + 1))
                    if gain is None:
                        nc.scalar.activation(xnT[:, half, :], t_ps[half][:], ACT.Copy).then_inc(xT_done, 1)
                    else:
                        nc.scalar.activation(xnT[:, half, :], t_ps[half][:], ACT.Identity, bias=gain_sb[:, 1:2],
                                             scale=gain_sb[:, 0:1]).then_inc(xT_done, 1)
                for n in range(2 * items + 1):
                    k = b * (2 * items) + n
                    if n < 2 * items:
                        act.wait_ge(val_done, k + (1 + NB))
                        act.wait_ge(stored[n % NB], (b * (2 * items // NB) + (n // NB + 1)) * 16)
                        nc.scalar.activation(parts[n % NB][:, 0, :], val[n % NB][:], ACT.Copy).then_inc(hi_done, 1)
                    if n > 0:
                        act.wait_ge(rem_done, k + NB)
                        nc.scalar.activation(parts[(n - 1) % NB][:, 1, :], rem[(n - 1) % NB][:], ACT.Copy).then_inc(mid_done, 1)

        @block.gpsimd
        def _(pool):
            if v_width > hd:
                for vp in vpad:
                    nc.gpsimd.memset(vp[:], 0.0).then_inc(v_preset, 1)
                pool.wait_ge(v_preset, 2)
                for vp in vpad:
                    nc.gpsimd.memset(vp[:, :, :, hd:hd + 1], 1.0).then_inc(v_preset, 1)
            pool.sem_inc(lo_done, NB)
            with pool.Fori(0, BATCH) as b:
                for n in range(2 * items):
                    pool.wait_ge(mid_done, b * (2 * items) + (n + 1))
                    nc.gpsimd.tensor_tensor(parts[n % NB][:, 2, :], rem[n % NB][:], parts[n % NB][:, 1, :],
                                            ALU.subtract).then_inc(lo_done, 1)

        @block.vector
        def _(dve):
            dve.sem_inc(v_stored[0], 16)
            dve.sem_inc(v_stored[1], 16)
            dve.sem_inc(rem_done, NB)
            if v_width > hd:
                dve.wait_ge(v_preset, 4)
            dve.wait_ge(loaded, 16 * n_loads)

            def norm(b):
                for half in range(2):
                    apply_norm(nc, xn[half], src, mv, rstd, b * KB + half * CPT).then_inc(xn_done, 1)

            def sequence(b, last):
                def value(n):
                    k, half, i = b * (2 * items) + n, n // items, n % items
                    dve.wait_ge(item_ready, k + 1)
                    dve.wait_ge(rem_done, k + 1)
                    out, fresh = val[n % NB][:], item_ps[n % NB][:]
                    if qk_bias is not None:
                        ins = nc.vector.tensor_scalar(out, fresh, bias_sb[:, i:i + 1], None, ALU.add)
                    elif pos is not None:
                        ins = nc.vector.tensor_tensor(out, fresh, pos_sb[:, half * CH:(half + 1) * CH], ALU.add)
                    else:
                        ins = nc.vector.tensor_copy(out, fresh)
                    ins.then_inc(val_done, 1)

                def remainder(n):
                    k = b * (2 * items) + n
                    dve.wait_ge(hi_done, k + 1)
                    dve.wait_ge(lo_done, k + 1)
                    nc.vector.tensor_tensor(rem[n % NB][:], val[n % NB][:], parts[n % NB][:, 0, :],
                                            ALU.subtract).then_inc(rem_done, 1)

                def values_out(half):
                    c = b * 2 + half
                    for i in range(v_items):
                        dve.wait_ge(v_ready, c * v_items + (i + 1))
                        if i == 0:
                            dve.wait_ge(v_stored[half], (b + 1) * 16)
                        bank = v_ps[half if v_items == 1 else i % 2]
                        t0, tn = (0, CPT) if v_items == 1 else (i, 1)
                        out = vpad[half][:, t0:t0 + tn, :, 0:hd]
                        fresh = bank[:].rearrange("p (t h v) -> p t h v", t=tn, v=hd)
                        if v_bias is None:
                            ins = nc.vector.tensor_copy(out, fresh)
                        else:
                            ins = nc.vector.tensor_tensor(
                                out, fresh, vb_sb[:].rearrange("p (o h v) -> p o h v", o=1, v=hd)
                                .to_broadcast([P, tn, heads, hd]), ALU.add)
                        ins.then_inc(v_done, 1)

                value(0)
                for n in range(2 * items):
                    if n == items - 1:
                        values_out(0)
                    if n + 1 < 2 * items:
                        value(n + 1)
                    remainder(n)
                    if n == items and not last:
                        norm(b + 1)
                values_out(1)

            norm(0)
            with dve.Fori(0, BATCH - 1) as b:
                sequence(b, False)
            sequence(BATCH - 1, True)


PAIRS = 9
SPLIT_ROWS = 96


class Shape:

    def __init__(self, heads, hd, v_width, causal):
        self.heads, self.hd, self.v_width, self.causal = heads, hd, v_width, causal
        self.wide = hd == 64
        self.per_exp = 1 if self.wide else 2
        self.exps = heads // self.per_exp
        self.steps = [(hq, kb) for hq in range(2) for kb in range(KB) if not causal or kb < CPT * (hq + 1)]
        self.slots = [(j, qt, kh) for j in range(heads) for qt in range(KB) for kh in range(2)
                      if not causal or CPT * kh <= qt]
        self.half_end = [max(n for n, (hq, _) in enumerate(self.steps) if hq == h) for h in range(2)]
        self.lead = 5 if causal else 4
        self.n = len(self.steps)

    def off(self, hq, kb):
        return max(0, kb - CPT * hq) * P if self.causal else 0

    def a_slots(self, n):
        total = len(self.slots)
        first, last = (n + self.lead) * total // self.n, (n + 1 + self.lead) * total // self.n
        return [(1 + s // total, s % total) for s in range(first, last)]

    def head_start(self):
        return range(self.lead * len(self.slots) // self.n)


def attention(nc, name, shape, scale, qs, ks, vs, ctx_nat, consts, floor=None):
    H, W, S = shape.heads, shape.wide, shape.n
    NA = len(shape.slots)
    vcols = H * shape.v_width
    feats = ctx_nat.shape[1] // TILES
    unit_feats = H * shape.hd
    vrows = P // H
    with ExitStack() as ctx:
        def sb(n, shp, dt=FP32):
            return ctx.enter_context(nc.sbuf_tensor(f"{name}_{n}", shp, dt))

        def ps(n, shp):
            return ctx.enter_context(nc.psum_tensor(f"{name}_{n}", shp, FP32))

        def sem(n):
            return nc.alloc_semaphore(f"{name}_{n}")

        ident, ident_bf, mask_a, mask_b = consts["ident"], consts["ident_bf"], consts["mask_a"], consts["mask_b"]
        R = GROUPS
        NB = 2 if W else 4
        LAG = 1 if W else 2
        TURN = 2
        if W:
            q_op = [sb(f"q_op{i}", [P, 2, H, T], BF16) for i in range(R)]
            k_op = [sb(f"k_op{i}", [P, 3, H, T], BF16) for i in range(R)]
            m_op = [sb(f"m_op{i}", [P, H, T], BF16) for i in range(2)]
        else:
            q_op = [sb(f"q_op{i}", [SPLIT_ROWS, H, T], BF16) for i in range(R)]
            k_op = [sb(f"k_op{i}", [SPLIT_ROWS, H, T], BF16) for i in range(R)]
        v_op = [sb(f"v_op{i}", [P, KB, vcols]) for i in range(R)]
        probs = [sb(f"probs{i}", [P, H, CH]) for i in range(NB)]
        o_sb = [sb(f"o_sb{i}", [P, CH]) for i in range(2)]
        if W:
            key_sum = sb("key_sum", [P, H, CH])
            ones = sb("ones", [P, 32])
            sum_sb = sb("sum_sb", [H * 32, CH])
        rec = sb("rec", [P, CPT, H])
        part_max = [sb(f"part_max{i}", [P, 2, H * KB]) for i in range(2)]
        row_max = sb("row_max", [P, H * KB])
        neg_max = sb("neg_max", [H * KB, P])
        neg_rem = sb("neg_rem", [H * KB, P])
        zeros = sb("zeros", [H * KB, 1])
        max_parts = [sb(f"max_parts{i}", [H * KB, 3, P], BF16) for i in range(2)]
        scores = [ps(f"scores{i}", [P, shape.per_exp, CH]) for i in range(2)]
        slot_ps = [ps(f"slot_ps{i}", [P, CH]) for i in range(2)]
        o_ps = ps("o_ps", [P, CH])
        turn_ps = ps("turn_ps", [P, CH])
        if W:
            sum_ps = ps("sum_ps", [H * 32, CH])
            sum_turn_ps = ps("sum_turn_ps", [P, CPT * H * 32])

        key_summed, sums_ready, sums_copied = sem("key_summed"), sem("sums_ready"), sem("sums_copied")
        preset, late_preset = sem("preset"), sem("late_preset")
        op_loaded = [sem(f"op_loaded{i}") for i in range(R)]
        max_loaded = [sem(f"max_loaded{i}") for i in range(R)]
        slot_ready, slot_done = sem("slot_ready"), sem("slot_done")
        row_max_done, neg_done, parts_done, pool_step = (
            sem("row_max_done"), sem("neg_done"), sem("parts_done"), sem("pool_step"))
        scores_ready, probs_done, pv_done = sem("scores_ready"), sem("probs_done"), sem("pv_done")
        o_copied, turned, turn_free, rec_done = sem("o_copied"), sem("turned"), sem("turn_free"), sem("rec_done")
        block = ctx.enter_context(nc.Block())

        def unit(b, g):
            return b * GROUPS + g

        def unit_before(b, g):
            return (b, g - 1) if g > 0 else (b - 1, GROUPS - 1)

        def next_unit(b, g, d):
            return (b, g + d) if g + d < GROUPS else (b + 1, g + d - GROUPS)

        n_loads = 11 if W else 21
        turns = 3 * GROUPS

        @block.sync
        def _(sp):
            def load(b, g):
                i = g
                b_ = ds(b, 1)
                if not W:
                    f0 = g * 32
                    for a in range(3):
                        for c in range(3):
                            r0 = (3 * a + c) * 8
                            for op, dram, part in ((q_op, qs, a), (k_op, ks, c)):
                                sp.dma_start(op[i][r0:r0 + 8, :, :],
                                             dram[b_, part, f0:f0 + 32, :]
                                             .rearrange("a (j r) t -> (a r) j t", r=8)).then_inc(op_loaded[i], 16)
                    sp.dma_start(q_op[i][72:75, :, :].rearrange("r j t -> r (j t)"), consts["zero_rows"]).then_inc(op_loaded[i], 16)
                    sp.dma_start(k_op[i][72:75, :, :].rearrange("r j t -> r (j t)"), consts["one_rows"]).then_inc(op_loaded[i], 16)
                    sp.dma_start(v_op[i][:], vs[b_, :, :, g * vcols:(g + 1) * vcols]
                                 .rearrange("a p k v -> (a p) k v")).then_inc(op_loaded[i], 16)
                else:
                    f0 = g * H * 64

                    def fetch(op, which, row, dram, part):
                        sp.dma_start(op[i][row:row + 64, which, :, :],
                                     dram[b_, part, f0:f0 + H * 64, :]
                                     .rearrange("a (j r) t -> (a r) j t", r=64)).then_inc(op_loaded[i], 16)

                    fetch(q_op, 0, 0, qs, 0)
                    fetch(q_op, 0, 64, qs, 1)
                    fetch(q_op, 1, 0, qs, 0)
                    fetch(q_op, 1, 64, qs, 2)
                    fetch(k_op, 0, 0, ks, 0)
                    fetch(k_op, 0, 64, ks, 0)
                    fetch(k_op, 1, 0, ks, 1)
                    fetch(k_op, 1, 64, ks, 1)
                    fetch(k_op, 2, 0, ks, 2)
                    fetch(k_op, 2, 64, ks, 0)
                    sp.dma_start(v_op[i][:], vs[b_, :, :, g * vcols:(g + 1) * vcols]
                                 .rearrange("a p k v -> (a p) k v")).then_inc(op_loaded[i], 16)

            def load_max(b, g):
                i = g
                sp.wait_ge(parts_done, unit(b, g) + 1)
                for part in range(3):
                    row = m_op[i % 2][part:part + 1, :, :] if W else q_op[i][72 + part:73 + part, :, :]
                    sp.dma_start(row.rearrange("r j t -> r (j t)"), max_parts[g % 2][:, part, :]).then_inc(max_loaded[i], 16)

            def sequence(b, last):
                for g in range(GROUPS):
                    if g < GROUPS - 1:
                        load_max(b, g + 1)
                    elif not last:
                        load_max(b + 1, 0)
                    if not last:
                        sp.wait_ge(pv_done, (unit(b, g) + 1) * S + NB)
                        load(b + 1, g)

            for g in range(R):
                if not W and g == 0:
                    sp.wait_ge(preset, 1)
                elif not W:
                    sp.wait_ge(late_preset, g)
                load(0, g)
                if g == 1:
                    if W:
                        sp.wait_ge(preset, 1)
                    load_max(0, 0)
            with sp.Fori(0, BATCH - 1) as b:
                sequence(b, False)
            sequence(BATCH - 1, True)

        @block.tensor
        def _(te):
            te.sem_inc(probs_done, shape.exps)
            te.sem_inc(o_copied, 1)
            def a_slot(b, g, s):
                j, qt, kh = shape.slots[s]
                i = g
                k = unit(b, g) * NA + s
                if s == 0:
                    te.wait_ge(op_loaded[i], (b + 1) * (16 * n_loads))
                if not (isinstance(k, int) and k < 2):
                    te.wait_ge(slot_done, k - 1)
                width = min(CH, (qt + 1) * P - kh * CH) if shape.causal else CH
                out = slot_ps[s % 2]
                q0, k0 = qt * P, kh * CH
                diag = shape.causal and qt // CPT == kh
                if W:
                    pairs = [(q_op[i][:, 0, j, q0:q0 + P], k_op[i][:, n, j, k0:k0 + width]) for n in range(2)]
                else:
                    pairs = [(q_op[i][:, j, q0:q0 + P], k_op[i][:, j, k0:k0 + width])]
                for n, (q, k_) in enumerate(pairs):
                    mm = nc.tensor.matmul(out[:, 0:width], q, k_, start=n == 0, stop=n == len(pairs) - 1 and not diag)
                if diag:
                    mm = nc.tensor.matmul(out[:, width - P:width], ident_bf[:], mask_a[:], start=False, stop=True)
                mm.then_inc(slot_ready, 1)

            def max_turn(b, g, k):
                te.wait_ge(row_max_done, unit(b, g) + 1)
                if not (isinstance(k, int) and k == 0):
                    te.wait_ge(turn_free, k)
                nc.tensor.transpose(turn_ps[0:H * KB, 0:P], row_max[:], ident[:]).then_inc(turned, 1)

            def o_turn(b, g, hq, k):
                if W:
                    te.wait_ge(sums_copied, unit(b, g) * 2 + (hq + 2))
                te.wait_ge(o_copied, unit(b, g) * 2 + (hq + 2))
                te.wait_ge(turn_free, k)
                for t in range(CPT):
                    mm = nc.tensor.transpose(turn_ps[:, t * P:(t + 1) * P], o_sb[hq][:, t * P:(t + 1) * P], ident[:])
                if W:
                    for t in range(CPT):
                        mm = nc.tensor.transpose(sum_turn_ps[:, t * H * 32:(t + 1) * H * 32], sum_sb[:, t * P:(t + 1) * P],
                                                 ident[0:H * 32, 0:H * 32])
                mm.then_inc(turned, 1)

            def sum_up(b, g, hq):
                te.wait_ge(key_summed, unit(b, g) * S + (shape.half_end[hq] + 1 + NB))
                te.wait_ge(sums_copied, unit(b, g) * 2 + (hq + 1))
                for j in range(H):
                    mm = nc.tensor.matmul(sum_ps[32 * j:32 * j + 32, :], ones[:], key_sum[:, j, :], start=True, stop=True)
                mm.then_inc(sums_ready, 1)

            def step_scores(b, g, n, e):
                hq, kb = shape.steps[n]
                i = g
                off = shape.off(hq, kb)
                gs = unit(b, g) * S + n
                te.wait_ge(probs_done, gs * shape.exps + (e + 1))
                diag = shape.causal and kb >= CPT * hq
                for jj in range(shape.per_exp):
                    j = e * shape.per_exp + jj
                    out = scores[e][:, jj, off:CH]
                    k0, q0, q1 = kb * P, hq * CH + off, (hq + 1) * CH
                    if W:
                        pairs = [(k_op[i][:, n_, j, k0:k0 + P], q_op[i][:, m_, j, q0:q1]) for n_, m_ in ((0, 0), (1, 0), (2, 1))]
                        pairs.append((consts["one_stat"][:], m_op[i % 2][:, j, q0:q1]))
                    else:
                        pairs = [(k_op[i][:, j, k0:k0 + P], q_op[i][:, j, q0:q1])]
                    for n_, (k_, q) in enumerate(pairs):
                        mm = nc.tensor.matmul(out, k_, q, start=n_ == 0, stop=n_ == len(pairs) - 1 and not diag)
                    if diag:
                        mm = nc.tensor.matmul(scores[e][:, jj, off:off + P], ident_bf[:], mask_b[:], start=False, stop=True)
                mm.then_inc(scores_ready, 1)

            def step_pv(b, g, n, part=None):
                hq, kb = shape.steps[n]
                i = g
                off = shape.off(hq, kb)
                if part != 1:
                    te.wait_ge(probs_done, (unit(b, g) * S + (n + 1)) * shape.exps + shape.exps)
                    if kb == 0:
                        te.wait_ge(o_copied, unit(b, g) * 2 + (hq + 1))
                whole = part is None or kb == 0
                if whole and part == 1:
                    return
                middle = (off + CH) // 2
                c0, c1 = (off, CH) if whole else (off, middle) if part == 0 else (middle, CH)
                for j in range(H):
                    v = v_op[i][:, kb, j * shape.v_width:(j + 1) * shape.v_width]
                    out = o_ps[vrows * j:vrows * (j + 1), c0:c1]
                    mm = nc.tensor.matmul(out, v, probs[n % NB][:, j, c0:c1], start=kb == 0,
                                          stop=n in shape.half_end and part != 0)
                if whole or part == 1:
                    mm.then_inc(pv_done, 1)

            def behind(b, g, n, k, first, part=None):
                before = not first or g > 0
                if n >= LAG:
                    step_pv(b, g, n - LAG, part)
                elif before:
                    step_pv(*unit_before(b, g), S + n - LAG, part)
                if part == 0:
                    return
                if W and n == 1 and before:
                    sum_up(*unit_before(b, g), 1)
                if W and n == shape.half_end[0] + 2:
                    sum_up(b, g, 0)
                if n == TURN and before:
                    o_turn(*unit_before(b, g), 1, k - 1)
                if n == shape.half_end[0] + TURN + 1:
                    o_turn(b, g, 0, k)

            def sequence(b, first, last):
                for g in range(GROUPS):
                    k = b * turns + (3 * g + 1)
                    te.wait_ge(max_loaded[g], (b + 1) * (3 * 16) + 16)
                    for n in range(S):
                        ahead = [(d, s) for d, s in shape.a_slots(n) if not last or g + d < GROUPS]
                        places = 2 if W else 4
                        cut = [len(ahead) * p // places for p in range(places + 1)]

                        def fill_slots(p):
                            for d, s in ahead[cut[p]:cut[p + 1]]:
                                a_slot(*next_unit(b, g, d), s)

                        if W:
                            for e in range(shape.exps):
                                step_scores(b, g, n, e)
                                fill_slots(e)
                            behind(b, g, n, k, first)
                        else:
                            for e in range(shape.exps):
                                behind(b, g, n, k, first, e)
                                fill_slots(2 * e)
                                step_scores(b, g, n, e)
                                fill_slots(2 * e + 1)
                        if n == S - shape.lead and not (last and g == GROUPS - 1):
                            max_turn(*next_unit(b, g, 1), k + 1)
                if last:
                    for n in range(S - LAG, S):
                        step_pv(b, GROUPS - 1, n)
                    if W:
                        sum_up(b, GROUPS - 1, 1)
                    o_turn(b, GROUPS - 1, 1, b * turns + turns - 1)

            for s in range(NA):
                a_slot(0, 0, s)
            max_turn(0, 0, 0)
            for s in shape.head_start():
                a_slot(0, 1, s)
            sequence(0, True, False)
            with te.Fori(1, BATCH - 1) as b:
                sequence(b, False, False)
            sequence(BATCH - 1, False, True)

        @block.gpsimd
        def _(pool):
            nc.gpsimd.memset(zeros[:], 0.0).then_inc(pool_step, 1)
            pool.wait_ge(pool_step, 1)
            if not W:
                for i in range(1, R):
                    nc.gpsimd.memset(q_op[i][64:96, :, :], 0.0)
                    nc.gpsimd.memset(k_op[i][64:96, :, :], 0.0).then_inc(late_preset, 1)
            for i in range(R):
                pool.sem_inc(max_loaded[i], 16)

            def split_max(b, g, k):
                out = max_parts[g % 2]
                u = unit(b, g)
                pool.wait_ge(turn_free, k + 1)
                if not (isinstance(u, int) and u < 2):
                    pool.wait_ge(max_loaded[(g + 2) % R], (b if g < 2 else b + 1) * 48 + 16)
                nc.gpsimd.tensor_tensor(out[:, 0, :], neg_max[:], zeros[:].to_broadcast([H * KB, P]), ALU.add).then_inc(pool_step, 1)
                pool.wait_ge(pool_step, u * 3 + 2)
                nc.gpsimd.tensor_tensor(neg_rem[:], neg_max[:], out[:, 0, :], ALU.subtract).then_inc(pool_step, 1)
                pool.wait_ge(pool_step, u * 3 + 3)
                nc.gpsimd.tensor_tensor(out[:, 1, :], neg_rem[:], zeros[:].to_broadcast([H * KB, P]), ALU.add).then_inc(pool_step, 1)
                pool.wait_ge(pool_step, u * 3 + 4)
                nc.gpsimd.tensor_tensor(out[:, 2, :], neg_rem[:], out[:, 1, :], ALU.subtract).then_inc(parts_done, 1)

            def sequence(b, last):
                for g in range(GROUPS - 1 if last else GROUPS):
                    split_max(*next_unit(b, g, 1), b * turns + (3 * g + 2))

            split_max(0, 0, 0)
            with pool.Fori(0, BATCH - 1) as b:
                sequence(b, False)
            sequence(BATCH - 1, True)

        @block.scalar
        def _(act):
            act.sem_inc(pv_done, NB)
            if W:
                act.sem_inc(key_summed, NB)
                act.sem_inc(sums_copied, 1)

            def copy_out(b, g, hq):
                act.wait_ge(pv_done, unit(b, g) * S + (shape.half_end[hq] + 1 + NB))
                nc.scalar.activation(o_sb[hq][:], o_ps[:], ACT.Copy).then_inc(o_copied, 1)

            def copy_sums(b, g, hq, k):
                act.wait_ge(sums_ready, unit(b, g) * 2 + (hq + 2))
                act.wait_ge(turned, k)
                nc.scalar.activation(sum_sb[:], sum_ps[:], ACT.Copy).then_inc(sums_copied, 1)

            def copies(b, g, n, first):
                before = not first or g > 0
                k = b * turns + (3 * g + 1)
                if W and n == 1 and before:
                    copy_sums(*unit_before(b, g), 1, k - 2)
                if W and n == shape.half_end[0] + 2:
                    copy_sums(b, g, 0, k)
                if n == LAG - 1 and before:
                    copy_out(*unit_before(b, g), 1)
                if n == shape.half_end[0] + LAG:
                    copy_out(b, g, 0)

            def sequence(b, first, last):
                for g in range(GROUPS):
                    for n, (hq, kb) in enumerate(shape.steps):
                        off = shape.off(hq, kb)
                        gs = unit(b, g) * S + n
                        if not W:
                            copies(b, g, n, first)
                        for e in range(shape.exps):
                            act.wait_ge(scores_ready, gs * shape.exps + (e + 1))
                            if e == 0:
                                act.wait_ge(pv_done, gs + 1)
                                if W:
                                    act.wait_ge(key_summed, gs + 1)
                            j = e * shape.per_exp
                            nc.scalar.activation(probs[n % NB][:, j:j + shape.per_exp, off:CH], scores[e][:, :, off:CH],
                                                 ACT.Exp, scale=scale).then_inc(probs_done, 1)
                        if W:
                            copies(b, g, n, first)
                if last:
                    copy_out(b, GROUPS - 1, 1)
                    if W:
                        copy_sums(b, GROUPS - 1, 1, b * turns + (turns - 1))

            sequence(0, True, False)
            with act.Fori(1, BATCH - 1) as b:
                sequence(b, False, False)
            sequence(BATCH - 1, False, True)

        @block.vector
        def _(dve):
            if W:
                for i in range(2):
                    ins = nc.vector.memset(m_op[i][:], 0.0)
                nc.vector.memset(ones[:], 1.0)
                ins.then_inc(preset, 1)
                dve.sem_inc(sums_ready, 1)
            else:
                nc.vector.memset(q_op[0][64:96, :, :], 0.0)
                nc.vector.memset(k_op[0][64:96, :, :], 0.0).then_inc(preset, 1)
            if shape.causal:
                for i in range(2):
                    nc.vector.memset(part_max[i][:, 1, :], -3e38).then_inc(rec_done, 1)
            base = 2 if shape.causal else 0

            def a_slot(b, g, s):
                j, qt, kh = shape.slots[s]
                width = min(CH, (qt + 1) * P - kh * CH) if shape.causal else CH
                col = j * KB + qt
                dve.wait_ge(slot_ready, unit(b, g) * NA + (s + 1))
                nc.vector.tensor_reduce(part_max[g % 2][:, kh, col:col + 1], slot_ps[s % 2][:, 0:width],
                                        axis=AX.X, op=ALU.max).then_inc(slot_done, 1)

            def row_maxima(b, g, k):
                u = unit(b, g)
                dve.wait_ge(slot_done, (u + 1) * NA)
                nc.vector.tensor_tensor(row_max[:], part_max[g % 2][:, 0, :], part_max[g % 2][:, 1, :],
                                        ALU.max).then_inc(row_max_done, 1)
                dve.wait_ge(turned, k + 1)
                if not (isinstance(u, int) and u == 0):
                    dve.wait_ge(parts_done, u)
                nc.vector.tensor_scalar(neg_max[:], turn_ps[0:H * KB, 0:P], -1.0, None, ALU.mult).then_inc(turn_free, 1)

            def add_keys(b, g, n):
                hq, kb = shape.steps[n]
                off = shape.off(hq, kb)
                gs = unit(b, g) * S + n
                dve.wait_ge(probs_done, (gs + 2) * shape.exps)
                if kb == 0:
                    dve.wait_ge(sums_ready, unit(b, g) * 2 + (hq + 1))
                    ins = nc.vector.tensor_copy(key_sum[:], probs[n % NB][:])
                else:
                    dve.wait_ge(key_summed, gs + NB)
                    ins = nc.vector.tensor_tensor(key_sum[:, :, off:CH], key_sum[:, :, off:CH], probs[n % NB][:, :, off:CH],
                                                  ALU.add)
                ins.then_inc(key_summed, 1)

            def normalise(b, g, hq, k):
                dve.wait_ge(turned, k + 1)
                count = (unit(b, g) * 2 + hq) * (2 if floor else 1) + (1 + base)
                o = turn_ps[:].rearrange("p (t j v) -> p t j v", t=CPT, j=H)
                sums = (sum_turn_ps[:].rearrange("p (t j v) -> p t j v", t=CPT, j=H)[:, :, :, 0] if W
                        else o[:, :, :, shape.hd])
                if floor:
                    nc.vector.tensor_scalar(rec[:], sums, floor, None, ALU.max).then_inc(rec_done, 1)
                    dve.wait_ge(rec_done, count)
                    nc.vector.reciprocal(rec[:], rec[:]).then_inc(rec_done, 1)
                    dve.wait_ge(rec_done, count + 1)
                else:
                    nc.vector.reciprocal(rec[:], sums).then_inc(rec_done, 1)
                    dve.wait_ge(rec_done, count)
                out = (ctx_nat[:, ds(b * (KB * feats) + hq * CPT * feats, CPT * feats)]
                       .rearrange("p (t f) -> p t f", f=feats)[:, :, g * unit_feats:(g + 1) * unit_feats]
                       .rearrange("p t (j d) -> p t j d", d=shape.hd))
                nc.vector.tensor_tensor(out, o[:, :, :, 0:shape.hd],
                                        rec[:].unsqueeze(3).to_broadcast([P, CPT, H, shape.hd]),
                                        ALU.mult).then_inc(turn_free, 1)

            def sequence(b, first, last):
                for g in range(GROUPS):
                    before = not first or g > 0
                    k = b * turns + (3 * g + 1)
                    for n in range(S):
                        for d, s in shape.a_slots(n):
                            if not last or g + d < GROUPS:
                                a_slot(*next_unit(b, g, d), s)
                        if W and n > 0:
                            add_keys(b, g, n - 1)
                        elif W and before:
                            add_keys(*unit_before(b, g), S - 1)
                        if n == TURN and before:
                            normalise(*unit_before(b, g), 1, k - 1)
                        if n == shape.half_end[0] + TURN + 1:
                            normalise(b, g, 0, k)
                        if n == S - shape.lead and not (last and g == GROUPS - 1):
                            row_maxima(*next_unit(b, g, 1), k + 1)
                if last:
                    if W:
                        add_keys(b, GROUPS - 1, S - 1)
                    normalise(b, GROUPS - 1, 1, b * turns + (turns - 1))

            for s in range(NA):
                a_slot(0, 0, s)
            row_maxima(0, 0, 0)
            for s in shape.head_start():
                a_slot(0, 1, s)
            sequence(0, True, False)
            with dve.Fori(1, BATCH - 1) as b:
                sequence(b, False, False)
            sequence(BATCH - 1, False, True)


def out_project(nc, name, nat, feats, wo, x, stats, consts, bias=None, rms=None):
    ft = feats // P
    NT = 4
    with ExitStack() as ctx:
        def sb(n, shp, dt=FP32):
            return ctx.enter_context(nc.sbuf_tensor(f"{name}_{n}", shp, dt))

        def sem(n):
            return nc.alloc_semaphore(f"{name}_{n}")

        w = sb("w", [P, ft, D])
        bias_sb = sb("bias_sb", [P, D])
        natT = [sb(f"natT{i}", [P, ft, CH]) for i in range(2)]
        t_ps = [ctx.enter_context(nc.psum_tensor(f"{name}_t_ps{i}", [P, CH], FP32)) for i in range(NT)]
        y_ps = [ctx.enter_context(nc.psum_tensor(f"{name}_y_ps{i}", [P, CH], FP32)) for i in range(2)]
        loaded, normed, turned, copied, y_ready, y_done, bias_done = (
            sem(n) for n in ("loaded", "normed", "turned", "copied", "y_ready", "y_done", "bias_done"))
        if rms is not None:
            group, eps_value, factor, weight = rms
            n_groups = TILES * feats // group
            weight_sb = sb("weight_sb", [P, 1])
            eps = sb("eps", [P, 1])
            square = sb("square", [P, TILES * feats])
            ms = sb("ms", [P, n_groups])
            rs = sb("rs", [P, n_groups])
            sq_done, ms_done, root_done, rs_done = (sem(n) for n in ("sq_done", "ms_done", "root_done", "rs_done"))
        n_loads = 1 + (bias is not None) + (rms is not None)
        block = ctx.enter_context(nc.Block())

        @block.sync
        def _(sp):
            sp.dma_start(w[:], wo.rearrange("(n p) d -> p n d", p=P)).then_inc(loaded, 16)
            if bias is not None:
                sp.dma_start(bias_sb[:], bias.to_broadcast([P, D])).then_inc(loaded, 16)
            if rms is not None:
                sp.dma_start(weight_sb[:], weight).then_inc(loaded, 16)

        @block.tensor
        def _(te):
            def turn(c):
                if rms is not None:
                    te.wait_ge(normed, c // 2 + 1)
                for f in range(ft):
                    p = c * ft + f
                    if p >= NT:
                        te.wait_ge(copied, p - NT + 1)
                    for t in range(CPT):
                        col = (c * CPT + t) * feats + f * P
                        mm = nc.tensor.transpose(t_ps[p % NT][:, t * P:(t + 1) * P], nat[:, col:col + P], consts["ident"][:])
                    mm.then_inc(turned, 1)

            turn(0)
            te.wait_ge(loaded, 16 * n_loads)
            for c in range(CHUNKS):
                if c + 1 < CHUNKS:
                    turn(c + 1)
                te.wait_ge(copied, (c + 1) * ft)
                if c >= 2:
                    te.wait_ge(y_done, c - 1)
                for t in range(CPT):
                    for f in range(ft):
                        mm = nc.tensor.matmul(y_ps[c % 2][:, t * D:(t + 1) * D], natT[c % 2][:, f, t * P:(t + 1) * P],
                                              w[:, f, :], start=f == 0, stop=f == ft - 1)
                mm.then_inc(y_ready, 1)

        @block.scalar
        def _(act):
            if rms is not None:
                act.wait_ge(loaded, 16 * n_loads)
                nc.scalar.activation(square[:], nat[:], ACT.Square).then_inc(sq_done, 1)
                act.wait_ge(ms_done, 2)
                nc.scalar.activation(rs[:], ms[:], ACT.Sqrt, bias=eps[:, 0:1], scale=1.0 / group).then_inc(root_done, 1)
            for p in range(CHUNKS * ft):
                c, f = p // ft, p % ft
                act.wait_ge(turned, p + 1)
                if c >= 2:
                    act.wait_ge(y_ready, c - 1)
                if rms is None:
                    nc.scalar.activation(natT[c % 2][:, f, :], t_ps[p % NT][:], ACT.Copy).then_inc(copied, 1)
                else:
                    nc.scalar.activation(natT[c % 2][:, f, :], t_ps[p % NT][:], ACT.Copy,
                                         scale=weight_sb[:, 0:1]).then_inc(copied, 1)

        @block.vector
        def _(dve):
            if rms is not None:
                nc.vector.memset(eps[:], eps_value).then_inc(ms_done, 1)
                dve.wait_ge(sq_done, 1)
                nc.vector.tensor_reduce(ms[:], square[:].rearrange("p (n g) -> p n g", g=group),
                                        axis=AX.X, op=ALU.add).then_inc(ms_done, 1)
                dve.wait_ge(root_done, 1)
                nc.vector.reciprocal(rs[:], rs[:]).then_inc(rs_done, 1)
                dve.wait_ge(rs_done, 1)
                nc.vector.tensor_scalar(rs[:], rs[:], factor, None, ALU.mult).then_inc(rs_done, 1)
                dve.wait_ge(rs_done, 2)
                n = KB * feats // group
                for b in range(BATCH):
                    part = nat[:, b * KB * feats:(b + 1) * KB * feats].rearrange("p (n g) -> p n g", g=group)
                    nc.vector.tensor_tensor(part, part, rs[:, b * n:(b + 1) * n].unsqueeze(2).to_broadcast([P, n, group]),
                                            ALU.mult).then_inc(normed, 1)
            if bias is not None:
                dve.wait_ge(loaded, 16 * n_loads)
                rows = x[:].rearrange("p (t d) -> p t d", d=D)
                nc.vector.tensor_tensor(rows, rows, bias_sb[:].unsqueeze(1).to_broadcast([P, TILES, D]),
                                        ALU.add).then_inc(bias_done, 1)
                dve.wait_ge(bias_done, 1)
            for c in range(CHUNKS):
                rows = x[:, c * CH:(c + 1) * CH]
                dve.wait_ge(y_ready, c + 1)
                nc.vector.tensor_tensor(rows, rows, y_ps[c % 2][:], ALU.add).then_inc(y_done, 1)
                if c > 0:
                    dve.wait_ge(y_done, c)
                    for t in range((c - 1) * CPT, c * CPT):
                        tile_stats(nc, stats, x, t)
            dve.wait_ge(y_done, CHUNKS)
            for t in range((CHUNKS - 1) * CPT, CHUNKS * CPT):
                tile_stats(nc, stats, x, t)


PAIR_PARTS = [(0, 0), (0, 1), (1, 0), (0, 2), (2, 0), (1, 1)]
MAP_ROWS = len(PAIR_PARTS) * 8


def cosine_scales(nc, name, raw, delta_col, delta_row, gain_col, sign_col, lambdas, factors, neg_lambda):
    with ExitStack() as ctx:
        def sb(n, shp):
            return ctx.enter_context(nc.sbuf_tensor(f"{name}_{n}", shp, FP32))

        raw_sb, col, row = sb("raw_sb", [P, 1]), sb("col", [P, 1]), sb("row", [P, 8])
        gain, sign, lam = sb("gain", [P, 1]), sb("sign", [P, 1]), sb("lam", [P, 4, 8])
        prod, dots, mean, tanh, sig = sb("prod", [P, 2, 8]), sb("dots", [P, 2]), sb("mean", [P, 1]), sb("tanh", [P, 1]), sb("sig", [P, 1])
        loaded = nc.alloc_semaphore(f"{name}_loaded")
        step = nc.alloc_semaphore(f"{name}_step")
        acted = nc.alloc_semaphore(f"{name}_acted")
        block = ctx.enter_context(nc.Block())

        @block.sync
        def _(sp):
            sp.dma_start(raw_sb[:], raw.to_broadcast([P, 1])).then_inc(loaded, 16)
            sp.dma_start(col[:], delta_col).then_inc(loaded, 16)
            sp.dma_start(row[:], delta_row.to_broadcast([P, 8])).then_inc(loaded, 16)
            sp.dma_start(gain[:], gain_col).then_inc(loaded, 16)
            sp.dma_start(sign[:], sign_col).then_inc(loaded, 16)
            sp.dma_start(lam[:].rearrange("p a b -> p (a b)"), lambdas.to_broadcast([P, 32])).then_inc(loaded, 16)

        @block.scalar
        def _(act):
            act.wait_ge(loaded, 96)
            nc.scalar.activation(sig[:], raw_sb[:], ACT.Exp, scale=-1.0).then_inc(acted, 1)
            act.wait_ge(step, 3)
            nc.scalar.activation(tanh[:], col[:], ACT.Tanh).then_inc(acted, 1)
            act.wait_ge(step, 5)
            nc.scalar.activation(dots[:], dots[:], ACT.Exp).then_inc(acted, 1)

        @block.vector
        def _(dve):
            count = [0]

            def then(ins):
                count[0] += 1
                ins.then_inc(step, 1)
                dve.wait_ge(step, count[0])

            dve.wait_ge(loaded, 96)
            then(nc.vector.tensor_reduce(mean[:], row[:], axis=AX.X, op=ALU.add))
            then(nc.vector.tensor_scalar(mean[:], mean[:], 1.0 / 8, None, ALU.mult))
            then(nc.vector.tensor_tensor(col[:], col[:], mean[:], ALU.subtract))
            then(nc.vector.tensor_tensor(prod[:], lam[:, 0:2, :], lam[:, 2:4, :], ALU.mult))
            then(nc.vector.tensor_reduce(dots[:], prod[:], axis=AX.X, op=ALU.add))
            dve.wait_ge(acted, 3)
            then(nc.vector.tensor_scalar(sig[:], sig[:], 1.0, None, ALU.add))
            then(nc.vector.reciprocal(sig[:], sig[:]))
            then(nc.vector.tensor_scalar(sig[:], sig[:], 15.0, None, ALU.mult))
            then(nc.vector.tensor_scalar(tanh[:], tanh[:], 0.5, 1.0, ALU.mult, ALU.add))
            then(nc.vector.tensor_tensor(factors[:, 0:1], sig[:], tanh[:], ALU.mult))
            then(nc.vector.tensor_tensor(gain[:], gain[:], sign[:], ALU.mult))
            then(nc.vector.tensor_tensor(factors[:, 1:2], factors[:, 0:1], gain[:], ALU.mult))
            then(nc.vector.tensor_tensor(neg_lambda[:], dots[:, 1:2], dots[:, 0:1], ALU.subtract))
            then(nc.vector.tensor_scalar(neg_lambda[:], neg_lambda[:], -0.5, None, ALU.add))


def project_cosine(nc, name, src, mv, rstd, wq, wk, wv, factors, ql, qd, ks, vs, ident):
    items = 3
    with ExitStack() as ctx:
        def sb(n, shp, dt=FP32):
            return ctx.enter_context(nc.sbuf_tensor(f"{name}_{n}", shp, dt))

        def ps(n):
            return ctx.enter_context(nc.psum_tensor(f"{name}_{n}", [P, CH], FP32))

        def sem(n):
            return nc.alloc_semaphore(f"{name}_{n}")

        w = [sb(f"w{i}", [P, D]) for i in range(3)]
        NB = 2 * items
        UNITS_B = 4
        xn = [sb(f"xn{i}", [P, CH]) for i in range(2)]
        xnT = sb("xnT", [P, 2, CH])
        square = [sb(f"square{i}", [P, CH]) for i in range(UNITS_B)]
        groups = CH // 8
        ss = sb("ss", [P, UNITS_B, groups])
        root = sb("root", [P, UNITS_B, groups])
        newton = sb("newton", [P, UNITS_B, groups])
        unit = [sb(f"unit{i}", [P, CH]) for i in range(UNITS_B)]
        val = [sb(f"val{i}", [P, CH]) for i in range(NB)]
        rem = [sb(f"rem{i}", [P, CH]) for i in range(NB)]
        parts = [sb(f"parts{i}", [P, 3, CH], BF16) for i in range(NB)]
        vpad = [sb(f"vpad{i}", [P, CPT, 8, 32]) for i in range(2)]
        v_ps = [ps(f"v_ps{i}") for i in range(2)]
        nat_ps = [ps(f"nat_ps{i}") for i in range(UNITS_B)]
        turn_ps = [ps(f"turn_ps{i}") for i in range(2)]
        (loaded, xn_done, xT_ready, xT_done, nat_ready, sq_done, ss_done, root_done, step, unit_done, unitT_ready,
         val_done, hi_done, rem_done, mid_done, lo_done, v_ready, v_done, v_preset) = (sem(n) for n in (
             "loaded", "xn_done", "xT_ready", "xT_done", "nat_ready", "sq_done", "ss_done", "root_done", "step",
             "unit_done", "unitT_ready", "val_done", "hi_done", "rem_done", "mid_done", "lo_done", "v_ready",
             "v_done", "v_preset"))
        stored = [sem(f"stored{i}") for i in range(NB)]
        v_stored = [sem(f"v_stored{i}") for i in range(2)]
        block = ctx.enter_context(nc.Block())

        @block.sync
        def _(sp):
            for i, dram in enumerate((wq, wk, wv)):
                sp.dma_start(w[i][:], dram).then_inc(loaded, 16)
            with sp.Fori(0, BATCH) as b:
                for half in range(2):
                    for i, dram in enumerate((ql, ks, qd)):
                        n = half * items + i
                        sp.wait_ge(lo_done, b * NB + (n + 1))
                        sp.dma_start(dram[ds(b, 1), :, :, half * CH:(half + 1) * CH]
                                     .rearrange("a k f t -> f (a k) t"), parts[n][:]).then_inc(stored[n], 16)
                    sp.wait_ge(v_done, b * 2 + (half + 3))
                    sp.dma_start(vs[ds(b, 1), :, half * CPT:(half + 1) * CPT, :].rearrange("a p k v -> (a p) k v"),
                                 vpad[half][:].rearrange("p k h v -> p k (h v)")).then_inc(v_stored[half], 16)
            for i in range(NB):
                sp.wait_ge(stored[i], 16 * (BATCH + 1))
            for i in range(2):
                sp.wait_ge(v_stored[i], 16 * (BATCH + 1))

        @block.tensor
        def _(te):
            te.wait_ge(loaded, 48)
            te.sem_inc(val_done, 1)
            te.sem_inc(v_done, 2)
            with te.Fori(0, BATCH) as b:
                te.wait_ge(val_done, b * NB + 1)
                for half in range(2):
                    te.wait_ge(xn_done, b * 2 + (half + 1))
                    for t in range(CPT):
                        mm = nc.tensor.transpose(turn_ps[half][:, t * P:(t + 1) * P], xn[half][:, t * P:(t + 1) * P], ident[:])
                    mm.then_inc(xT_ready, 1)
                for half in range(2):
                    te.wait_ge(xT_done, b * 2 + (half + 1))
                    for i in range(2):
                        for t in range(CPT):
                            mm = nc.tensor.matmul(nat_ps[2 * half + i][:, t * P:(t + 1) * P], xnT[:, half, t * P:(t + 1) * P],
                                                  w[i][:], start=True, stop=True)
                        mm.then_inc(nat_ready, 1)
                for half in range(2):
                    te.wait_ge(v_done, b * 2 + (half + 1))
                    for t in range(CPT):
                        mm = nc.tensor.matmul(v_ps[half][:, t * P:(t + 1) * P], xnT[:, half, t * P:(t + 1) * P], w[2][:],
                                              start=True, stop=True)
                    mm.then_inc(v_ready, 1)
                for half in range(2):
                    if half:
                        te.wait_ge(val_done, b * NB + (items + 1))
                    for i in range(2):
                        u = 2 * half + i
                        te.wait_ge(unit_done, b * UNITS_B + (u + 1))
                        for t in range(CPT):
                            mm = nc.tensor.transpose(turn_ps[i][:, t * P:(t + 1) * P], unit[u][:, t * P:(t + 1) * P], ident[:])
                        mm.then_inc(unitT_ready, 1)

        @block.scalar
        def _(act):
            for i in range(NB):
                act.sem_inc(stored[i], 16)
            with act.Fori(0, BATCH) as b:
                for half in range(2):
                    act.wait_ge(xT_ready, b * 2 + (half + 1))
                    nc.scalar.activation(xnT[:, half, :], turn_ps[half][:], ACT.Copy).then_inc(xT_done, 1)
                for u in range(UNITS_B):
                    act.wait_ge(nat_ready, b * UNITS_B + (u + 1))
                    nc.scalar.activation(square[u][:], nat_ps[u][:], ACT.Square).then_inc(sq_done, 1)
                act.wait_ge(ss_done, (b + 1) * (UNITS_B + 1))
                nc.scalar.activation(root[:], ss[:], ACT.Sqrt).then_inc(root_done, 1)
                for n in range(NB + 1):
                    if n < NB:
                        act.wait_ge(val_done, b * NB + (n + 2))
                        act.wait_ge(stored[n], (b + 1) * 16)
                        nc.scalar.activation(parts[n][:, 0, :], val[n][:], ACT.Copy).then_inc(hi_done, 1)
                    if n > 0:
                        act.wait_ge(rem_done, b * NB + n)
                        nc.scalar.activation(parts[n - 1][:, 1, :], rem[n - 1][:], ACT.Copy).then_inc(mid_done, 1)

        @block.gpsimd
        def _(pool):
            for vp in vpad:
                nc.gpsimd.memset(vp[:], 0.0).then_inc(v_preset, 1)
            pool.wait_ge(v_preset, 2)
            for vp in vpad:
                nc.gpsimd.memset(vp[:, :, :, 16:17], 1.0).then_inc(v_preset, 1)
            with pool.Fori(0, BATCH) as b:
                for n in range(NB):
                    pool.wait_ge(mid_done, b * NB + (n + 1))
                    nc.gpsimd.tensor_tensor(parts[n][:, 2, :], rem[n][:], parts[n][:, 1, :], ALU.subtract).then_inc(lo_done, 1)

        @block.vector
        def _(dve):
            dve.sem_inc(v_stored[0], 16)
            dve.sem_inc(v_stored[1], 16)
            dve.wait_ge(v_preset, 4)
            with dve.Fori(0, BATCH) as b:
                for half in range(2):
                    apply_norm(nc, xn[half], src, mv, rstd, b * KB + half * CPT).then_inc(xn_done, 1)
                for u in range(UNITS_B):
                    dve.wait_ge(sq_done, b * UNITS_B + (u + 1))
                    nc.vector.tensor_reduce(ss[:, u, :], square[u][:].rearrange("p (n g) -> p n g", g=8),
                                            axis=AX.X, op=ALU.add).then_inc(ss_done, 1)
                dve.wait_ge(ss_done, b * (UNITS_B + 1) + UNITS_B)
                nc.vector.tensor_scalar(ss[:], ss[:], 1e-12, None, ALU.max).then_inc(ss_done, 1)
                for half in range(2):
                    dve.wait_ge(v_ready, b * 2 + (half + 1))
                    dve.wait_ge(v_stored[half], (b + 1) * 16)
                    nc.vector.tensor_copy(vpad[half][:, :, :, 0:16], v_ps[half][:].rearrange("p (t h v) -> p t h v", t=CPT, v=16)) \
                        .then_inc(v_done, 1)
                dve.wait_ge(root_done, b + 1)
                nc.vector.reciprocal(root[:], root[:]).then_inc(step, 1)
                dve.wait_ge(step, b * 5 + 1)
                nc.vector.tensor_tensor(newton[:], root[:], root[:], ALU.mult).then_inc(step, 1)
                dve.wait_ge(step, b * 5 + 2)
                nc.vector.tensor_tensor(newton[:], newton[:], ss[:], ALU.mult).then_inc(step, 1)
                dve.wait_ge(step, b * 5 + 3)
                nc.vector.tensor_scalar(newton[:], newton[:], -0.5, 1.5, ALU.mult, ALU.add).then_inc(step, 1)
                dve.wait_ge(step, b * 5 + 4)
                nc.vector.tensor_tensor(root[:], root[:], newton[:], ALU.mult).then_inc(step, 1)
                dve.wait_ge(step, b * 5 + 5)
                for u in range(UNITS_B):
                    nc.vector.tensor_tensor(unit[u][:].rearrange("p (n g) -> p n g", g=8),
                                            nat_ps[u][:].rearrange("p (n g) -> p n g", g=8),
                                            root[:, u, :].unsqueeze(2).to_broadcast([P, groups, 8]),
                                            ALU.mult).then_inc(unit_done, 1)

                def value(n):
                    half, i = n // items, n % items
                    if i < 2:
                        dve.wait_ge(unitT_ready, b * UNITS_B + (2 * half + i + 1))
                    if i == 1:
                        ins = nc.vector.tensor_copy(val[n][:], turn_ps[1][:])
                    else:
                        ins = nc.vector.tensor_scalar(val[n][:], turn_ps[0][:], factors[:, i // 2:i // 2 + 1], None, ALU.mult)
                    ins.then_inc(val_done, 1)

                def remainder(n):
                    dve.wait_ge(hi_done, b * NB + (n + 1))
                    nc.vector.tensor_tensor(rem[n][:], val[n][:], parts[n][:, 0, :], ALU.subtract).then_inc(rem_done, 1)

                value(0)
                for n in range(NB):
                    if n + 1 < NB:
                        value(n + 1)
                    remainder(n)


def cosine_attention(nc, name, ql, qd, ks, vs, neg_lambda, ctx_nat, ident):
    S = 2 * KB
    NS = GROUPS * S
    with ExitStack() as ctx:
        def sb(n, shp, dt=FP32):
            return ctx.enter_context(nc.sbuf_tensor(f"{name}_{n}", shp, dt))

        def ps(n, shp):
            return ctx.enter_context(nc.psum_tensor(f"{name}_{n}", shp, FP32))

        def sem(n):
            return nc.alloc_semaphore(f"{name}_{n}")

        ops = [[sb(f"{n}{i}", [2 * MAP_ROWS, 2, T], BF16) for n in ("k_op", "qd_op", "q1_op", "q2_op")]
               for i in range(GROUPS)]
        v_op = [sb(f"v_op{i}", [P, KB, 64]) for i in range(GROUPS)]
        gate = [sb(f"gate{i}", [P, 2, CH]) for i in range(2)]
        probs = [[sb(f"probs{m}_{i}", [P, 2, CH]) for m in range(2)] for i in range(4)]
        o_sb = [sb(f"o_sb{i}", [P, CH]) for i in range(2)]
        rec = sb("rec", [P, CPT, 4])
        o_norm = sb("o_norm", [P, CPT, 4, 16])
        diff_ps = ps("diff_ps", [P, 2, CH])
        logit_ps = [ps(f"logit_ps{m}", [P, 2, CH]) for m in range(2)]
        o_ps, turn_ps = ps("o_ps", [P, CH]), ps("turn_ps", [P, CH])
        preset, late_preset = sem("preset"), sem("late_preset")
        op_loaded = [sem(f"op_loaded{i}") for i in range(GROUPS)]
        diff_ready, gate_done, exp_done, pv_done = sem("diff_ready"), sem("gate_done"), sem("exp_done"), sem("pv_done")
        logit_ready = [sem(f"logit_ready{m}") for m in range(2)]
        sum_done = [sem(f"sum_done{m}") for m in range(2)]
        o_copied, turned, turn_free, rec_done = sem("o_copied"), sem("turned"), sem("turn_free"), sem("rec_done")
        block = ctx.enter_context(nc.Block())

        def where(s):
            return s // S, s % S // KB, s % KB

        def behind(b, s, d):
            if s >= d:
                return (b, s - d) if s - d < NS else None
            return None if isinstance(b, int) and b == 0 else (b - 1, s - d + NS)

        DEPTH = 5

        n_loads = 2 * 3 * len(PAIR_PARTS) + 1

        @block.sync
        def _(sp):
            def load(b, g):
                k_op, qd_op, q1_op, q2_op = ops[g]
                for m in range(2):
                    for n, (qp, kp) in enumerate(PAIR_PARTS):
                        r0 = m * MAP_ROWS + n * 8
                        for op, dram, part in ((k_op, ks, kp), (qd_op, qd, qp), ((q1_op, q2_op)[m], ql, qp)):
                            src = dram[ds(b, 1), part, g * 32:(g + 1) * 32, :] \
                                .rearrange("a (j m r) t -> (a r) m j t", j=2, m=2)[:, m, :, :]
                            sp.dma_start(op[r0:r0 + 8, :, :], src).then_inc(op_loaded[g], 16)
                sp.dma_start(v_op[g][:], vs[ds(b, 1), :, :, g * 64:(g + 1) * 64]
                             .rearrange("a p k v -> (a p) k v")).then_inc(op_loaded[g], 16)

            for g in range(GROUPS):
                if g == 0:
                    sp.wait_ge(preset, 1)
                else:
                    sp.wait_ge(late_preset, g)
                load(0, g)
            with sp.Fori(0, BATCH - 1) as b:
                for g in range(GROUPS):
                    sp.wait_ge(pv_done, b * NS + (g + 1) * S)
                    load(b + 1, g)

        @block.gpsimd
        def _(pool):
            for g in range(1, GROUPS):
                nc.gpsimd.memset(ops[g][2][:], 0.0)
                nc.gpsimd.memset(ops[g][3][:], 0.0).then_inc(late_preset, 1)

        @block.tensor
        def _(te):
            te.sem_inc(gate_done, 1)
            te.sem_inc(sum_done[0], 1)
            te.sem_inc(sum_done[1], 1)
            te.sem_inc(o_copied, 1)
            te.sem_inc(turn_free, 1)

            def product(out, q, s):
                g, hq, kb = where(s)
                for j in range(2):
                    mm = nc.tensor.matmul(out[:, j, :], ops[g][0][:, j, kb * P:(kb + 1) * P],
                                          q[:, j, hq * CH:(hq + 1) * CH], start=True, stop=True)
                return mm

            def steps(b, todo):
                for s in todo:
                    if s < NS:
                        g, hq, kb = where(s)
                        if s % S == 0:
                            te.wait_ge(op_loaded[g], (b + 1) * (16 * n_loads))
                        te.wait_ge(gate_done, b * NS + (s + 1))
                        product(diff_ps, ops[g][1], s).then_inc(diff_ready, 1)
                        for m in range(2):
                            te.wait_ge(sum_done[m], b * NS + (s + 1))
                            product(logit_ps[m], ops[g][2 + m], s).then_inc(logit_ready[m], 1)
                    if behind(b, s, 2):
                        b2, s2 = behind(b, s, 2)
                        g, hq, kb = where(s2)
                        te.wait_ge(exp_done, (b2 * NS + (s2 + 1)) * 2)
                        if kb == 0:
                            te.wait_ge(o_copied, b2 * (2 * GROUPS) + (2 * g + hq + 1))
                        for j in range(2):
                            for m in range(2):
                                c0 = 32 * (2 * j + m)
                                mm = nc.tensor.matmul(o_ps[c0:c0 + 32, :], v_op[g][:, kb, j * 32:(j + 1) * 32],
                                                      probs[s2 % 4][m][:, j, :], start=kb == 0, stop=kb == KB - 1)
                        mm.then_inc(pv_done, 1)
                    if behind(b, s, 4) and (s - 4) % KB == KB - 1:
                        b4, s4 = behind(b, s, 4)
                        g, hq, kb = where(s4)
                        h = b4 * (2 * GROUPS) + (2 * g + hq)
                        te.wait_ge(o_copied, h + 2)
                        te.wait_ge(turn_free, h + 1)
                        for t in range(CPT):
                            mm = nc.tensor.transpose(turn_ps[:, t * P:(t + 1) * P], o_sb[hq][:, t * P:(t + 1) * P], ident[:])
                        mm.then_inc(turned, 1)

            steps(0, range(NS))
            with te.Fori(1, BATCH) as b:
                steps(b, range(NS))
            steps(BATCH - 1, range(NS, NS + DEPTH))

        @block.scalar
        def _(act):
            def steps(b, todo):
                for s in todo:
                    if s < NS:
                        act.wait_ge(diff_ready, b * NS + (s + 1))
                        nc.scalar.activation(gate[s % 2][:], diff_ps[:], ACT.Tanh).then_inc(gate_done, 1)
                    if behind(b, s, 1):
                        b1, s1 = behind(b, s, 1)
                        for m in range(2):
                            tile = probs[s1 % 4][m]
                            act.wait_ge(sum_done[m], b1 * NS + (s1 + 2))
                            nc.scalar.activation(tile[:], tile[:], ACT.Exp).then_inc(exp_done, 1)

            steps(0, range(NS))
            with act.Fori(1, BATCH) as b:
                steps(b, range(NS))
            steps(BATCH - 1, range(NS, NS + DEPTH))

        @block.vector
        def _(dve):
            nc.vector.memset(ops[0][2][:], 0.0)
            nc.vector.memset(ops[0][3][:], 0.0).then_inc(preset, 1)

            def steps(b, todo):
                for s in todo:
                    if behind(b, s, 5) and (s - 5) % KB == KB - 1:
                        b5, s5 = behind(b, s, 5)
                        g, hq, kb = where(s5)
                        h = b5 * (2 * GROUPS) + (2 * g + hq)
                        o = turn_ps[:].rearrange("p (t j v) -> p t j v", t=CPT, j=4)
                        dve.wait_ge(turned, h + 1)
                        nc.vector.reciprocal(rec[:], o[:, :, :, 16]).then_inc(rec_done, 1)
                        dve.wait_ge(rec_done, h * 2 + 1)
                        nc.vector.tensor_tensor(o_norm[:], o[:, :, :, 0:16], rec[:].unsqueeze(3)
                                                .to_broadcast([P, CPT, 4, 16]), ALU.mult).then_inc(rec_done, 1)
                        dve.wait_ge(rec_done, h * 2 + 2)
                        pair = o_norm[:].rearrange("p t (j m) d -> p t j m d", m=2)
                        out = (ctx_nat[:, ds(b5 * (KB * D) + hq * CH, CH)].rearrange("p (t f) -> p t f", f=D)
                               [:, :, g * 32:(g + 1) * 32].rearrange("p t (j d) -> p t j d", d=16))
                        nc.vector.scalar_tensor_tensor(out=out, in0=pair[:, :, :, 1, :], scalar=neg_lambda[:, 0:1],
                                                       in1=pair[:, :, :, 0, :], op0=ALU.mult, op1=ALU.add) \
                            .then_inc(turn_free, 1)
                    if behind(b, s, 3) and (s - 3) % KB == KB - 1:
                        b3, s3 = behind(b, s, 3)
                        hq = where(s3)[1]
                        dve.wait_ge(pv_done, b3 * NS + (s3 + 1))
                        nc.vector.tensor_copy(o_sb[hq][:], o_ps[:]).then_inc(o_copied, 1)
                    if s < NS:
                        dve.wait_ge(gate_done, b * NS + (s + 2))
                        for m, op in enumerate((ALU.add, ALU.subtract)):
                            dve.wait_ge(logit_ready[m], b * NS + (s + 1))
                            nc.vector.tensor_tensor(probs[s % 4][m][:], logit_ps[m][:], gate[s % 2][:], op) \
                                .then_inc(sum_done[m], 1)

            steps(0, range(NS))
            with dve.Fori(1, BATCH) as b:
                steps(b, range(NS))
            steps(BATCH - 1, range(NS, NS + DEPTH))


def route(nc, name, xn, w_router, n_experts, logits, ident):
    E = n_experts
    with ExitStack() as ctx:
        def sem(n):
            return nc.alloc_semaphore(f"{name}_{n}")

        w = ctx.enter_context(nc.sbuf_tensor(f"{name}_w", [P, E], FP32))
        xnT = [ctx.enter_context(nc.sbuf_tensor(f"{name}_xnT{i}", [P, CH], FP32)) for i in range(2)]
        t_ps = [ctx.enter_context(nc.psum_tensor(f"{name}_t_ps{i}", [P, CH], FP32)) for i in range(2)]
        l_ps = ctx.enter_context(nc.psum_tensor(f"{name}_l_ps", [P, TILES * E], FP32))
        loaded, turned, copied, l_ready = (sem(n) for n in ("loaded", "turned", "copied", "l_ready"))
        block = ctx.enter_context(nc.Block())

        @block.sync
        def _(sp):
            sp.dma_start(w[:], w_router).then_inc(loaded, 16)

        @block.tensor
        def _(te):
            def turn(c):
                if c >= 2:
                    te.wait_ge(copied, c - 1)
                for t in range(CPT):
                    col = (c * CPT + t) * D
                    mm = nc.tensor.transpose(t_ps[c % 2][:, t * P:(t + 1) * P], xn[:, col:col + D], ident[:])
                mm.then_inc(turned, 1)

            turn(0)
            te.wait_ge(loaded, 16)
            for c in range(CHUNKS):
                if c + 1 < CHUNKS:
                    turn(c + 1)
                te.wait_ge(copied, c + 1)
                for t in range(CPT):
                    col = (c * CPT + t) * E
                    mm = nc.tensor.matmul(l_ps[:, col:col + E], xnT[c % 2][:, t * P:(t + 1) * P], w[:], start=True, stop=True)
                mm.then_inc(l_ready, 1)

        @block.scalar
        def _(act):
            for c in range(CHUNKS):
                act.wait_ge(turned, c + 1)
                if c >= 2:
                    act.wait_ge(l_ready, c - 1)
                nc.scalar.activation(xnT[c % 2][:], t_ps[c % 2][:], ACT.Copy).then_inc(copied, 1)

        @block.vector
        def _(dve):
            dve.wait_ge(l_ready, CHUNKS)
            nc.vector.tensor_copy(logits[:], l_ps[:])


def wide(ap, n):
    return ap.unsqueeze(2).to_broadcast([P, TILES, n])


def first_of_max(nc, then, out, v, best, descending, E):
    then(nc.vector.tensor_reduce(best[:], v, axis=AX.X, op=ALU.max))
    then(nc.vector.tensor_tensor(out[:], v, wide(best[:], E), ALU.is_equal))
    then(nc.vector.tensor_tensor(out[:], out[:], descending[:].unsqueeze(1).to_broadcast([P, TILES, E]), ALU.mult))
    then(nc.vector.tensor_reduce(best[:], out[:], axis=AX.X, op=ALU.max))
    then(nc.vector.tensor_tensor(out[:], out[:], wide(best[:], E), ALU.is_equal))


def top2_coefficients(nc, name, logits, descending, parts):
    E = 16
    with ExitStack() as ctx:
        def sb(n, shp, dt=FP32):
            return ctx.enter_context(nc.sbuf_tensor(f"{name}_{n}", shp, dt))

        prob, first, second = sb("prob", [P, TILES, E]), sb("first", [P, TILES, E]), sb("second", [P, TILES, E])
        best = sb("best", [P, TILES])
        step = nc.alloc_semaphore(f"{name}_step")
        exp_done = nc.alloc_semaphore(f"{name}_exp_done")
        block = ctx.enter_context(nc.Block())

        @block.scalar
        def _(act):
            act.wait_ge(step, 3)
            nc.scalar.activation(prob[:], prob[:], ACT.Exp).then_inc(exp_done, 1)

        @block.vector
        def _(dve):
            count = [0]

            def then(ins):
                count[0] += 1
                ins.then_inc(step, 1)
                dve.wait_ge(step, count[0])

            l = logits[:].rearrange("p (t e) -> p t e", e=E)
            then(nc.vector.memset(parts[:], 0.0))
            then(nc.vector.tensor_reduce(best[:], l, axis=AX.X, op=ALU.max))
            then(nc.vector.tensor_tensor(prob[:], l, wide(best[:], E), ALU.subtract))
            dve.wait_ge(exp_done, 1)
            then(nc.vector.tensor_reduce(best[:], prob[:], axis=AX.X, op=ALU.add))
            then(nc.vector.reciprocal(best[:], best[:]))
            then(nc.vector.tensor_tensor(prob[:], prob[:], wide(best[:], E), ALU.mult))
            first_of_max(nc, then, first, prob[:], best, descending, E)
            then(nc.vector.scalar_tensor_tensor(out=first[:], in0=first[:], scalar=-4.0, in1=prob[:],
                                                op0=ALU.mult, op1=ALU.add))
            first_of_max(nc, then, second, first[:], best, descending, E)
            then(nc.vector.tensor_scalar(first[:], first[:], 0.0, None, ALU.is_lt))
            then(nc.vector.tensor_tensor(second[:], second[:], first[:], ALU.add))
            then(nc.vector.tensor_tensor(prob[:], prob[:], second[:], ALU.mult))
            for i in range(3):
                then(nc.vector.tensor_copy(parts[:, :, 32 * i:32 * i + E], prob[:]))
                if i < 2:
                    then(nc.vector.tensor_tensor(prob[:], prob[:], parts[:, :, 32 * i:32 * i + E], ALU.subtract))


def soft_experts(nc, name, x, mv, rstd, gate_w, up_w, down_w, s_gate, s_up, s_down, coef, select, ident):
    PAIRS_ = 8
    ITEMS = PAIRS_ + 1
    TURN, BACK = 3, 1
    with ExitStack() as ctx:
        def sb(n, shp, dt=FP32):
            return ctx.enter_context(nc.sbuf_tensor(f"{name}_{n}", shp, dt))

        def ps(n, dt=FP32):
            return ctx.enter_context(nc.psum_tensor(f"{name}_{n}", [P, CH], dt))

        def sem(n):
            return nc.alloc_semaphore(f"{name}_{n}")

        g_w, u_w, d_w = sb("g_w", [P, ITEMS, P]), sb("u_w", [P, ITEMS, P]), sb("d_w", [P, ITEMS, D])
        sel = sb("sel", [96, PAIRS_, P], BF16)
        ident_bf = sb("ident_bf", [P, P], BF16)
        xn = [sb(f"xn{i}", [P, CH]) for i in range(2)]
        xnT = [sb(f"xnT{i}", [P, CH]) for i in range(2)]
        coefT = [sb(f"coefT{i}", [96, CH], BF16) for i in range(2)]
        silu = [sb(f"silu{i}", [P, CH]) for i in range(2)]
        product = sb("product", [P, CH])
        inter = [sb(f"inter{i}", [P, CH]) for i in range(2)]
        yT = sb("yT", [P, CH])
        t_ps, c_ps, y_ps, ct_ps = ps("t_ps"), ps("c_ps"), ps("y_ps"), ps("ct_ps", BF16)
        g_ps = [ps(f"g_ps{i}") for i in range(2)]
        u_ps = [ps(f"u_ps{i}") for i in range(2)]
        (loaded, xn_done, turned, xT_done, ct_ready, ct_done, g_ready, uc_ready, silu_done, product_done, inter_done,
         down_done, y_ready, y_copied, back, added) = (sem(n) for n in (
             "loaded", "xn_done", "turned", "xT_done", "ct_ready", "ct_done", "g_ready", "uc_ready", "silu_done",
             "product_done", "inter_done", "down_done", "y_ready", "y_copied", "back", "added"))
        block = ctx.enter_context(nc.Block())

        @block.sync
        def _(sp):
            for w, dram, shared in ((g_w, gate_w, s_gate), (u_w, up_w, s_up)):
                sp.dma_start(w[:, 0:PAIRS_, :].rearrange("c n (e f) -> c (n e) f", f=64),
                             dram.rearrange("e c f -> c e f")).then_inc(loaded, 16)
                sp.dma_start(w[:, PAIRS_, :], shared).then_inc(loaded, 16)
            sp.dma_start(d_w[:, 0:PAIRS_, :], down_w.rearrange("(n e) f d -> (e f) n d", e=2)).then_inc(loaded, 16)
            sp.dma_start(d_w[:, PAIRS_, :], s_down).then_inc(loaded, 16)
            sp.dma_start(sel[:], select[0]).then_inc(loaded, 16)
            sp.dma_start(ident_bf[:], select[1]).then_inc(loaded, 16)

        @block.tensor
        def _(te):
            te.wait_ge(loaded, 16 * 8)
            te.sem_inc(silu_done, 2)
            te.sem_inc(inter_done, 2)
            te.sem_inc(added, 1)
            te.sem_inc(y_copied, 1)
            te.sem_inc(back, 1)
            with te.Fori(0, BATCH) as b:
                def turn(half):
                    c = b * 2 + half
                    if half == 0:
                        te.wait_ge(added, c + 1)
                    te.wait_ge(xn_done, c + 1)
                    for t in range(CPT):
                        mm = nc.tensor.transpose(t_ps[:, t * P:(t + 1) * P], xn[half][:, t * P:(t + 1) * P], ident[:])
                    mm.then_inc(turned, 1)
                    for t in range(CPT):
                        mm = nc.tensor.transpose(ct_ps[0:96, t * P:(t + 1) * P],
                                                 coef[:].rearrange("p t n -> p (t n)")[:, ds((b * KB + half * CPT + t) * 96, 96)],
                                                 ident_bf[:])
                    mm.then_inc(ct_ready, 1)

                def turn_back(half):
                    c = b * 2 + half
                    te.wait_ge(y_copied, c + 2)
                    if half == 1:
                        te.wait_ge(added, c + 1)
                    for t in range(CPT):
                        mm = nc.tensor.transpose(t_ps[:, t * P:(t + 1) * P], yT[:, t * P:(t + 1) * P], ident[:])
                    mm.then_inc(back, 1)

                turn(0)
                for half in range(2):
                    c = b * 2 + half
                    te.wait_ge(xT_done, c + 1)
                    te.wait_ge(ct_done, c + 1)

                    def down(i):
                        te.wait_ge(inter_done, c * ITEMS + (i + 3))
                        if i == 0:
                            te.wait_ge(y_copied, c + 1)
                        nc.tensor.matmul(y_ps[:], d_w[:, i, :], inter[(half + i) % 2][:],
                                         start=i == 0, stop=i == ITEMS - 1).then_inc(down_done, 1)

                    for i in range(ITEMS):
                        k = c * ITEMS + i
                        j = (half + i) % 2
                        te.wait_ge(silu_done, k + 1)
                        nc.tensor.matmul(g_ps[j][:], g_w[:, i, :], xnT[half][:], start=True, stop=True).then_inc(g_ready, 1)
                        te.wait_ge(inter_done, k + 1)
                        mm = nc.tensor.matmul(u_ps[j][:], u_w[:, i, :], xnT[half][:], start=True, stop=True)
                        if i < PAIRS_:
                            te.wait_ge(inter_done, k + 2)
                            mm = nc.tensor.matmul(c_ps[:], sel[:, i, :], coefT[half][:], start=True, stop=True)
                        mm.then_inc(uc_ready, 1)
                        if i > 0:
                            down(i - 1)
                        if half == 0 and i == TURN:
                            turn(1)
                        if half == 1 and i == BACK:
                            turn_back(0)
                    down(ITEMS - 1)
                turn_back(1)

        @block.scalar
        def _(act):
            with act.Fori(0, BATCH) as b:
                def take(half):
                    act.wait_ge(turned, b * 2 + (half + 1))
                    nc.scalar.activation(xnT[half][:], t_ps[:], ACT.Copy).then_inc(xT_done, 1)
                    act.wait_ge(ct_ready, b * 2 + (half + 1))
                    nc.scalar.activation(coefT[half][:], ct_ps[0:96, :], ACT.Copy).then_inc(ct_done, 1)

                take(0)
                for half in range(2):
                    c = b * 2 + half
                    for i in range(ITEMS):
                        k = c * ITEMS + i
                        act.wait_ge(g_ready, k + 1)
                        act.wait_ge(inter_done, k + 1)
                        nc.scalar.activation(silu[(half + i) % 2][:], g_ps[(half + i) % 2][:], ACT.Silu).then_inc(silu_done, 1)
                        if half == 0 and i == TURN:
                            take(1)
                    act.wait_ge(down_done, (c + 1) * ITEMS + 2)
                    act.wait_ge(back, c + 1)
                    nc.scalar.activation(yT[:], y_ps[:], ACT.Copy).then_inc(y_copied, 1)

        @block.vector
        def _(dve):
            dve.sem_inc(down_done, 2)
            with dve.Fori(0, BATCH) as b:
                for half in range(2):
                    apply_norm(nc, xn[half], x, mv, rstd, b * KB + half * CPT).then_inc(xn_done, 1)

                def add(half):
                    dve.wait_ge(back, b * 2 + (half + 2))
                    rows = x[:, ds(b * (KB * D) + half * CH, CH)]
                    nc.vector.tensor_tensor(rows, rows, t_ps[:], ALU.add).then_inc(added, 1)

                for half in range(2):
                    c = b * 2 + half
                    for i in range(ITEMS):
                        k = c * ITEMS + i
                        j = (half + i) % 2
                        dve.wait_ge(silu_done, k + 3)
                        dve.wait_ge(uc_ready, k + 1)
                        if i < PAIRS_:
                            dve.wait_ge(inter_done, k + 2)
                            nc.vector.tensor_tensor(product[:], silu[j][:], u_ps[j][:], ALU.mult).then_inc(product_done, 1)
                            dve.wait_ge(product_done, c * PAIRS_ + (i + 1))
                            dve.wait_ge(down_done, k + 1)
                            nc.vector.tensor_tensor(inter[j][:], product[:], c_ps[:], ALU.mult).then_inc(inter_done, 1)
                        else:
                            dve.wait_ge(down_done, k + 1)
                            nc.vector.tensor_tensor(inter[j][:], silu[j][:], u_ps[j][:], ALU.mult).then_inc(inter_done, 1)
                        if half == 1 and i == BACK:
                            add(0)
                add(1)


def channel_mix(nc, name, x, mv, rstd, w_r, w_k, w_v, mu, ident):
    with ExitStack() as ctx:
        def sb(n, shp):
            return ctx.enter_context(nc.sbuf_tensor(f"{name}_{n}", shp, FP32))

        def ps(n):
            return ctx.enter_context(nc.psum_tensor(f"{name}_{n}", [P, CH], FP32))

        def sem(n):
            return nc.alloc_semaphore(f"{name}_{n}")

        w = [sb(f"w{i}", [P, D]) for i in range(3)]
        mu_sb, rest = sb("mu_sb", [P, 2]), sb("rest", [P, 2])
        xn = [sb(f"xn{i}", [P, CH]) for i in range(2)]
        xnT = sb("xnT", [P, T + 1])
        before = [sb(f"before{i}", [P, CH]) for i in range(2)]
        mixed = [[sb(f"mixed{h}{i}", [P, CH]) for i in range(2)] for h in range(2)]
        relu = [sb(f"relu{i}", [P, CH]) for i in range(2)]
        kact = [sb(f"kact{i}", [P, CH]) for i in range(2)]
        r_sb = [sb(f"r_sb{i}", [P, CH]) for i in range(2)]
        gated = sb("gated", [P, CH])
        t_ps, r_ps, k_ps, o_ps = ([ps(f"{n}{i}") for i in range(2)] for n in ("t_ps", "r_ps", "k_ps", "o_ps"))
        (loaded, ready, xn_done, turned, xT_done, before_done, mixed_done, r_ready, k_ready, relu_done, kact_done, r_done,
         o_ready, gated_done, added) = (sem(n) for n in (
             "loaded", "ready", "xn_done", "turned", "xT_done", "before_done", "mixed_done", "r_ready", "k_ready",
             "relu_done", "kact_done", "r_done", "o_ready", "gated_done", "added"))
        block = ctx.enter_context(nc.Block())

        @block.sync
        def _(sp):
            for sb_, dram in zip(w, (w_r, w_k, w_v)):
                sp.dma_start(sb_[:], dram).then_inc(loaded, 16)
            sp.dma_start(mu_sb[:], mu).then_inc(loaded, 16)

        @block.tensor
        def _(te):
            te.wait_ge(loaded, 64)
            with te.Fori(0, BATCH) as b:
                te.wait_ge(added, b * 2 + 1)
                for h in range(2):
                    te.wait_ge(xn_done, b * 2 + (h + 1))
                    for t in range(CPT):
                        mm = nc.tensor.transpose(t_ps[h][:, t * P:(t + 1) * P], xn[h][:, t * P:(t + 1) * P], ident[:])
                    mm.then_inc(turned, 1)
                for h in range(2):
                    c = b * 2 + h
                    te.wait_ge(mixed_done, c * 2 + 2)
                    nc.tensor.matmul(k_ps[h][:], w[1][:], mixed[h][1][:], start=True, stop=True).then_inc(k_ready, 1)
                    for t in range(CPT):
                        mm = nc.tensor.matmul(r_ps[h][:, t * D:(t + 1) * D], mixed[h][0][:, t * P:(t + 1) * P], w[0][:],
                                              start=True, stop=True)
                    mm.then_inc(r_ready, 1)
                for h in range(2):
                    te.wait_ge(kact_done, b * 2 + (h + 1))
                    for t in range(CPT):
                        mm = nc.tensor.matmul(o_ps[h][:, t * D:(t + 1) * D], kact[h][:, t * P:(t + 1) * P], w[2][:],
                                              start=True, stop=True)
                    mm.then_inc(o_ready, 1)

        @block.scalar
        def _(act):
            act.wait_ge(ready, 2)
            with act.Fori(0, BATCH) as b:
                for h in range(2):
                    act.wait_ge(turned, b * 2 + (h + 1))
                    nc.scalar.activation(xnT[:, 1 + h * CH:1 + (h + 1) * CH], t_ps[h][:], ACT.Copy).then_inc(xT_done, 1)
                for h in range(2):
                    act.wait_ge(k_ready, b * 2 + (h + 1))
                    nc.scalar.activation(relu[h][:], k_ps[h][:], ACT.Relu).then_inc(relu_done, 1)
                    act.wait_ge(r_ready, b * 2 + (h + 1))
                    nc.scalar.activation(r_sb[h][:], r_ps[h][:], ACT.Sigmoid).then_inc(r_done, 1)

        @block.gpsimd
        def _(pool):
            with pool.Fori(0, BATCH) as b:
                for h in range(2):
                    pool.wait_ge(relu_done, b * 2 + (h + 1))
                    nc.gpsimd.tensor_tensor(kact[h][:], relu[h][:], relu[h][:], ALU.mult).then_inc(kact_done, 1)

        @block.vector
        def _(dve):
            dve.sem_inc(added, 1)
            nc.vector.memset(xnT[:, 0:1], 0.0).then_inc(ready, 1)
            dve.wait_ge(loaded, 64)
            nc.vector.tensor_scalar(rest[:], mu_sb[:], -1.0, 1.0, ALU.mult, ALU.add).then_inc(ready, 1)
            dve.wait_ge(ready, 2)
            with dve.Fori(0, BATCH) as b:
                for h in range(2):
                    apply_norm(nc, xn[h], x, mv, rstd, b * KB + h * CPT).then_inc(xn_done, 1)
                for h in range(2):
                    c = b * 2 + h
                    dve.wait_ge(xT_done, c + 1)
                    for i in range(2):
                        nc.vector.tensor_scalar(before[i][:], xnT[:, h * CH:(h + 1) * CH], rest[:, i:i + 1], None,
                                                ALU.mult).then_inc(before_done, 1)
                    for i in range(2):
                        dve.wait_ge(before_done, c * 2 + (i + 1))
                        nc.vector.scalar_tensor_tensor(out=mixed[h][i][:], in0=xnT[:, 1 + h * CH:1 + (h + 1) * CH],
                                                       scalar=mu_sb[:, i:i + 1], in1=before[i][:],
                                                       op0=ALU.mult, op1=ALU.add).then_inc(mixed_done, 1)
                    dve.wait_ge(mixed_done, c * 2 + 2)
                for h in range(2):
                    c = b * 2 + h
                    dve.wait_ge(r_done, c + 1)
                    dve.wait_ge(o_ready, c + 1)
                    nc.vector.tensor_tensor(gated[:], r_sb[h][:], o_ps[h][:], ALU.mult).then_inc(gated_done, 1)
                    dve.wait_ge(gated_done, c + 1)
                    rows = x[:, ds(b * (KB * D) + h * CH, CH)]
                    nc.vector.tensor_tensor(rows, rows, gated[:], ALU.add).then_inc(added, 1)
                    dve.wait_ge(added, c + 2)


EXPERTS = 8
CAP = TOK // EXPERTS
HID = 512


def assign_slots(nc, name, logits, descending, before_me, gate, slot_in, slot_out):
    E = EXPERTS
    with ExitStack() as ctx:
        def sb(n, shp, dt=FP32):
            return ctx.enter_context(nc.sbuf_tensor(f"{name}_{n}", shp, dt))

        shifted, hot, rank = sb("shifted", [P, TILES, E]), sb("hot", [P, TILES, E]), sb("rank", [P, TILES, E])
        hot_bf = sb("hot_bf", [P, TILES, E], BF16)
        sums = [sb(f"sums{i}", [P, TILES, E]) for i in range(2)]
        best, expert, pos, keep, slot = (sb(n, [P, TILES]) for n in ("best", "expert", "pos", "keep", "slot"))
        before = sb("before", [P, 2, P], BF16)
        loaded = nc.alloc_semaphore(f"{name}_loaded")
        in_ps = ctx.enter_context(nc.psum_tensor(f"{name}_in_ps", [P, TILES, E], FP32))
        all_ps = ctx.enter_context(nc.psum_tensor(f"{name}_all_ps", [P, TILES, E], FP32))
        step, exp_done, counted = (nc.alloc_semaphore(f"{name}_{n}") for n in ("step", "exp_done", "counted"))
        block = ctx.enter_context(nc.Block())

        @block.sync
        def _(sp):
            sp.dma_start(before[:], before_me).then_inc(loaded, 16)

        @block.scalar
        def _(act):
            act.wait_ge(step, 2)
            nc.scalar.activation(shifted[:], shifted[:], ACT.Exp).then_inc(exp_done, 1)

        @block.tensor
        def _(te):
            te.wait_ge(loaded, 16)
            te.wait_ge(exp_done, 2)
            flat = hot_bf[:].rearrange("p t e -> p (t e)")
            nc.tensor.matmul(in_ps[:].rearrange("p t e -> p (t e)"), before[:, 0, :], flat, start=True, stop=True)
            nc.tensor.matmul(all_ps[:].rearrange("p t e -> p (t e)"), before[:, 1, :], flat, start=True, stop=True) \
                .then_inc(counted, 1)

        @block.vector
        def _(dve):
            count = [0]

            def then(ins):
                count[0] += 1
                ins.then_inc(step, 1)
                dve.wait_ge(step, count[0])

            l = logits[:].rearrange("p (t e) -> p t e", e=E)
            then(nc.vector.tensor_reduce(best[:], l, axis=AX.X, op=ALU.max))
            then(nc.vector.tensor_tensor(shifted[:], l, wide(best[:], E), ALU.subtract))
            dve.wait_ge(exp_done, 1)
            then(nc.vector.tensor_reduce(best[:], shifted[:], axis=AX.X, op=ALU.add))
            then(nc.vector.reciprocal(gate[:], best[:]))
            first_of_max(nc, then, hot, l, best, descending, E)
            then(nc.vector.tensor_copy(hot_bf[:], hot[:]))
            dve.sem_inc(exp_done, 1)
            then(nc.vector.tensor_scalar(expert[:], best[:], -1.0, float(E), ALU.mult, ALU.add))
            dve.wait_ge(counted, 1)
            then(nc.vector.tensor_copy(sums[0][:], all_ps[:]))
            a, d = 0, 1
            while d < TILES:
                then(nc.vector.tensor_copy(sums[1 - a][:, 0:d, :], sums[a][:, 0:d, :]))
                then(nc.vector.tensor_tensor(sums[1 - a][:, d:, :], sums[a][:, d:, :], sums[a][:, 0:TILES - d, :], ALU.add))
                a, d = 1 - a, d * 2
            then(nc.vector.tensor_tensor(rank[:], sums[a][:], all_ps[:], ALU.subtract))
            then(nc.vector.tensor_tensor(rank[:], rank[:], in_ps[:], ALU.add))
            then(nc.vector.tensor_tensor(rank[:], rank[:], hot[:], ALU.mult))
            then(nc.vector.tensor_reduce(pos[:], rank[:], axis=AX.X, op=ALU.add))
            then(nc.vector.tensor_scalar(keep[:], pos[:], float(CAP), None, ALU.is_lt))
            then(nc.vector.scalar_tensor_tensor(out=slot[:], in0=expert[:], scalar=float(CAP), in1=pos[:],
                                                op0=ALU.mult, op1=ALU.add))
            then(nc.vector.tensor_tensor(gate[:], gate[:], keep[:], ALU.mult))
            then(nc.vector.tensor_tensor(slot[:], slot[:], keep[:], ALU.mult))
            then(nc.vector.tensor_copy(slot_out[:], slot[:]))
            then(nc.vector.tensor_scalar(keep[:], keep[:], -2.0 * TOK, 2.0 * TOK, ALU.mult, ALU.add))
            then(nc.vector.tensor_tensor(slot[:], slot[:], keep[:], ALU.add))
            then(nc.vector.tensor_copy(slot_in[:], slot[:]))


def dispatch(nc, name, xn, slot_in, slots):
    with ExitStack() as ctx:
        sent = nc.alloc_semaphore(f"{name}_sent")
        block = ctx.enter_context(nc.Block())

        @block.gpsimd
        def _(pool):
            for t in range(TILES):
                nc.gpsimd.indirect_dma_start(out=slots, out_offset=bass.IndirectOffsetOnAxis(ap=slot_in[:, t:t + 1], axis=0),
                                             in_=xn[:, t * D:(t + 1) * D], in_offset=None,
                                             bounds_check=TOK - 1, oob_is_err=False).then_inc(sent, 16)
            pool.wait_ge(sent, 16 * TILES)


def slot_experts(nc, name, slots, w1, w2, biases, results, ident):
    FB = HID // P
    with ExitStack() as ctx:
        def sb(n, shp):
            return ctx.enter_context(nc.sbuf_tensor(f"{name}_{n}", shp, FP32))

        def ps(n):
            return ctx.enter_context(nc.psum_tensor(f"{name}_{n}", [P, CH], FP32))

        def sem(n):
            return nc.alloc_semaphore(f"{name}_{n}")

        w1_sb = [sb(f"w1_sb{i}", [P, HID]) for i in range(2)]
        w2_sb = [sb(f"w2_sb{i}", [P, FB, D]) for i in range(2)]
        b_sb = [sb(f"b_sb{i}", [P, FB + 1]) for i in range(2)]
        rows = [sb(f"rows{i}", [P, CPT, D]) for i in range(2)]
        rowsT = [sb(f"rowsT{i}", [P, CH]) for i in range(2)]
        hid = [sb(f"hid{i}", [P, FB, CH]) for i in range(2)]
        yT = [sb(f"yT{i}", [P, CH]) for i in range(2)]
        out = [sb(f"out{i}", [P, CPT, D]) for i in range(2)]
        t_ps, y_ps, back_ps = ps("t_ps"), ps("y_ps"), ps("back_ps")
        h_ps = [ps(f"h_ps{i}") for i in range(FB)]
        loaded = [sem(f"loaded{i}") for i in range(2)]
        stored, drained = sem("stored"), sem("drained")
        turned, turn_copied, h_ready, h_done, y_ready, y_done, back, out_done = (
            sem(n) for n in ("turned", "turn_copied", "h_ready", "h_done", "y_ready", "y_done", "back", "out_done"))
        n_loads = 3 + (biases is not None)
        block = ctx.enter_context(nc.Block())

        @block.sync
        def _(sp):
            with sp.Fori(0, EXPERTS // 2) as pair:
                for i in range(2):
                    e = pair * 2 + i
                    sp.wait_ge(y_done, e + 1)
                    sp.dma_start(rows[i][:], slots[ds(e * CAP, CAP), :].rearrange("(n p) d -> p n d", p=P)).then_inc(loaded[i], 16)
                    sp.dma_start(w1_sb[i][:], w1[ds(e, 1), :, :].rearrange("a c f -> (a c) f")).then_inc(loaded[i], 16)
                    sp.dma_start(w2_sb[i][:], w2[ds(e, 1), :, :].rearrange("a (n p) d -> (a p) n d", p=P)).then_inc(loaded[i], 16)
                    if biases is not None:
                        sp.dma_start(b_sb[i][:], biases[ds(e, 1), :, :].rearrange("a p n -> (a p) n")).then_inc(loaded[i], 16)

        @block.gpsimd
        def _(pool):
            with pool.Fori(0, EXPERTS // 2) as pair:
                for i in range(2):
                    e = pair * 2 + i
                    pool.wait_ge(out_done, e + 2)
                    pool.dma_start(results[ds(e * CAP, CAP), :].rearrange("(n p) d -> p n d", p=P), out[i][:]).then_inc(stored, 16)
                    pool.wait_ge(stored, e * 16 + 16)
                    pool.sem_inc(drained, 1)

        @block.tensor
        def _(te):
            te.sem_inc(turn_copied, 1)
            te.sem_inc(h_done, FB)
            te.sem_inc(y_done, 2)
            te.sem_inc(out_done, 1)
            with te.Fori(0, EXPERTS // 2) as pair:
                for i in range(2):
                    e = pair * 2 + i
                    te.wait_ge(loaded[i], (pair + 1) * (16 * n_loads))
                    te.wait_ge(turn_copied, e + 1)
                    for t in range(CPT):
                        mm = nc.tensor.transpose(t_ps[:, t * P:(t + 1) * P], rows[i][:, t, :], ident[:])
                    mm.then_inc(turned, 1)
                    te.wait_ge(turn_copied, e + 2)
                    for f in range(FB):
                        te.wait_ge(h_done, e * FB + (f + 1))
                        nc.tensor.matmul(h_ps[f][:], w1_sb[i][:, f * P:(f + 1) * P], rowsT[i][:],
                                         start=True, stop=True).then_inc(h_ready, 1)
                    te.wait_ge(y_done, e + 2)
                    for f in range(FB):
                        te.wait_ge(h_done, e * FB + (f + 1 + FB))
                        mm = nc.tensor.matmul(y_ps[:], w2_sb[i][:, f, :], hid[i][:, f, :], start=f == 0, stop=f == FB - 1)
                    mm.then_inc(y_ready, 1)
                    te.wait_ge(y_done, e + 3)
                    te.wait_ge(out_done, e + 1)
                    for t in range(CPT):
                        mm = nc.tensor.transpose(back_ps[:, t * P:(t + 1) * P], yT[i][:, t * P:(t + 1) * P], ident[:])
                    mm.then_inc(back, 1)

        @block.scalar
        def _(act):
            with act.Fori(0, EXPERTS // 2) as pair:
                for i in range(2):
                    e = pair * 2 + i
                    act.wait_ge(turned, e + 1)
                    nc.scalar.activation(rowsT[i][:], t_ps[:], ACT.Copy).then_inc(turn_copied, 1)
                    for f in range(FB):
                        act.wait_ge(h_ready, e * FB + (f + 1))
                        if biases is None:
                            nc.scalar.activation(hid[i][:, f, :], h_ps[f][:], ACT.Relu).then_inc(h_done, 1)
                        else:
                            nc.scalar.activation(hid[i][:, f, :], h_ps[f][:], ACT.Relu, bias=b_sb[i][:, f:f + 1]).then_inc(h_done, 1)

        @block.vector
        def _(dve):
            dve.sem_inc(drained, 2)
            with dve.Fori(0, EXPERTS // 2) as pair:
                for i in range(2):
                    e = pair * 2 + i
                    dve.wait_ge(y_ready, e + 1)
                    if biases is None:
                        nc.vector.tensor_copy(yT[i][:], y_ps[:]).then_inc(y_done, 1)
                    else:
                        nc.vector.tensor_scalar(yT[i][:], y_ps[:], b_sb[i][:, FB:FB + 1], None, ALU.add).then_inc(y_done, 1)
                    dve.wait_ge(drained, e + 1)
                    dve.wait_ge(back, e + 1)
                    nc.vector.tensor_copy(out[i][:].rearrange("p n d -> p (n d)"), back_ps[:]).then_inc(out_done, 1)


def combine(nc, name, x, results, slot_out, gate, stats):
    with ExitStack() as ctx:
        y = ctx.enter_context(nc.sbuf_tensor(f"{name}_y", [P, TILES * D], FP32))
        fetched = [nc.alloc_semaphore(f"{name}_fetched{b}") for b in range(BATCH)]
        added = nc.alloc_semaphore(f"{name}_added")
        block = ctx.enter_context(nc.Block())

        @block.gpsimd
        def _(pool):
            for t in range(TILES):
                nc.gpsimd.indirect_dma_start(out=y[:, t * D:(t + 1) * D], out_offset=None, in_=results,
                                             in_offset=bass.IndirectOffsetOnAxis(ap=slot_out[:, t:t + 1], axis=0)) \
                    .then_inc(fetched[t // KB], 16)

        @block.vector
        def _(dve):
            for t in range(TILES):
                if t % KB == 0:
                    dve.wait_ge(fetched[t // KB], 16 * KB)
                rows = x[:, t * D:(t + 1) * D]
                nc.vector.scalar_tensor_tensor(out=rows, in0=y[:, t * D:(t + 1) * D], scalar=gate[:, t:t + 1], in1=rows,
                                               op0=ALU.mult, op1=ALU.add).then_inc(added, 1)
                if t % KB == KB - 1 and stats is not None:
                    dve.wait_ge(added, t + 1)
                    for u in range(t + 1 - KB, t + 1):
                        tile_stats(nc, stats, x, u)


def four_layers(nc, a, out):
    with ExitStack() as ctx:
        def sb(n, shp, dt=FP32):
            return ctx.enter_context(nc.sbuf_tensor(n, shp, dt))

        def dram(n, shp, dt):
            return nc.dram_tensor(n, shp, dt, kind="Internal").ap()

        x = sb("x_sb", [P, TILES * D])
        mv, rstd, stats = sb("mv", [P, TILES, 2]), sb("rstd", [P, TILES]), sb("stats", [P, TILES * 6])
        consts = {n: sb(n + "_sb", [P, P], FP32 if n == "ident" else BF16)
                  for n in ("ident", "ident_bf", "mask_a", "mask_b", "one_stat")}
        descending = {n: sb(f"descending{n}", [P, n]) for n in (16, EXPERTS)}
        consts["zero_rows"], consts["one_rows"] = a["zero_rows"], a["one_rows"]
        ident = consts["ident"]
        scratch = [dram(f"scratch_{n}", [BATCH, 3, D, T], BF16) for n in ("q", "k", "g")]
        scratch_v = dram("scratch_v", [BATCH, P, KB, 512], FP32)
        scratch_v2 = dram("scratch_v2", [BATCH, P, KB, 256], FP32)
        wide_q, wide_k = (dram(f"wide_{n}", [BATCH, 3, 512, T], BF16) for n in ("q", "k"))
        wide_v = dram("wide_v", [BATCH, P, KB, 512], FP32)
        slots = [dram(f"slots{i}", [TOK, D], FP32) for i in range(2)]
        results = [dram(f"results{i}", [TOK, D], FP32) for i in range(2)]
        loaded, zeroed, filled, sent = (nc.alloc_semaphore(n) for n in ("x_loaded", "zeroed", "filled", "sent"))

        with nc.Block() as block:
            @block.sync
            def _(sp):
                sp.dma_start(x[:].rearrange("p (n d) -> p n d", d=D), a["x"].rearrange("(n p) d -> p n d", p=P)).then_inc(loaded, 16)
                for n in ("ident", "ident_bf", "mask_a", "mask_b", "one_stat"):
                    sp.dma_start(consts[n][:], a[n]).then_inc(loaded, 16)
                for n, t in descending.items():
                    sp.dma_start(t[:], a["descending"][:, 16 - n:16].to_broadcast([P, n])).then_inc(loaded, 16)
                sp.wait_ge(loaded, 16 * 8)

        def maxed(name, shape, feats, q, k, v, floor, wo, bias):
            with nc.sbuf_tensor(name + "_nat", [P, TILES * feats], FP32) as nat:
                attention(nc, name, shape, shape.hd ** -0.5, q, k, v, nat, consts, floor)
                out_project(nc, name + "o", nat, feats, wo, x, stats, consts, bias)

        def moe(name, i, w_router, w1, w2, biases):
            with ExitStack() as inner:
                def sbi(n, shp, dt=FP32):
                    return inner.enter_context(nc.sbuf_tensor(f"{name}_{n}", shp, dt))

                xn, logits = sbi("xn", [P, TILES * D]), sbi("logits", [P, TILES * EXPERTS])
                gate, slot_in, slot_out = sbi("gate", [P, TILES]), sbi("slot_in", [P, TILES], U32), sbi("slot_out", [P, TILES], U32)
                layer_stats(nc, name + "n", x, mv, rstd, dst=xn, stats=stats)
                route(nc, name + "r", xn, w_router, EXPERTS, logits, ident)
                assign_slots(nc, name + "a", logits, descending[EXPERTS], a["before_me"], gate, slot_in, slot_out)
                dispatch(nc, name + "d", xn, slot_in, slots[i])
                slot_experts(nc, name + "e", slots[i], w1, w2, biases, results[i], ident)
                combine(nc, name + "c", x, results[i], slot_out, gate, stats if i == 0 else None)

        with cleared_semaphores(nc):
            with nc.sbuf_tensor("zero_slots", [P, TILES * D], FP32) as zeros:
                with nc.Block() as block:
                    @block.gpsimd
                    def _(pool):
                        nc.gpsimd.memset(zeros[:], 0.0).then_inc(zeroed, 1)

                    @block.sync
                    def _(sp):
                        sp.wait_ge(zeroed, 1)
                        for s in slots:
                            sp.dma_start(s.rearrange("(p n) d -> p (n d)", p=P), zeros[:]).then_inc(filled, 16)

                layer_stats(nc, "n0", x, mv, rstd)
                project(nc, "p0", x, mv, rstd, a["L0_Wq"], a["L0_Wk"], a["L0_Wv"], scratch[0], scratch[1], scratch_v, ident, 16, 32)
                with nc.Block() as block:
                    @block.sync
                    def _(sp):
                        sp.wait_ge(filled, 32)

            maxed("a0", Shape(4, 8, 32, True), D, scratch[0], scratch[1], scratch_v, None, a["L0_Wo"], None)
            with nc.sbuf_tensor("logits0", [P, TILES * 16], FP32) as logits, nc.sbuf_tensor("coef0", [P, TILES, 96], BF16) as coef:
                with nc.sbuf_tensor("xn0", [P, TILES * D], FP32) as xn0:
                    layer_stats(nc, "m0", x, mv, rstd, dst=xn0, stats=stats)
                    route(nc, "r0", xn0, a["L0_router"], 16, logits, ident)
                top2_coefficients(nc, "c0", logits, descending[16], coef)
                soft_experts(nc, "e0", x, mv, rstd, a["L0_gate"], a["L0_up"], a["L0_down"], a["L0_sgate"], a["L0_sup"], a["L0_sdown"],
                             coef, (a["select"], a["ident_bf"]), ident)

        with cleared_semaphores(nc):
            with nc.sbuf_tensor("xn1", [P, TILES * D], FP32) as xn1:
                layer_stats(nc, "n1", x, mv, rstd, dst=xn1)
                layer_stats(nc, "n1b", xn1, mv, rstd)
                project(nc, "p1", xn1, mv, rstd, a["L1_Wq"], a["L1_Wk"], a["L1_Wv"], scratch[0], scratch[1], scratch_v, ident, 16, 32,
                        gain=a["L1_gain"], qk_bias=a["L1_bqk"], v_bias=a["L1_bv"])
            maxed("a1", Shape(4, 8, 32, False), D, scratch[0], scratch[1], scratch_v, 1e-12, a["L1_Wo"], a["L1_bo"])
            layer_stats(nc, "m1", x, mv, rstd, stats=stats)
            channel_mix(nc, "f1", x, mv, rstd, a["L1_Wr"], a["L1_Wkk"], a["L1_Wvv"], a["L1_mu"], ident)

        with cleared_semaphores(nc):
            layer_stats(nc, "n2", x, mv, rstd)
            project(nc, "p2", x, mv, rstd, a["L2_Wq"], a["L2_Wk"], a["L2_Wv"], wide_q, wide_k, wide_v, ident, 8, 64, pos=a["pos"])
            maxed("a2", Shape(2, 64, 64, True), 512, wide_q, wide_k, wide_v, None, a["L2_Wo"], None)
            moe("f2", 0, a["L2_Wr"], a["L2_W1"], a["L2_W2"], None)

        with cleared_semaphores(nc):
            with nc.sbuf_tensor("factors", [P, 2], FP32) as factors, nc.sbuf_tensor("neg_lambda", [P, 1], FP32) as neg_lambda, \
                    nc.sbuf_tensor("nat3", [P, TILES * D], FP32) as nat:
                layer_stats(nc, "n3", x, mv, rstd, stats=stats)
                cosine_scales(nc, "s3", a["L3_raw"], a["L3_delta_col"], a["L3_delta_row"], a["L3_gain"], a["L3_sign"], a["L3_lambdas"],
                              factors, neg_lambda)
                project_cosine(nc, "p3", x, mv, rstd, a["L3_Wq"], a["L3_Wk"], a["L3_Wv"], factors, scratch[0], scratch[2], scratch[1],
                               scratch_v2, ident)
                cosine_attention(nc, "a3", scratch[0], scratch[2], scratch[1], scratch_v2, neg_lambda, nat, ident)
                out_project(nc, "o3", nat, D, a["L3_Wo"], x, stats, consts, bias=a["L3_bo"], rms=(16, 1e-5, 0.5, a["L3_subln"]))
            moe("f3", 1, a["L3_wg"], a["L3_w1"], a["L3_w2"], a["L3_b"])

        with nc.Block() as block:
            @block.sync
            def _(sp):
                sp.dma_start(out.rearrange("(n p) d -> p n d", p=P), x[:].rearrange("p (n d) -> p n d", d=D)).then_inc(sent, 16)
                sp.wait_ge(sent, 16)


def shape_constants():
    bf16 = mybir.dt.np(BF16)
    i = np.arange(P)
    one_stat = np.zeros((P, P))
    one_stat[:3] = 1
    select = np.zeros((96, 8, P))
    for part in range(3):
        for e in range(16):
            select[32 * part + e, e // 2, 64 * (e % 2):64 * (e % 2) + 64] = 1
    before_me = np.stack([i[:, None] < i[None, :], np.ones((P, P), bool)], 1)
    pos = np.arange(T, dtype=np.float32)[:, None]
    div = np.exp(np.arange(0, 64, 2, dtype=np.float32) * np.float32(-np.log(10000.0) / 64))
    ang = pos * div
    pe = np.stack([np.sin(ang), np.cos(ang)], -1).reshape(T, 64).astype(np.float32)
    return {
        "ident": np.eye(P, dtype=np.float32),
        "ident_bf": np.eye(P).astype(bf16),
        "mask_a": np.where(i[None] > i[:, None], NEG, 0).astype(bf16),
        "mask_b": np.where(i[:, None] > i[None], NEG, 0).astype(bf16),
        "one_stat": one_stat.astype(bf16),
        "zero_rows": np.zeros((3, 4 * T), bf16),
        "one_rows": np.ones((3, 4 * T), bf16),
        "select": select.astype(bf16),
        "before_me": before_me.astype(bf16),
        "descending": np.arange(16, 0, -1, dtype=np.float32).reshape(1, 16),
        "pos": np.ascontiguousarray(np.concatenate([pe.T, pe.T])),
        "L3_sign": np.tile(np.repeat(np.array([1, -1], np.float32), 8), 8).reshape(P, 1),
    }


def lay_out(i):
    def t(n):
        return np.ascontiguousarray(i[n].T)

    c = np.ascontiguousarray
    qkv1, b1 = i["L1_attn_W_qkv"], i["L1_attn_b_qkv"]
    qkv2 = c(i["L2_attn_Wqkv"].reshape(8, 3, 64, D).transpose(1, 3, 0, 2)).reshape(3, D, 512)
    return {
        "x": c(i["L0_attn_x"].reshape(TOK, D)),
        "L0_Wq": t("L0_attn_Wq"), "L0_Wk": t("L0_attn_Wk"), "L0_Wv": t("L0_attn_Wv"), "L0_Wo": t("L0_attn_Wo"),
        "L0_router": i["L0_ffn_router_w"], "L0_gate": i["L0_ffn_gate_w"], "L0_up": i["L0_ffn_up_w"],
        "L0_down": i["L0_ffn_down_w"], "L0_sgate": i["L0_ffn_shared_gate_w"], "L0_sup": i["L0_ffn_shared_up_w"],
        "L0_sdown": i["L0_ffn_shared_down_w"],
        "L1_Wq": c(qkv1[:, 0:D]), "L1_Wk": c(qkv1[:, D:2 * D]), "L1_Wv": c(qkv1[:, 2 * D:]),
        "L1_bqk": c(b1[0:2 * D].reshape(2, D).T), "L1_bv": c(b1[2 * D:].reshape(1, D)),
        "L1_gain": c(np.stack([i["L1_attn_ln_gamma"], i["L1_attn_ln_beta"]], 1)),
        "L1_Wo": i["L1_attn_W_proj"], "L1_bo": c(i["L1_attn_b_proj"].reshape(1, D)),
        "L1_Wr": t("L1_ffn_W_r"), "L1_Wkk": t("L1_ffn_W_k"), "L1_Wvv": t("L1_ffn_W_v"),
        "L1_mu": c(np.stack([i["L1_ffn_mu_r"], i["L1_ffn_mu_k"]], 1)),
        "L2_Wq": qkv2[0], "L2_Wk": qkv2[1], "L2_Wv": qkv2[2], "L2_Wo": t("L2_attn_Wo"),
        "L2_Wr": i["L2_ffn_Wr"], "L2_W1": i["L2_ffn_W1"], "L2_W2": i["L2_ffn_W2"],
        "L3_Wq": t("L3_attn_Wq"), "L3_Wk": t("L3_attn_Wk"), "L3_Wv": t("L3_attn_Wv"), "L3_Wo": t("L3_attn_Wo"),
        "L3_bo": c(i["L3_attn_bo"].reshape(1, D)),
        "L3_raw": c(i["L3_attn_cos_logit_scale_raw"].reshape(1, 1)),
        "L3_delta_col": np.repeat(i["L3_attn_cos_head_delta"], 16).reshape(P, 1),
        "L3_delta_row": c(i["L3_attn_cos_head_delta"].reshape(1, 8)),
        "L3_gain": np.repeat(i["L3_attn_delta_gain"], 16).reshape(P, 1),
        "L3_lambdas": np.concatenate([i[f"L3_attn_lambda_{n}"] for n in ("q1", "q2", "k1", "k2")]).reshape(1, 32),
        "L3_subln": np.tile(i["L3_attn_subln_weight"], 8).reshape(P, 1),
        "L3_wg": i["L3_ffn_wg"], "L3_w1": i["L3_ffn_w1"], "L3_w2": i["L3_ffn_w2"],
        "L3_b": c(np.concatenate([i["L3_ffn_b1"].reshape(EXPERTS, 4, P).transpose(0, 2, 1),
                                  i["L3_ffn_b2"].reshape(EXPERTS, P, 1)], 2)),
    }


def kernel(**inputs):
    import concourse.bacc as bacc
    from concourse.bass_utils import run_bass_kernel_spmd

    arrays = {**shape_constants(), **lay_out({n: np.asarray(v) for n, v in inputs.items()})}
    arrays = {f"in_{n}": np.ascontiguousarray(v) for n, v in arrays.items()}
    nc = bacc.Bacc("TRN2", target_bir_lowering=False, num_devices=1)
    a = {n[3:]: nc.dram_tensor(n, v.shape, mybir.dt.from_np(v.dtype), kind="ExternalInput").ap() for n, v in arrays.items()}
    out = nc.dram_tensor("out", (TOK, D), FP32, kind="ExternalOutput").ap()
    four_layers(nc, a, out)
    r = run_bass_kernel_spmd(nc, [arrays], core_ids=[0])
    return r.results[0]["out"].reshape(BATCH, T, D)
```
